# Optimizing a Trainium2 kernel written in Bass

```python
import numpy as np
import jax
import jax.numpy as jnp

def _softmax(x, axis=-1):
    return jax.nn.softmax(x, axis=axis)

def _gelu(x):
    return jax.nn.gelu(x, approximate=True)

def _silu(x):
    return jax.nn.silu(x)

def _sigmoid(x):
    return jax.nn.sigmoid(x)

def _layernorm(x, axis=-1, eps=1e-05):
    m = jnp.mean(x, axis=axis, keepdims=True)
    v = jnp.var(x, axis=axis, keepdims=True)
    return (x - m) / jnp.sqrt(v + eps)

def _scatter_add(tgt, idx, src, axis=0):
    return tgt.at[idx].add(src)

def _segment_sum(src, seg, n):
    return jax.ops.segment_sum(src, seg, n)
kernel_name = 'mk_seq_postln_d2_jaxref_r4_6f1f05'

def setup_inputs(seed: int=0):
    np.random.seed(seed)
    _w = jnp.asarray

    def _L0_attn_setup():
        import jax, jax.numpy as jnp
        import numpy as np
        import math
        E = 512
        H = 16
        HD = E // H // 2
        DEPTH = 12
        LAMBDA_INIT = 0.8 - 0.6 * math.exp(-0.3 * DEPTH)
        key = jax.random.key(seed)
        ks = jax.random.split(key, 9)
        s = 0.02
        return {'x': jax.random.normal(ks[0], (2, 512, E), jnp.float32), 'Wq': jax.random.normal(ks[1], (E, E), jnp.float32) * s, 'Wk': jax.random.normal(ks[2], (E, E), jnp.float32) * s, 'Wv': jax.random.normal(ks[3], (E, E), jnp.float32) * s, 'Wo': jax.random.normal(ks[4], (E, E), jnp.float32) * s, 'lq1': jax.random.normal(ks[5], (HD,), jnp.float32) * 0.1, 'lk1': jax.random.normal(ks[6], (HD,), jnp.float32) * 0.1, 'lq2': jax.random.normal(ks[7], (HD,), jnp.float32) * 0.1, 'lk2': jax.random.normal(ks[8], (HD,), jnp.float32) * 0.1}
    _L0_attn_in = _L0_attn_setup()

    def _L0_ffn_setup():
        import jax, jax.numpy as jnp
        import numpy as np
        B, S, H = (4, 512, 512)
        E = 8
        F = H // E
        TOPK = 2
        LORA_R = 16
        LORA_SCALE = 1.0
        key = jax.random.key(seed)
        ks = jax.random.split(key, 7)
        x = jax.random.normal(ks[0], (B, S, H), dtype=jnp.float32)
        G = jax.random.normal(ks[1], (H, E), dtype=jnp.float32)
        gate_w = jax.random.normal(ks[2], (E, F, H), dtype=jnp.float32) * np.float32(np.sqrt(2.0 / H))
        up_w = jax.random.normal(ks[3], (E, F, H), dtype=jnp.float32) * np.float32(np.sqrt(2.0 / H))
        down_w = jax.random.normal(ks[4], (E, H, F), dtype=jnp.float32) * np.float32(np.sqrt(2.0 / F))
        lora_A = jax.random.normal(ks[5], (E, LORA_R, H), dtype=jnp.float32) * np.float32(np.sqrt(2.0 / H))
        lora_B = jax.random.normal(ks[6], (E, H, LORA_R), dtype=jnp.float32) * np.float32(np.sqrt(2.0 / LORA_R))
        return {'x': x, 'G': G, 'gate_w': gate_w, 'up_w': up_w, 'down_w': down_w, 'lora_A': lora_A, 'lora_B': lora_B}
    _L0_ffn_in = _L0_ffn_setup()

    def _L1_attn_setup():
        import jax, jax.numpy as jnp
        import numpy as np
        from jax import lax
        HID = 512
        NH = 64
        P = 64
        N = 128
        G = 1
        CS = 64
        K = 4
        D_INNER = NH * P
        CONV_DIM = D_INNER + 2 * G * N
        PROJ = D_INNER + CONV_DIM + NH
        EPS = 1e-05
        BATCH, SEQ = (2, 512)

        def _segsum(x):
            T = x.shape[-1]
            xc = jnp.cumsum(x, axis=-1)
            seg = xc[..., :, None] - xc[..., None, :]
            mask = jnp.tril(jnp.ones((T, T), dtype=bool))
            return jnp.where(mask, seg, -jnp.inf)

        def _mamba2_forward(hidden_states, W_in, conv_w, conv_b, dt_bias, A_log, D_param, norm_w, W_out):
            B_, L_ = hidden_states.shape[:2]
            proj = hidden_states @ W_in.T
            z = proj[..., :D_INNER]
            xBC = proj[..., D_INNER:D_INNER + CONV_DIM]
            dt = proj[..., D_INNER + CONV_DIM:]
            xc = lax.conv_general_dilated(jnp.transpose(xBC, (0, 2, 1)), conv_w, window_strides=(1,), padding=[(K - 1, 0)], feature_group_count=CONV_DIM)
            xc = xc + conv_b[None, :, None]
            xBC = jax.nn.silu(jnp.transpose(xc, (0, 2, 1)))
            x = xBC[..., :D_INNER].reshape(B_, L_, NH, P)
            Bm = xBC[..., D_INNER:D_INNER + G * N].reshape(B_, L_, G, N)
            Cm = xBC[..., D_INNER + G * N:].reshape(B_, L_, G, N)
            dt = jax.nn.softplus(dt + dt_bias)
            A = -jnp.exp(A_log)
            Bh = jnp.repeat(Bm, NH // G, axis=2)
            Ch = jnp.repeat(Cm, NH // G, axis=2)
            nc = L_ // CS
            x_dt = (x * dt[..., None]).reshape(B_, nc, CS, NH, P)
            B_c = Bh.reshape(B_, nc, CS, NH, N)
            C_c = Ch.reshape(B_, nc, CS, NH, N)
            dA = jnp.transpose((dt * A).reshape(B_, nc, CS, NH), (0, 3, 1, 2))
            A_cum = jnp.cumsum(dA, axis=-1)
            Lmat = jnp.exp(_segsum(dA))
            Y_diag = jnp.einsum('bclhn,bcshn,bhcls,bcshp->bclhp', C_c, B_c, Lmat, x_dt)
            decay_states = jnp.exp(A_cum[..., -1:] - A_cum)
            states = jnp.einsum('bclhn,bhcl,bclhp->bchpn', B_c, decay_states, x_dt)
            da_last = A_cum[..., -1]

            def step(prev, inp):
                s_k, d_k = inp
                new = prev * jnp.exp(d_k)[..., None, None] + s_k
                return (new, prev)
            _, prev_states = lax.scan(step, jnp.zeros((B_, NH, P, N), dtype=x.dtype), (jnp.transpose(states, (1, 0, 2, 3, 4)), jnp.transpose(da_last, (2, 0, 1))))
            prev_states = jnp.transpose(prev_states, (1, 2, 0, 3, 4))
            Y_off = jnp.einsum('bclhn,bhcpn,bhcl->bclhp', C_c, prev_states, jnp.exp(A_cum))
            y = (Y_diag + Y_off).reshape(B_, L_, NH, P) + D_param[None, None, :, None] * x
            y = y.reshape(B_, L_, D_INNER)
            g = y * jax.nn.silu(z)
            gs = D_INNER // G
            gr = g.reshape(B_, L_, G, gs)
            var = jnp.mean(gr * gr, axis=-1, keepdims=True)
            gn = (gr * lax.rsqrt(var + EPS)).reshape(B_, L_, D_INNER) * norm_w
            return gn @ W_out.T
        key = jax.random.key(seed)
        ks = jax.random.split(key, 8)
        hidden_states = jax.random.normal(ks[0], (BATCH, SEQ, HID), dtype=jnp.float32)
        W_in = jax.random.normal(ks[1], (PROJ, HID), dtype=jnp.float32) * 0.02
        conv_w = jax.random.normal(ks[2], (CONV_DIM, 1, K), dtype=jnp.float32) * 0.2
        conv_b = jax.random.normal(ks[3], (CONV_DIM,), dtype=jnp.float32) * 0.02
        dt = jnp.exp(jax.random.uniform(ks[4], (NH,)) * (np.log(0.1) - np.log(0.001)) + np.log(0.001))
        dt_bias = (dt + jnp.log(-jnp.expm1(-dt))).astype(jnp.float32)
        A_log = jnp.log(jnp.arange(1, NH + 1, dtype=jnp.float32))
        D_param = jnp.ones((NH,), dtype=jnp.float32)
        norm_w = jnp.ones((D_INNER,), dtype=jnp.float32)
        W_out = jax.random.normal(ks[5], (HID, D_INNER), dtype=jnp.float32) * 0.02
        return {'hidden_states': hidden_states, 'W_in': W_in, 'conv_w': conv_w, 'conv_b': conv_b, 'dt_bias': dt_bias, 'A_log': A_log, 'D_param': D_param, 'norm_w': norm_w, 'W_out': W_out}
    _L1_attn_in = _L1_attn_setup()

    def _L1_ffn_setup():
        import jax, jax.numpy as jnp
        import numpy as np
        HIDDEN = 512
        INTER = 2048
        B, S = (4, 256)

        def _qmatmul(x, w_int8, scale):
            y = jnp.einsum('bsh,ho->bso', x, w_int8.astype(x.dtype))
            return y * scale
        key = jax.random.key(seed)
        ks = jax.random.split(key, 7)
        x = jax.random.normal(ks[0], (B, S, HIDDEN), dtype=jnp.float32)
        w_gate = jax.random.randint(ks[1], (HIDDEN, INTER), -128, 128, dtype=jnp.int32).astype(jnp.int8)
        w_up = jax.random.randint(ks[2], (HIDDEN, INTER), -128, 128, dtype=jnp.int32).astype(jnp.int8)
        w_down = jax.random.randint(ks[3], (INTER, HIDDEN), -128, 128, dtype=jnp.int32).astype(jnp.int8)
        s_gate = jax.random.uniform(ks[4], (INTER,), dtype=jnp.float32) * 0.02 + 0.001
        s_up = jax.random.uniform(ks[5], (INTER,), dtype=jnp.float32) * 0.02 + 0.001
        s_down = jax.random.uniform(ks[6], (HIDDEN,), dtype=jnp.float32) * 0.02 + 0.001
        return {'x': x, 'w_gate': w_gate, 'w_up': w_up, 'w_down': w_down, 's_gate': s_gate, 's_up': s_up, 's_down': s_down}
    _L1_ffn_in = _L1_ffn_setup()
    _d = {'L0_attn_x': _L0_attn_in['x'], 'L0_attn_Wq': _L0_attn_in['Wq'], 'L0_attn_Wk': _L0_attn_in['Wk'], 'L0_attn_Wv': _L0_attn_in['Wv'], 'L0_attn_Wo': _L0_attn_in['Wo'], 'L0_attn_lq1': _L0_attn_in['lq1'], 'L0_attn_lk1': _L0_attn_in['lk1'], 'L0_attn_lq2': _L0_attn_in['lq2'], 'L0_attn_lk2': _L0_attn_in['lk2'], 'L0_ffn_G': _L0_ffn_in['G'], 'L0_ffn_gate_w': _L0_ffn_in['gate_w'], 'L0_ffn_up_w': _L0_ffn_in['up_w'], 'L0_ffn_down_w': _L0_ffn_in['down_w'], 'L0_ffn_lora_A': _L0_ffn_in['lora_A'], 'L0_ffn_lora_B': _L0_ffn_in['lora_B'], 'L1_attn_W_in': _L1_attn_in['W_in'], 'L1_attn_conv_w': _L1_attn_in['conv_w'], 'L1_attn_conv_b': _L1_attn_in['conv_b'], 'L1_attn_dt_bias': _L1_attn_in['dt_bias'], 'L1_attn_A_log': _L1_attn_in['A_log'], 'L1_attn_D_param': _L1_attn_in['D_param'], 'L1_attn_norm_w': _L1_attn_in['norm_w'], 'L1_attn_W_out': _L1_attn_in['W_out'], 'L1_ffn_w_gate': _L1_ffn_in['w_gate'], 'L1_ffn_w_up': _L1_ffn_in['w_up'], 'L1_ffn_w_down': _L1_ffn_in['w_down'], 'L1_ffn_s_gate': _L1_ffn_in['s_gate'], 'L1_ffn_s_up': _L1_ffn_in['s_up'], 'L1_ffn_s_down': _L1_ffn_in['s_down']}
    _x0 = _d['L0_attn_x']
    _d['L0_attn_x'] = jax.random.normal(jax.random.fold_in(jax.random.key(seed), 1), (1, 2048, 512), dtype=_x0.dtype)
    del _x0
    return _d

def reference(L0_attn_x, L0_attn_Wq, L0_attn_Wk, L0_attn_Wv, L0_attn_Wo, L0_attn_lq1, L0_attn_lk1, L0_attn_lq2, L0_attn_lk2, L0_ffn_G, L0_ffn_gate_w, L0_ffn_up_w, L0_ffn_down_w, L0_ffn_lora_A, L0_ffn_lora_B, L1_attn_W_in, L1_attn_conv_w, L1_attn_conv_b, L1_attn_dt_bias, L1_attn_A_log, L1_attn_D_param, L1_attn_norm_w, L1_attn_W_out, L1_ffn_w_gate, L1_ffn_w_up, L1_ffn_w_down, L1_ffn_s_gate, L1_ffn_s_up, L1_ffn_s_down):

    def _L0_attn_ref(x, Wq, Wk, Wv, Wo, lq1, lk1, lq2, lk2):
        import jax, jax.numpy as jnp
        import numpy as np
        import math
        E = 512
        H = 16
        HD = E // H // 2
        DEPTH = 12
        LAMBDA_INIT = 0.8 - 0.6 * math.exp(-0.3 * DEPTH)
        b, t, e = x.shape
        scaling = HD ** (-0.5)
        q = (x @ Wq).reshape(b, t, 2 * H, HD).transpose(0, 2, 1, 3) * scaling
        k = (x @ Wk).reshape(b, t, 2 * H, HD).transpose(0, 2, 1, 3)
        v = (x @ Wv).reshape(b, t, H, 2 * HD).transpose(0, 2, 1, 3)
        scores = jnp.einsum('bhqd,bhkd->bhqk', q, k)
        causal = jnp.triu(jnp.full((t, t), -jnp.inf, dtype=jnp.float32), 1)
        aw = jax.nn.softmax((scores + causal).astype(jnp.float32), axis=-1)
        lam = jnp.exp(jnp.sum(lq1 * lk1)) - jnp.exp(jnp.sum(lq2 * lk2)) + LAMBDA_INIT
        aw = aw.reshape(b, H, 2, t, t)
        aw = aw[:, :, 0] - lam * aw[:, :, 1]
        attn = jnp.einsum('bhqk,bhkd->bhqd', aw, v)
        attn = attn * jax.lax.rsqrt(jnp.mean(attn * attn, axis=-1, keepdims=True) + 1e-05)
        attn = attn * (1.0 - LAMBDA_INIT)
        attn = attn.transpose(0, 2, 1, 3).reshape(b, t, H * 2 * HD)
        return attn @ Wo

    def _L0_ffn_ref(x, G, gate_w, up_w, down_w, lora_A, lora_B):
        import jax, jax.numpy as jnp
        import numpy as np
        B, S, H = (4, 512, 512)
        E = 8
        F = H // E
        TOPK = 2
        LORA_R = 16
        LORA_SCALE = 1.0
        scores = jax.nn.softmax(jnp.einsum('bsh,he->bse', x, G), axis=-1)
        value, indices = jax.lax.top_k(scores, TOPK)
        onehot = jax.nn.one_hot(indices, E, dtype=value.dtype)
        w = jnp.einsum('bsk,bske->bse', value, onehot)
        gate = jax.nn.silu(jnp.einsum('bsh,efh->bsef', x, gate_w))
        up = jnp.einsum('bsh,efh->bsef', x, up_w)
        gated = gate * up
        out = jnp.einsum('bsef,bse,ehf->bsh', gated, w, down_w)
        lr = jnp.einsum('bsh,erh->bser', x, lora_A)
        out = out + LORA_SCALE * jnp.einsum('bser,bse,ehr->bsh', lr, w, lora_B)
        return out

    def _L1_attn_ref(hidden_states, W_in, conv_w, conv_b, dt_bias, A_log, D_param, norm_w, W_out):
        import jax, jax.numpy as jnp
        import numpy as np
        from jax import lax
        HID = 512
        NH = 64
        P = 64
        N = 128
        G = 1
        CS = 64
        K = 4
        D_INNER = NH * P
        CONV_DIM = D_INNER + 2 * G * N
        PROJ = D_INNER + CONV_DIM + NH
        EPS = 1e-05
        BATCH, SEQ = (2, 512)

        def _segsum(x):
            T = x.shape[-1]
            xc = jnp.cumsum(x, axis=-1)
            seg = xc[..., :, None] - xc[..., None, :]
            mask = jnp.tril(jnp.ones((T, T), dtype=bool))
            return jnp.where(mask, seg, -jnp.inf)

        def _mamba2_forward(hidden_states, W_in, conv_w, conv_b, dt_bias, A_log, D_param, norm_w, W_out):
            B_, L_ = hidden_states.shape[:2]
            proj = hidden_states @ W_in.T
            z = proj[..., :D_INNER]
            xBC = proj[..., D_INNER:D_INNER + CONV_DIM]
            dt = proj[..., D_INNER + CONV_DIM:]
            xc = lax.conv_general_dilated(jnp.transpose(xBC, (0, 2, 1)), conv_w, window_strides=(1,), padding=[(K - 1, 0)], feature_group_count=CONV_DIM)
            xc = xc + conv_b[None, :, None]
            xBC = jax.nn.silu(jnp.transpose(xc, (0, 2, 1)))
            x = xBC[..., :D_INNER].reshape(B_, L_, NH, P)
            Bm = xBC[..., D_INNER:D_INNER + G * N].reshape(B_, L_, G, N)
            Cm = xBC[..., D_INNER + G * N:].reshape(B_, L_, G, N)
            dt = jax.nn.softplus(dt + dt_bias)
            A = -jnp.exp(A_log)
            Bh = jnp.repeat(Bm, NH // G, axis=2)
            Ch = jnp.repeat(Cm, NH // G, axis=2)
            nc = L_ // CS
            x_dt = (x * dt[..., None]).reshape(B_, nc, CS, NH, P)
            B_c = Bh.reshape(B_, nc, CS, NH, N)
            C_c = Ch.reshape(B_, nc, CS, NH, N)
            dA = jnp.transpose((dt * A).reshape(B_, nc, CS, NH), (0, 3, 1, 2))
            A_cum = jnp.cumsum(dA, axis=-1)
            Lmat = jnp.exp(_segsum(dA))
            Y_diag = jnp.einsum('bclhn,bcshn,bhcls,bcshp->bclhp', C_c, B_c, Lmat, x_dt)
            decay_states = jnp.exp(A_cum[..., -1:] - A_cum)
            states = jnp.einsum('bclhn,bhcl,bclhp->bchpn', B_c, decay_states, x_dt)
            da_last = A_cum[..., -1]

            def step(prev, inp):
                s_k, d_k = inp
                new = prev * jnp.exp(d_k)[..., None, None] + s_k
                return (new, prev)
            _, prev_states = lax.scan(step, jnp.zeros((B_, NH, P, N), dtype=x.dtype), (jnp.transpose(states, (1, 0, 2, 3, 4)), jnp.transpose(da_last, (2, 0, 1))))
            prev_states = jnp.transpose(prev_states, (1, 2, 0, 3, 4))
            Y_off = jnp.einsum('bclhn,bhcpn,bhcl->bclhp', C_c, prev_states, jnp.exp(A_cum))
            y = (Y_diag + Y_off).reshape(B_, L_, NH, P) + D_param[None, None, :, None] * x
            y = y.reshape(B_, L_, D_INNER)
            g = y * jax.nn.silu(z)
            gs = D_INNER // G
            gr = g.reshape(B_, L_, G, gs)
            var = jnp.mean(gr * gr, axis=-1, keepdims=True)
            gn = (gr * lax.rsqrt(var + EPS)).reshape(B_, L_, D_INNER) * norm_w
            return gn @ W_out.T
        return _mamba2_forward(hidden_states, W_in, conv_w, conv_b, dt_bias, A_log, D_param, norm_w, W_out)

    def _L1_ffn_ref(x, w_gate, w_up, w_down, s_gate, s_up, s_down):
        import jax, jax.numpy as jnp
        import numpy as np
        HIDDEN = 512
        INTER = 2048
        B, S = (4, 256)

        def _qmatmul(x, w_int8, scale):
            y = jnp.einsum('bsh,ho->bso', x, w_int8.astype(x.dtype))
            return y * scale
        gate = jax.nn.silu(_qmatmul(x, w_gate, s_gate))
        up = _qmatmul(x, w_up, s_up)
        fuse = gate * up
        return _qmatmul(fuse, w_down, s_down)
    x = L0_attn_x
    x = _layernorm(x + _L0_attn_ref(x, L0_attn_Wq, L0_attn_Wk, L0_attn_Wv, L0_attn_Wo, L0_attn_lq1, L0_attn_lk1, L0_attn_lq2, L0_attn_lk2), axis=-1)
    x = _layernorm(x + _L0_ffn_ref(x, L0_ffn_G, L0_ffn_gate_w, L0_ffn_up_w, L0_ffn_down_w, L0_ffn_lora_A, L0_ffn_lora_B), axis=-1)
    x = _layernorm(x + _L1_attn_ref(x, L1_attn_W_in, L1_attn_conv_w, L1_attn_conv_b, L1_attn_dt_bias, L1_attn_A_log, L1_attn_D_param, L1_attn_norm_w, L1_attn_W_out), axis=-1)
    x = _layernorm(x + _L1_ffn_ref(x, L1_ffn_w_gate, L1_ffn_w_up, L1_ffn_w_down, L1_ffn_s_gate, L1_ffn_s_up, L1_ffn_s_down), axis=-1)
    return x

_drawn_inputs = setup_inputs


def setup_inputs(seed=0):
    import zlib

    import numpy as np

    out = dict(_drawn_inputs(seed))
    spreads = {'L1_attn_D_param': (1.0, 0.2), 'L1_attn_norm_w': (1.0, 0.2)}
    factors = {'L0_attn_lq1': 2.83, 'L1_attn_dt_bias': 8.0, 'L1_attn_A_log': 8.0}
    for name, (base, spread) in spreads.items():
        noise = np.random.default_rng([zlib.crc32(name.encode()), seed]).standard_normal(out[name].shape)
        drawn = base * np.exp(spread * noise) if base else spread * noise
        out[name] = jnp.asarray(drawn.astype(out[name].dtype))
    for name, factor in factors.items():
        out[name] = (out[name] * factor).astype(out[name].dtype)
    return out
```

```python
import math
from contextlib import ExitStack

import concourse.bass as bass
from concourse import mybir

F32 = mybir.dt.float32
F32R = mybir.dt.float32r
BF16 = mybir.dt.bfloat16
ALU = mybir.AluOpType
ACT = mybir.ActivationFunctionType
AX = mybir.AxisListType
ds = bass.ds

P = 128
T = 2048
E = 512
TT = T // P
EK = E // P
CHUNK = 512
NCH = T // CHUNK
LN_EPS = 1e-5
NEG = -3.0e38

HD = 16
PAIRS = 16
VD = 2 * HD
LAMBDA_INIT = 0.8 - 0.6 * math.exp(-0.3 * 12)


def constants(nc, g):
    made = g.sem("constants_made")
    with nc.Block() as block:

        @block.gpsimd
        def _(pool):
            pool.memset(g.ident[:, :], 0.0).then_inc(made, 1)
            pool.memset(g.identb[:, :], 0.0).then_inc(made, 1)
            pool.memset(g.causal[:, :], 0.0).then_inc(made, 1)
            pool.wait_ge(made, 3)
            for m in (g.ident, g.identb):
                pool.affine_select(out=m[:, :], in_=m[:, :], compare_op=ALU.not_equal, fill=1.0, base=0,
                                   pattern=[[-1, P]], channel_multiplier=1).then_inc(made, 1)
            pool.affine_select(out=g.causal[:, :], in_=g.causal[:, :], compare_op=ALU.is_ge, fill=NEG, base=0,
                               pattern=[[-1, P]], channel_multiplier=1).then_inc(made, 1)
            pool.wait_ge(made, 6)


def product3(pe, out, lhs, rhs, start=True, stop=True):
    (lh, ll), (rh, rl) = lhs, rhs
    pe.matmul(out, ll, rh, start=start, stop=False)
    pe.matmul(out, lh, rl, start=False, stop=False)
    return pe.matmul(out, lh, rh, start=False, stop=stop)


def qkv(nc, g, xT, Wq, Wk, Wv, QD, KD):
    with ExitStack() as ctx:
        sb = lambda name, shape, dt=F32: ctx.enter_context(nc.sbuf_tensor(name, shape, dt))
        wraw = [sb(f"wraw_{w}", [P, EK, E]) for w in "qkv"]
        wh = [sb(f"wh_{w}", [P, EK, E], F32R) for w in "qkv"]
        wl = [sb(f"wl_{w}", [P, EK, E], F32R) for w in "qkv"]
        xraw = sb("xraw", [P, 2, T])
        NS = 4
        sh = sb("qk_high", [P, NS, CHUNK], F32R)
        sl = sb("qk_low", [P, NS, CHUNK], F32R)
        ps = [ctx.enter_context(nc.psum_tensor(f"qkv_ps{i}", [P, CHUNK], F32)) for i in range(8)]
        w_in = [g.sem(f"w_in_{w}") for w in "qkv"]
        x_in = [g.sem("x_in0"), g.sem("x_in1")]
        w_high, w_low = g.sem("w_high"), g.sem("w_low")
        x_high, x_low = g.sem("x_high"), g.sem("x_low")
        prod, high, low = g.sem("qk_prod"), g.sem("qk_high"), g.sem("qk_low")
        out = [g.sem(f"qk_out{i}") for i in range(NS)]
        v_prod, v_done = g.sem("v_prod"), g.sem("v_done")
        outs = [(w, m, c) for c in range(NCH) for w in range(2) for m in range(EK)]
        with nc.Block() as block:

            @block.sync
            def _(sp):
                for w, W in enumerate((Wq, Wk, Wv)):
                    sp.dma_start(wraw[w][:, :, :], W.rearrange("(k p) n -> p k n", p=P)).then_inc(w_in[w], 16)
                    if w == 0:
                        for k in range(2):
                            sp.dma_start(xraw[:, k, :], xT[k * P:(k + 1) * P, :]).then_inc(x_in[k], 16)
                for k in range(2, EK):
                    sp.wait_ge(x_low, k - 1)
                    sp.dma_start(xraw[:, k % 2, :], xT[k * P:(k + 1) * P, :]).then_inc(x_in[k % 2], 16)
                for n, (w, m, c) in enumerate(outs):
                    sp.wait_ge(low, n + 1)
                    for part, s in enumerate((sh, sl)):
                        sp.dma_start((QD, KD)[w][part, m * P:(m + 1) * P, c * CHUNK:(c + 1) * CHUNK],
                                     s[:, n % NS, :].bitcast(F32)).then_inc(out[n % NS], 16)
                for i in range(NS):
                    sp.wait_ge(out[i], 32 * (len(outs) // NS))

            @block.scalar
            def _(act):
                for w in range(2):
                    act.wait_ge(w_in[w], 16)
                    act.activation(wh[w][:, :, :], wraw[w][:, :, :], ACT.Copy).then_inc(w_high, 1)
                    for k in range(2 * w, 2 * w + 2):
                        act.wait_ge(x_in[k % 2], 16 * (k // 2 + 1))
                        act.activation(g.xh[:, k, :], xraw[:, k % 2, :], ACT.Copy).then_inc(x_high, 1)
                act.wait_ge(w_in[2], 16)
                act.activation(wh[2][:, :, :], wraw[2][:, :, :], ACT.Copy).then_inc(w_high, 1)
                for n, (w, m, c) in enumerate(outs):
                    act.wait_ge(prod, n + 1)
                    if n >= NS:
                        act.wait_ge(out[n % NS], 32 * (n // NS))
                    act.activation(sh[:, n % NS, :], ps[n % 8][:, :], ACT.Copy,
                                   scale=(HD ** -0.5, 1.0)[w]).then_inc(high, 1)
                for i in range(TT):
                    act.wait_ge(v_prod, i + 1)
                    act.activation(g.V[:, i, :], ps[i % 8][:, :], ACT.Copy).then_inc(v_done, 1)

            @block.vector
            def _(dve):
                for w in range(3):
                    dve.wait_ge(w_high, w + 1)
                    dve.tensor_tensor(wl[w][:, :, :], wraw[w][:, :, :], wh[w][:, :, :].bitcast(F32),
                                      ALU.subtract).then_inc(w_low, 1)
                    if w < 2:
                        for k in range(2 * w, 2 * w + 2):
                            dve.wait_ge(x_high, k + 1)
                            dve.tensor_tensor(g.xl[:, k, :], xraw[:, k % 2, :], g.xh[:, k, :].bitcast(F32),
                                              ALU.subtract).then_inc(x_low, 1)
                for n, (w, m, c) in enumerate(outs):
                    dve.wait_ge(high, n + 1)
                    dve.scalar_tensor_tensor(out=sl[:, n % NS, :], in0=ps[n % 8][:, :], scalar=(HD ** -0.5, 1.0)[w],
                                             in1=sh[:, n % NS, :].bitcast(F32), op0=ALU.mult,
                                             op1=ALU.subtract).then_inc(low, 1)

            @block.tensor
            def _(pe):
                pe.wait_ge(w_low, 2)
                pe.wait_ge(x_low, EK)
                for n, (w, m, c) in enumerate(outs):
                    if n >= 8:
                        pe.wait_ge(low, n - 7)
                    for k in range(EK):
                        mm = product3(pe, ps[n % 8][:, :],
                                      (wh[w][:, k, m * P:(m + 1) * P], wl[w][:, k, m * P:(m + 1) * P]),
                                      (g.xh[:, k, c * CHUNK:(c + 1) * CHUNK], g.xl[:, k, c * CHUNK:(c + 1) * CHUNK]),
                                      start=(k == 0), stop=(k == EK - 1))
                    mm.then_inc(prod, 1)
                pe.wait_ge(w_low, 3)
                for i in range(TT):
                    if i < 8:
                        pe.wait_ge(low, len(outs) - 7 + i)
                    else:
                        pe.wait_ge(v_done, i - 7)
                    for k in range(EK):
                        mm = product3(pe, ps[i % 8][:, :],
                                      (g.xh[:, k, i * P:(i + 1) * P], g.xl[:, k, i * P:(i + 1) * P]),
                                      (wh[2][:, k, :], wl[2][:, k, :]), start=(k == 0), stop=(k == EK - 1))
                    mm.then_inc(v_prod, 1)


def attention(nc, g, QD, KD, lams):
    ITER = PAIRS // 2
    order = list(range(0, TT, 2)) + list(range(TT - 1, 0, -2))
    rows = [(b, i) for b in range(2) for i in order]
    NR = len(rows)
    HALF = 1024
    halves = [1 + (i >= TT // 2) for _, i in rows]
    groups = [(i + 4) // 4 for _, i in rows]
    u0 = [2 * sum(halves[:r]) for r in range(NR + 1)]
    g0 = [sum(groups[:r]) for r in range(NR + 1)]
    NU, NG = u0[NR], g0[NR]
    twos = [2 * sum(h == 2 for h in halves[:r]) for r in range(NR + 1)]
    NT = twos[NR]
    LOADS = 16
    with ExitStack() as ctx:
        sb = lambda name, shape, dt=F32: ctx.enter_context(nc.sbuf_tensor(name, shape, dt))
        QS = [sb(f"QS{b}", [P, T], F32R) for b in range(2)]
        KS = [sb(f"KS{b}", [P, T], F32R) for b in range(2)]
        Pr = [[sb(f"probs{s}_{b}", [P, T]) for b in range(3)] for s in range(2)]
        awT = [sb(f"awT{b}", [P, 4, P]) for b in range(2)]
        part = sb("part_max", [P, 2, 2])
        nm = sb("neg_max", [P, 2, 2])
        L = sb("sums", [P, 2, 2, 2])
        Ls = sb("row_sums", [P, 2, 2])
        rL = sb("inv_sums", [P, 2, 2])
        rr = sb("ratio", [P, 2])
        lv = sb("lambda_vecs", [P, 4, HD])
        lp = sb("lambda_products", [P, 2, HD])
        le = sb("lambda_sums", [P, 4])
        slot = [ctx.enter_context(nc.psum_tensor(f"score{i}", [P, HALF], F32)) for i in range(3)]
        tp = ctx.enter_context(nc.psum_tensor("awT_ps", [P, 4, P], F32))
        po = ctx.enter_context(nc.psum_tensor("pv_ps", [P, VD], F32))
        lam_in, lam = g.sem("lam_in"), g.sem("lam")
        lam_sum, lam_exp = g.sem("lam_sum"), g.sem("lam_exp")
        loaded = [g.sem("qk_loaded0"), g.sem("qk_loaded1")]
        scored, part_ready, max_ready = g.sem("scored"), g.sem("part_ready"), g.sem("max_ready")
        exped, sums_ready, inv_ready, ratio_ready = g.sem("exped"), g.sem("sums"), g.sem("inv"), g.sem("ratio")
        combined, turned, turned_out = g.sem("combined"), g.sem("turned"), g.sem("turned_out")
        pv_done, pv_part, pv_read = g.sem("pv_done"), g.sem("pv_part"), g.sem("pv_read")

        def load(sp, b, pair):
            for s in range(2):
                for r in range(4):
                    at = 64 * s + HD * r
                    sp.dma_start(QS[b][at:at + HD, :].bitcast(F32), QD[r // 2, ds(pair * VD + s * HD, HD), :]).then_inc(loaded[b], 16)
                    sp.dma_start(KS[b][at:at + HD, :].bitcast(F32), KD[r % 2, ds(pair * VD + s * HD, HD), :]).then_inc(loaded[b], 16)

        with nc.Block() as block:

            @block.sync
            def _(sp):
                for n, v in enumerate(lams):
                    sp.dma_start(lv[:, n, :], v.partition_broadcast(P)).then_inc(lam_in, 16)
                for b in range(2):
                    load(sp, b, b)
                with sp.Fori(1, ITER) as it:
                    for b in range(2):
                        sp.wait_ge(scored, (it - 1) * NU + u0[(b + 1) * TT])
                        load(sp, b, 2 * it + b)

            @block.tensor
            def _(pe):
                with pe.Fori(0, ITER) as it:
                    for t in range(NR + 2):
                        todo = []
                        if t < NR:
                            b, i = rows[t]
                            if i == order[0]:
                                pe.wait_ge(loaded[b], (it + 1) * 16 * LOADS)

                        def unit(n):
                            u = u0[t] + n
                            s, hf = n // halves[t], n % halves[t]
                            cols = min(HALF, (i + 1) * P - hf * HALF)
                            pe.wait_ge(exped, it * NU + max(u - 2, 0))
                            diag = hf == halves[t] - 1
                            for c in range(0, cols, CHUNK):
                                w = min(CHUNK, cols - c)
                                mm = pe.matmul(slot[u % 3][:, c:c + w], QS[b][64 * s:64 * s + 64, i * P:(i + 1) * P],
                                               KS[b][64 * s:64 * s + 64, hf * HALF + c:hf * HALF + c + w],
                                               start=True, stop=True)
                            if diag:
                                mm = pe.matmul(slot[u % 3][:, cols - P:cols], g.identb[:, :], g.causal[:, :],
                                               start=False, stop=True, skip_group_check=True)
                            mm.then_inc(scored, 1)

                        def turn(n):
                            r = t - 2
                            gg = g0[r] + n
                            if n == 0:
                                pe.wait_ge(combined, it * NR + r + 1)
                            pe.wait_ge(turned_out, it * NG + gg)
                            for j in range(4 * n, min(4 * n + 4, rows[r][1] + 1)):
                                mm = pe.transpose(tp[:, j % 4, :], Pr[0][r % 3][:, j * P:(j + 1) * P], g.ident[:, :])
                            mm.then_inc(turned, 1)

                        def times_v(n):
                            r = t - 2
                            br, ir = rows[r]
                            gg = g0[r] + n
                            pe.wait_ge(turned_out, it * NG + gg + 1)
                            if n == 0:
                                pe.wait_ge(pv_read, it * NR + r)
                            for j in range(4 * n, min(4 * n + 4, ir + 1)):
                                mm = pe.matmul(po[:, :], awT[gg % 2][:, j % 4, :], g.V[:, j, ds(it * 2 * VD + br * VD, VD)],
                                               start=(j == 0), stop=(j == ir))
                            if n == groups[r] - 1:
                                mm.then_inc(pv_done, 1)
                            else:
                                mm.then_inc(pv_part, 1)

                        nu = 2 * halves[t] if t < NR else 0
                        ng = groups[t - 2] if t >= 2 else 0
                        if ng:
                            turn(0)
                        for n in range(max(nu, ng)):
                            if n < nu:
                                unit(n)
                            if n + 1 < ng:
                                turn(n + 1)
                            if n < ng:
                                times_v(n)

            @block.scalar
            def _(act):
                act.wait_ge(lam_sum, 2)
                act.activation(le[:, 2:4], le[:, 0:2], ACT.Exp).then_inc(lam_exp, 1)
                with act.Fori(0, ITER) as it:
                    for t in range(NR + 2):

                        def exps(s):
                            for hf in range(halves[t]):
                                u = u0[t] + s * halves[t] + hf
                                cols = min(HALF, (rows[t][1] + 1) * P - hf * HALF)
                                if hf == 0:
                                    act.wait_ge(max_ready, it * 2 * NR + 2 * t + s + 1)
                                if hf == 0 and s == 0:
                                    act.wait_ge(turned, it * NG + (g0[t - 2] if t >= 3 else 0))
                                act.activation(Pr[s][t % 3][:, hf * HALF:hf * HALF + cols], slot[u % 3][:, 0:cols],
                                               ACT.Exp, bias=nm[:, t % 2, s:s + 1],
                                               accum_out=L[:, t % 2, s, hf:hf + 1]).then_inc(exped, 1)

                        def out(n):
                            gg = g0[t - 2] + n
                            cnt = min(4, rows[t - 2][1] + 1 - 4 * n)
                            act.wait_ge(turned, it * NG + gg + 1)
                            r = max(x for x in range(NR) if g0[x] <= max(gg - 2, 0))
                            if gg >= 2:
                                last = gg - 2 == g0[r + 1] - 1
                                if last:
                                    act.wait_ge(pv_done, it * NR + r + 1)
                                else:
                                    act.wait_ge(pv_part, it * (NG - NR) + (gg - 2 - r) + 1)
                            else:
                                act.wait_ge(pv_done, it * NR)
                            act.activation(awT[gg % 2][:, 0:cnt, :], tp[:, 0:cnt, :], ACT.Copy).then_inc(turned_out, 1)

                        ng = groups[t - 2] if t >= 2 else 0
                        for n in range(min(2, ng)):
                            out(n)
                        if t < NR:
                            exps(0)
                        for n in range(2, ng):
                            out(n)
                        if t < NR:
                            exps(1)

            @block.vector
            def _(dve):
                dve.wait_ge(lam_in, 64)
                for n in range(2):
                    dve.tensor_tensor(lp[:, n, :], lv[:, 2 * n, :], lv[:, 2 * n + 1, :], ALU.mult).then_inc(lam, 1)
                dve.wait_ge(lam, 2)
                for n in range(2):
                    dve.tensor_reduce(le[:, n:n + 1], lp[:, n, :], AX.X, ALU.add).then_inc(lam_sum, 1)
                dve.wait_ge(lam_exp, 1)
                dve.tensor_tensor(le[:, 0:1], le[:, 3:4], le[:, 2:3], ALU.subtract).then_inc(lam, 1)
                dve.wait_ge(lam, 3)
                dve.tensor_scalar(g.neg_lam[:, :], le[:, 0:1], -LAMBDA_INIT, None, ALU.add).then_inc(lam, 1)
                dve.wait_ge(lam, 4)
                with dve.Fori(0, ITER) as it:
                    for t in range(NR + 2):
                        if t < NR:
                            for s in range(2):
                                for hf in range(halves[t]):
                                    u = u0[t] + s * halves[t] + hf
                                    cols = min(HALF, (rows[t][1] + 1) * P - hf * HALF)
                                    dve.wait_ge(scored, it * NU + u + 1)
                                    if halves[t] == 1:
                                        dve.tensor_reduce(nm[:, t % 2, s:s + 1], slot[u % 3][:, 0:cols], AX.X, ALU.max,
                                                          negate=True).then_inc(max_ready, 1)
                                    else:
                                        dve.tensor_reduce(part[:, s, hf:hf + 1], slot[u % 3][:, 0:cols], AX.X,
                                                          ALU.max).then_inc(part_ready, 1)
                                if halves[t] == 2:
                                    dve.wait_ge(part_ready, 2 * (it * NT + twos[t] + s + 1))
                                    dve.tensor_reduce(nm[:, t % 2, s:s + 1], part[:, s, :], AX.X, ALU.max,
                                                      negate=True).then_inc(max_ready, 1)
                        if 1 <= t <= NR:
                            r = t - 1
                            n = (rows[r][1] + 1) * P
                            dve.wait_ge(exped, it * NU + u0[r + 1])
                            dve.tensor_reduce(Ls[:, r % 2, :], L[:, r % 2, :, 0:halves[r]], AX.X, ALU.add).then_inc(sums_ready, 1)
                            dve.wait_ge(sums_ready, it * NR + r + 1)
                            dve.reciprocal(rL[:, r % 2, :], Ls[:, r % 2, :]).then_inc(inv_ready, 1)
                            dve.wait_ge(inv_ready, it * NR + r + 1)
                            dve.scalar_tensor_tensor(out=rr[:, r % 2:r % 2 + 1], in0=Ls[:, r % 2, 0:1],
                                                     scalar=rL[:, r % 2, 1:2], in1=g.neg_lam[:, :], op0=ALU.mult,
                                                     op1=ALU.mult).then_inc(ratio_ready, 1)
                            dve.wait_ge(ratio_ready, it * NR + r + 1)
                            dve.scalar_tensor_tensor(out=Pr[0][r % 3][:, 0:n], in0=Pr[1][r % 3][:, 0:n],
                                                     scalar=rr[:, r % 2:r % 2 + 1], in1=Pr[0][r % 3][:, 0:n],
                                                     op0=ALU.mult, op1=ALU.add).then_inc(combined, 1)
                        if t >= 2:
                            r = t - 2
                            br, ir = rows[r]
                            dve.wait_ge(pv_done, it * NR + r + 1)
                            dve.tensor_scalar(g.A[:, ir, ds(it * 2 * VD + br * VD, VD)], po[:, :], rL[:, r % 2, 0:1],
                                              None, ALU.mult).then_inc(pv_read, 1)


LOADB = 4


def split_weights(nc, g, what, items):
    w_in = [g.sem(f"sw_{what}_in{b}") for b in range(2)]
    w_high, w_low = g.sem(f"sw_{what}_high"), g.sem(f"sw_{what}_low")
    with nc.Block() as block:

        @block.sync
        def _(sp):
            for n, (src, raw, hi, lo) in enumerate(items):
                if n >= 2:
                    sp.wait_ge(w_low, n - 1)
                sp.dma_start(raw, src).then_inc(w_in[n % 2], 16)

        @block.scalar
        def _(act):
            for n, (src, raw, hi, lo) in enumerate(items):
                act.wait_ge(w_in[n % 2], 16 * (n // 2 + 1))
                act.activation(hi, raw, ACT.Copy).then_inc(w_high, 1)

        @block.vector
        def _(dve):
            for n, (src, raw, hi, lo) in enumerate(items):
                dve.wait_ge(w_high, n + 1)
                dve.tensor_tensor(lo, raw, hi.bitcast(F32), ALU.subtract).then_inc(w_low, 1)


def rms_norm(nc, g, A):
    with ExitStack() as ctx:
        sb = lambda name, shape, dt=F32: ctx.enter_context(nc.sbuf_tensor(name, shape, dt))
        sq = sb("rn_sq", [P, 2, E])
        ms = sb("rn_ms", [P, TT, PAIRS])
        squared, summed = g.sem("rn_squared"), g.sem("rn_summed")
        biased, rooted, inverted, scaled = g.sem("rn_biased"), g.sem("rn_rooted"), g.sem("rn_inv"), g.sem("rn_scaled")
        with nc.Block() as block:

            @block.scalar
            def _(act):
                for i in range(TT):
                    if i >= 2:
                        act.wait_ge(summed, i - 1)
                    act.activation(sq[:, i % 2, :], A[:, i, :], ACT.Square).then_inc(squared, 1)
                act.wait_ge(biased, 1)
                act.activation(ms[:, :, :], ms[:, :, :], ACT.Sqrt).then_inc(rooted, 1)

            @block.vector
            def _(dve):
                for i in range(TT):
                    dve.wait_ge(squared, i + 1)
                    dve.tensor_reduce(ms[:, i, :], sq[:, i % 2, :].rearrange("p (h d) -> p h d", d=VD), AX.X,
                                      ALU.add).then_inc(summed, 1)
                dve.wait_ge(summed, TT)
                c = 1.0 - LAMBDA_INIT
                dve.tensor_scalar(ms[:, :, :], ms[:, :, :], 1.0 / VD / c / c, LN_EPS / c / c, ALU.mult, ALU.add).then_inc(biased, 1)
                dve.wait_ge(rooted, 1)
                dve.reciprocal(ms[:, :, :], ms[:, :, :]).then_inc(inverted, 1)
                dve.wait_ge(inverted, 1)
                for i in range(TT):
                    a = A[:, i, :].rearrange("p (h d) -> p h d", d=VD)
                    dve.tensor_tensor(a, a, ms[:, i, :].unsqueeze(2).to_broadcast([P, PAIRS, VD]), ALU.mult).then_inc(scaled, 1)


def turn(nc, g, X, xh, xl, mv=None):
    tag = g.tag()
    with ExitStack() as ctx:
        rstd = ctx.enter_context(nc.sbuf_tensor(f"rstd{tag}", [P, TT], F32))
        tp = [ctx.enter_context(nc.psum_tensor(f"turn{tag}_{b}", [P, EK, P], F32)) for b in range(LOADB)]
        eps, root, inv, normed = (g.sem(f"{n}{tag}") for n in ("ln_eps", "ln_root", "ln_inv", "ln_normed"))
        turned, high, low = (g.sem(f"{n}{tag}") for n in ("turned", "turn_high", "turn_low"))
        with nc.Block() as block:

            @block.scalar
            def _(act):
                if mv is not None:
                    act.wait_ge(eps, 1)
                    act.activation(rstd[:, :], rstd[:, :], ACT.Sqrt).then_inc(root, 1)
                for i in range(TT):
                    act.wait_ge(turned, i + 1)
                    act.activation(xh[:, :, i * P:(i + 1) * P], tp[i % LOADB][:, :, :], ACT.Copy).then_inc(high, 1)

            @block.vector
            def _(dve):
                if mv is not None:
                    dve.tensor_scalar(rstd[:, :], mv[:, :, 1], LN_EPS, None, ALU.add).then_inc(eps, 1)
                    dve.wait_ge(root, 1)
                    dve.reciprocal(rstd[:, :], rstd[:, :]).then_inc(inv, 1)
                    dve.wait_ge(inv, 1)
                ahead = 4 if mv is not None else 0
                for i in range(TT + ahead):
                    if mv is not None and i < TT:
                        dve.tensor_scalar(X[:, i, :], X[:, i, :], mv[:, i, 0:1], rstd[:, i:i + 1], ALU.subtract,
                                          ALU.mult).then_inc(normed, 1)
                    if i >= ahead:
                        n = i - ahead
                        dve.wait_ge(high, n + 1)
                        dve.tensor_tensor(xl[:, :, n * P:(n + 1) * P], tp[n % LOADB][:, :, :],
                                          xh[:, :, n * P:(n + 1) * P].bitcast(F32), ALU.subtract).then_inc(low, 1)

            @block.tensor
            def _(pe):
                for i in range(TT):
                    if mv is not None:
                        pe.wait_ge(normed, i + 1)
                    if i >= LOADB:
                        pe.wait_ge(low, i - LOADB + 1)
                    for k in range(EK):
                        mm = pe.transpose(tp[i % LOADB][:, k, :], X[:, i, k * P:(k + 1) * P], g.ident[:, :])
                    mm.then_inc(turned, 1)


def project_out(nc, g, x_dram, X, ah, al, wh, wl, mv):
    NB = 4
    with ExitStack() as ctx:
        xin = ctx.enter_context(nc.sbuf_tensor("po_x", [P, NB, E], F32))
        st = ctx.enter_context(nc.sbuf_tensor("po_stats", [P, 2, 6], F32))
        ps = [ctx.enter_context(nc.psum_tensor(f"po_ps{b}", [P, E], F32)) for b in range(NB)]
        x_in = [g.sem(f"po_x{b}") for b in range(NB)]
        done, added, stats, aggr = g.sem("po_done"), g.sem("po_added"), g.sem("po_stats"), g.sem("po_aggr")
        with nc.Block() as block:

            @block.sync
            def _(sp):
                for i in range(TT):
                    if i >= NB:
                        sp.wait_ge(added, i - NB + 1)
                    sp.dma_start(xin[:, i % NB, :], x_dram[i * P:(i + 1) * P, :]).then_inc(x_in[i % NB], 16)

            @block.tensor
            def _(pe):
                for i in range(TT):
                    if i >= NB:
                        pe.wait_ge(added, i - NB + 1)
                    for k in range(EK):
                        mm = product3(pe, ps[i % NB][:, :], (ah[:, k, i * P:(i + 1) * P], al[:, k, i * P:(i + 1) * P]),
                                      (wh[:, k, :], wl[:, k, :]), start=(k == 0), stop=(k == EK - 1))
                    mm.then_inc(done, 1)

            @block.vector
            def _(dve):
                for i in range(TT):
                    dve.wait_ge(done, i + 1)
                    dve.wait_ge(x_in[i % NB], 16 * (i // NB + 1))
                    dve.tensor_tensor(X[:, i, :], ps[i % NB][:, :], xin[:, i % NB, :], ALU.add).then_inc(added, 1)
                    dve.wait_ge(added, i + 1)
                    dve.bn_stats(st[:, i % 2, :], X[:, i, :]).then_inc(stats, 1)
                    dve.wait_ge(stats, i + 1)
                    dve.bn_aggr(mv[:, i, :], st[:, i % 2, :]).then_inc(aggr, 1)


EX = 8
EF = 64
RANK = 16
FK = EX * EF // P


def moe(nc, g, X, xh, xl, W, mv):
    AR = EX * RANK + EX
    with ExitStack() as ctx:
        sb = lambda name, shape, dt=F32: ctx.enter_context(nc.sbuf_tensor(name, shape, dt))
        lr = sb("moe_lr", [P, TT, EX * RANK])
        ex = sb("moe_exp", [P, TT, EX])
        m = sb("moe_max", [P, TT])
        beats = sb("moe_beats", [P, TT, EX, EX])
        ties = sb("moe_ties", [P, TT, EX, EX])
        lower = sb("moe_lower", [P, EX, EX])
        rank = sb("moe_rank", [P, TT, EX])
        w = sb("moe_w", [P, TT, EX])
        with ExitStack() as inner:
            ps = [inner.enter_context(nc.psum_tensor(f"moe_ar{b}", [P, AR], F32)) for b in range(4)]
            made, prod, read_l, read_r = g.sem("moe_made"), g.sem("moe_prod"), g.sem("moe_read_l"), g.sem("moe_read_r")
            step, exped = g.sem("moe_step"), g.sem("moe_exped")
            with nc.Block() as block:

                @block.gpsimd
                def _(pool):
                    pool.memset(lower[:, :, :], 1.0).then_inc(made, 1)
                    pool.wait_ge(made, 1)
                    pool.affine_select(out=lower[:, :, :], in_=lower[:, :, :], compare_op=ALU.is_gt, fill=0.0, base=0,
                                       pattern=[[1, EX], [-1, EX]], channel_multiplier=0).then_inc(made, 1)

                @block.tensor
                def _(pe):
                    for i in range(TT):
                        if i >= 4:
                            pe.wait_ge(read_r, i - 3)
                        for k in range(EK):
                            mm = product3(pe, ps[i % 4][:, :], (xh[:, k, i * P:(i + 1) * P], xl[:, k, i * P:(i + 1) * P]),
                                          (W["first"][0][:, k, :], W["first"][1][:, k, :]), start=(k == 0), stop=(k == EK - 1))
                        mm.then_inc(prod, 1)

                @block.scalar
                def _(act):
                    for i in range(TT):
                        act.wait_ge(prod, i + 1)
                        act.activation(lr[:, i, :], ps[i % 4][:, 0:EX * RANK], ACT.Copy).then_inc(read_l, 1)
                    act.wait_ge(step, 2)
                    act.activation(ex[:, :, :], ex[:, :, :], ACT.Exp).then_inc(exped, 1)

                @block.vector
                def _(dve):
                    for i in range(TT):
                        dve.wait_ge(read_l, i + 1)
                        dve.tensor_copy(ex[:, i, :], ps[i % 4][:, EX * RANK:AR]).then_inc(read_r, 1)
                    dve.wait_ge(read_r, TT)
                    bc = lambda a: a.unsqueeze(2).to_broadcast([P, TT, EX])
                    dve.tensor_reduce(m[:, :], ex[:, :, :], AX.X, ALU.max).then_inc(step, 1)
                    dve.wait_ge(step, 1)
                    dve.tensor_tensor(ex[:, :, :], ex[:, :, :], bc(m[:, :]), ALU.subtract).then_inc(step, 1)
                    dve.wait_ge(exped, 1)
                    dve.tensor_reduce(m[:, :], ex[:, :, :], AX.X, ALU.add).then_inc(step, 1)
                    dve.wait_ge(step, 3)
                    dve.reciprocal(m[:, :], m[:, :]).then_inc(step, 1)
                    dve.wait_ge(step, 4)
                    dve.tensor_tensor(ex[:, :, :], ex[:, :, :], bc(m[:, :]), ALU.mult).then_inc(step, 1)
                    dve.wait_ge(step, 5)
                    dve.wait_ge(made, 2)
                    si = ex[:, :, :].unsqueeze(3).to_broadcast([P, TT, EX, EX])
                    sj = ex[:, :, :].unsqueeze(2).to_broadcast([P, TT, EX, EX])
                    dve.tensor_tensor(beats[:, :, :, :], sj, si, ALU.is_gt).then_inc(step, 1)
                    dve.tensor_tensor(ties[:, :, :, :], sj, si, ALU.is_equal).then_inc(step, 1)
                    dve.wait_ge(step, 7)
                    dve.tensor_tensor(ties[:, :, :, :], ties[:, :, :, :],
                                      lower[:, :, :].unsqueeze(1).to_broadcast([P, TT, EX, EX]), ALU.mult).then_inc(step, 1)
                    dve.wait_ge(step, 8)
                    dve.tensor_tensor(beats[:, :, :, :], beats[:, :, :, :], ties[:, :, :, :], ALU.add).then_inc(step, 1)
                    dve.wait_ge(step, 9)
                    dve.tensor_reduce(rank[:, :, :], beats[:, :, :, :], AX.X, ALU.add).then_inc(step, 1)
                    dve.wait_ge(step, 10)
                    dve.scalar_tensor_tensor(out=w[:, :, :], in0=rank[:, :, :], scalar=1.5, in1=ex[:, :, :],
                                             op0=ALU.is_lt, op1=ALU.mult).then_inc(step, 1)
                    dve.wait_ge(step, 11)

        sg = sb("moe_silu", [P, 2, E])
        gt = sb("moe_gated", [P, 2, E])
        lw = sb("moe_lw", [P, 2, EX * RANK])
        gh, gl = sb("moe_gh", [P, 2, FK, P], F32R), sb("moe_gl", [P, 2, FK, P], F32R)
        lh, ll = sb("moe_lh", [P, 2, P], F32R), sb("moe_ll", [P, 2, P], F32R)
        st = sb("moe_stats", [P, 2, 6])
        pb = lambda n, s: ctx.enter_context(nc.psum_tensor(n, s, F32))
        pg, pu = [pb(f"moe_g{b}", [P, E]) for b in range(2)], [pb(f"moe_u{b}", [P, E]) for b in range(2)]
        pt, pl, pd = pb("moe_t", [P, FK, P]), pb("moe_l", [P, P]), [pb(f"moe_d{b}", [P, E]) for b in range(2)]
        gate, up, silu, mul, gated = g.sem("moe_gate"), g.sem("moe_up"), g.sem("moe_silu"), g.sem("moe_mul"), g.sem("moe_gated")
        turned, high, low, down = g.sem("moe_turned"), g.sem("moe_high"), g.sem("moe_low"), g.sem("moe_down")
        lweighed, added, stats, aggr = g.sem("moe_lweighed"), g.sem("moe_added"), g.sem("moe_stats"), g.sem("moe_aggr")
        with nc.Block() as block:

            @block.tensor
            def _(pe):
                for i in range(TT + 2):
                    if i < TT:
                        a = lambda k: (xh[:, k, i * P:(i + 1) * P], xl[:, k, i * P:(i + 1) * P])
                        if i >= 2:
                            pe.wait_ge(mul, i - 1)
                        for k in range(EK):
                            mm = product3(pe, pg[i % 2][:, :], a(k), (W["gate"][0][:, k, :], W["gate"][1][:, k, :]),
                                          start=(k == 0), stop=(k == EK - 1))
                        mm.then_inc(gate, 1)
                        for k in range(EK):
                            mm = product3(pe, pu[i % 2][:, :], a(k), (W["up"][0][:, k, :], W["up"][1][:, k, :]),
                                          start=(k == 0), stop=(k == EK - 1))
                        mm.then_inc(up, 1)
                    if 1 <= i <= TT:
                        n = i - 1
                        pe.wait_ge(gated, n + 1)
                        pe.wait_ge(lweighed, n + 1)
                        pe.wait_ge(low, 2 * n)
                        for f in range(FK):
                            pe.transpose(pt[:, f, :], gt[:, n % 2, f * P:(f + 1) * P], g.ident[:, :])
                        pe.transpose(pl[:, :], lw[:, n % 2, :], g.ident[:, :]).then_inc(turned, 1)
                    if i >= 2:
                        n = i - 2
                        pe.wait_ge(low, 2 * n + 2)
                        if n >= 2:
                            pe.wait_ge(added, n - 1)
                        for f in range(FK):
                            product3(pe, pd[n % 2][:, :], (gh[:, n % 2, f, :], gl[:, n % 2, f, :]),
                                     (W["down"][0][:, f, :], W["down"][1][:, f, :]), start=(f == 0), stop=False)
                        product3(pe, pd[n % 2][:, :], (lh[:, n % 2, :], ll[:, n % 2, :]),
                                 (W["loraB"][0], W["loraB"][1]), start=False, stop=True).then_inc(down, 1)

            @block.scalar
            def _(act):
                for i in range(TT + 1):
                    if i < TT:
                        act.wait_ge(gate, i + 1)
                        if i >= 2:
                            act.wait_ge(mul, i - 1)
                        act.activation(sg[:, i % 2, :], pg[i % 2][:, :], ACT.Silu).then_inc(silu, 1)
                    if i >= 1:
                        n = i - 1
                        act.wait_ge(turned, n + 1)
                        if n >= 2:
                            act.wait_ge(down, n - 1)
                        act.activation(gh[:, n % 2, :, :], pt[:, :, :], ACT.Copy).then_inc(high, 1)
                        act.activation(lh[:, n % 2, :], pl[:, :], ACT.Copy).then_inc(high, 1)

            @block.vector
            def _(dve):
                for i in range(TT + 2):
                    if i < TT:
                        dve.wait_ge(silu, i + 1)
                        dve.wait_ge(up, i + 1)
                        dve.tensor_tensor(sg[:, i % 2, :], sg[:, i % 2, :], pu[i % 2][:, :], ALU.mult).then_inc(mul, 1)
                        if i >= 2:
                            dve.wait_ge(turned, i - 1)
                        dve.tensor_tensor(lw[:, i % 2, :].rearrange("p (e r) -> p e r", r=RANK),
                                          lr[:, i, :].rearrange("p (e r) -> p e r", r=RANK),
                                          w[:, i, :].unsqueeze(2).to_broadcast([P, EX, RANK]), ALU.mult).then_inc(lweighed, 1)
                        dve.wait_ge(mul, i + 1)
                        dve.tensor_tensor(gt[:, i % 2, :].rearrange("p (e f) -> p e f", f=EF),
                                          sg[:, i % 2, :].rearrange("p (e f) -> p e f", f=EF),
                                          w[:, i, :].unsqueeze(2).to_broadcast([P, EX, EF]), ALU.mult).then_inc(gated, 1)
                    if 1 <= i <= TT:
                        n = i - 1
                        if n >= 2:
                            dve.wait_ge(down, n - 1)
                        dve.wait_ge(high, 2 * n + 2)
                        dve.tensor_tensor(gl[:, n % 2, :, :], pt[:, :, :], gh[:, n % 2, :, :].bitcast(F32), ALU.subtract).then_inc(low, 1)
                        dve.tensor_tensor(ll[:, n % 2, :], pl[:, :], lh[:, n % 2, :].bitcast(F32), ALU.subtract).then_inc(low, 1)
                    if i >= 2:
                        n = i - 2
                        dve.wait_ge(down, n + 1)
                        dve.tensor_tensor(X[:, n, :], pd[n % 2][:, :], X[:, n, :], ALU.add).then_inc(added, 1)
                        dve.wait_ge(added, n + 1)
                        dve.bn_stats(st[:, n % 2, :], X[:, n, :]).then_inc(stats, 1)
                        dve.wait_ge(stats, n + 1)
                        dve.bn_aggr(mv[:, n, :], st[:, n % 2, :]).then_inc(aggr, 1)


def parts(nc, ctx, name, shape):
    return tuple(ctx.enter_context(nc.sbuf_tensor(f"{name}_{s}", shape, F32R)) for s in ("high", "low"))


NH = 64
HP = 64
DI = NH * HP
NS = 128
TAPS = 4
CL = P
XO, BO, DTO = DI, 2 * DI, 2 * DI + 2 * NS
GH = 4
GROUPS = NH // GH
GC = GH * HP
GT = GC // P
HALVES = 2
HC = TT // HALVES
HT = HC * CL
KINDS = 4


def scan_inputs(nc, g, xh, xl, W, ch, dt_bias, A_log, D):
    with ExitStack() as ctx:
        sb = lambda name, shape, dt=F32: ctx.enter_context(nc.sbuf_tensor(name, shape, dt))
        raw = sb("si_raw", [P, 2, TAPS - 1 + T])
        acc = sb("si_acc", [P, 2, T])
        BT, CT = acc[:, 0, :], acc[:, 1, :]
        z = sb("si_z", [P, TT, NH])
        bias = sb("si_bias", [P, NH])
        eA = sb("si_eA", [P, NH])
        dA = sb("si_dA", [P, TT, NH])
        vec_in, hist = g.sem("si_vec"), g.sem("si_hist")
        prod, read, dprod, dread = g.sem("si_prod"), g.sem("si_read"), g.sem("si_dprod"), g.sem("si_dread")
        conv, silu = g.sem("si_conv"), g.sem("si_silu")
        with ExitStack() as inner:
            ps = [inner.enter_context(nc.psum_tensor(f"si_ps{b}", [P, CHUNK], F32)) for b in range(8)]
            with nc.Block() as block:

                @block.sync
                def _(sp):
                    sp.dma_start(bias[:, :], dt_bias.partition_broadcast(P)).then_inc(vec_in, 16)
                    sp.dma_start(eA[:, :], A_log.partition_broadcast(P)).then_inc(vec_in, 16)

                @block.tensor
                def _(pe):
                    for n in range(2 * NCH):
                        j, c = n % 2, n // 2
                        for k in range(EK):
                            mm = product3(pe, ps[n][:, :], (W[0][:, k, j * P:(j + 1) * P], W[1][:, k, j * P:(j + 1) * P]),
                                          (xh[:, k, c * CHUNK:(c + 1) * CHUNK], xl[:, k, c * CHUNK:(c + 1) * CHUNK]),
                                          start=(k == 0), stop=(k == EK - 1))
                        mm.then_inc(prod, 1)
                    for i in range(TT):
                        if i < 8:
                            pe.wait_ge(read, i + 1)
                        else:
                            pe.wait_ge(dread, i - 7)
                        for k in range(EK):
                            mm = product3(pe, ps[i % 8][:, 0:NH], (xh[:, k, i * P:(i + 1) * P], xl[:, k, i * P:(i + 1) * P]),
                                          (W[0][:, k, 2 * NS:], W[1][:, k, 2 * NS:]), start=(k == 0), stop=(k == EK - 1))
                        mm.then_inc(dprod, 1)

                @block.scalar
                def _(act):
                    for n in range(2 * NCH):
                        j, c = n % 2, n // 2
                        act.wait_ge(prod, n + 1)
                        act.activation(raw[:, j, TAPS - 1 + c * CHUNK:TAPS - 1 + (c + 1) * CHUNK], ps[n][:, :],
                                       ACT.Copy).then_inc(read, 1)
                    for i in range(TT):
                        act.wait_ge(dprod, i + 1)
                        act.activation(z[:, i, :], ps[i % 8][:, 0:NH], ACT.Copy).then_inc(dread, 1)
                    act.wait_ge(conv, 8)
                    for j in range(2):
                        act.activation(acc[:, j, :], acc[:, j, :], ACT.Silu).then_inc(silu, 1)
                    act.wait_ge(vec_in, 32)
                    act.activation(eA[:, :], eA[:, :], ACT.Exp).then_inc(silu, 1)
                    act.wait_ge(silu, 3)

                @block.vector
                def _(dve):
                    for j in range(2):
                        dve.memset(raw[:, j, 0:TAPS - 1], 0.0).then_inc(hist, 1)
                    dve.wait_ge(hist, 2)
                    dve.wait_ge(read, 2 * NCH)
                    for tap in range(TAPS):
                        for j in range(2):
                            src = raw[:, j, tap:tap + T]
                            w = ch[:, DI // P + j, tap:tap + 1]
                            if tap == 0:
                                dve.tensor_scalar(acc[:, j, :], src, w, ch[:, DI // P + j, TAPS:TAPS + 1], ALU.mult,
                                                  ALU.add).then_inc(conv, 1)
                            else:
                                dve.wait_ge(conv, 2 * tap + j - 1)
                                dve.scalar_tensor_tensor(out=acc[:, j, :], in0=src, scalar=w, in1=acc[:, j, :],
                                                         op0=ALU.mult, op1=ALU.add).then_inc(conv, 1)

        u, s, s2, q = (raw[:, j, h * TT * NH:(h + 1) * TT * NH] for j in range(2) for h in range(2))
        step, exped = g.sem("si_step"), g.sem("si_exped")
        zf = z[:, :, :].rearrange("p c h -> p (c h)")
        with nc.Block() as block:

            @block.scalar
            def _(act):
                act.wait_ge(step, 2)
                act.activation(u, u, ACT.Exp, scale=-1.0).then_inc(exped, 1)

            @block.vector
            def _(dve):
                n = [0]

                def then(ins):
                    ins.then_inc(step, 1)
                    n[0] += 1
                    dve.wait_ge(step, n[0])

                then(dve.tensor_tensor(z[:, :, :], z[:, :, :], bias[:, :].unsqueeze(1).to_broadcast([P, TT, NH]), ALU.add))
                then(dve.scalar_tensor_tensor(out=u, in0=zf, scalar=-1.0, in1=zf, op0=ALU.mult, op1=ALU.max))
                dve.wait_ge(exped, 1)
                then(dve.tensor_scalar(s, u, 2.0, None, ALU.add))
                then(dve.reciprocal(s, s))
                then(dve.tensor_tensor(s, s, u, ALU.mult))
                then(dve.tensor_tensor(s2, s, s, ALU.mult))
                then(dve.tensor_scalar(q, s2, 1.0 / 15, None, ALU.mult))
                for k in (13, 11, 9, 7, 5, 3):
                    then(dve.scalar_tensor_tensor(out=q, in0=q, scalar=1.0 / k, in1=s2, op0=ALU.add,
                                                  op1=ALU.mult))
                then(dve.scalar_tensor_tensor(out=q, in0=q, scalar=1.0, in1=s, op0=ALU.add, op1=ALU.mult))
                then(dve.tensor_scalar(zf, zf, 0.0, None, ALU.max))
                then(dve.scalar_tensor_tensor(out=zf, in0=q, scalar=2.0, in1=zf, op0=ALU.mult, op1=ALU.add))
                then(dve.scalar_tensor_tensor(out=dA[:, :, :], in0=z[:, :, :], scalar=-1.0,
                                              in1=eA[:, :].unsqueeze(1).to_broadcast([P, TT, NH]), op0=ALU.mult, op1=ALU.mult))

        sm = sb("si_small", [P, GROUPS, HALVES, KINDS, HC, GH])
        upto, after, ones = sb("si_upto", [P, P]), sb("si_after", [P, P]), sb("si_ones", [P, P])
        made, summed, sexp, copied = g.sem("si_made"), g.sem("si_summed"), g.sem("si_sexp"), g.sem("si_copied")
        stored = g.sem("si_stored")
        with ExitStack() as inner:
            ps = [inner.enter_context(nc.psum_tensor(f"si_sum{b}", [P, HC, NH], F32)) for b in range(6)]
            with nc.Block() as block:

                @block.gpsimd
                def _(pool):
                    for m in (upto, after, ones):
                        pool.memset(m[:, :], 1.0).then_inc(made, 1)
                    pool.wait_ge(made, 3)
                    pool.affine_select(out=upto[:, :], in_=upto[:, :], compare_op=ALU.is_ge, fill=0.0, base=0,
                                       pattern=[[1, P]], channel_multiplier=-1).then_inc(made, 1)
                    pool.affine_select(out=after[:, :], in_=after[:, :], compare_op=ALU.is_gt, fill=0.0, base=0,
                                       pattern=[[-1, P]], channel_multiplier=1).then_inc(made, 1)

                @block.tensor
                def _(pe):
                    pe.wait_ge(made, 5)
                    for q, m in enumerate((upto, after, ones)):
                        for hf in range(HALVES):
                            pe.matmul(ps[2 * q + hf][:, :, :], m[:, :], dA[:, hf * HC:(hf + 1) * HC, :],
                                      start=True, stop=True).then_inc(summed, 1)

                @block.scalar
                def _(act):
                    for q in range(3):
                        for hf in range(HALVES):
                            act.wait_ge(summed, 2 * q + hf + 1)
                            act.activation(sm[:, :, hf, q + 1, :, :],
                                           ps[2 * q + hf][:, :, :].rearrange("p c (g h) -> p g c h", h=GH), ACT.Exp).then_inc(sexp, 1)

                @block.vector
                def _(dve):
                    for hf in range(HALVES):
                        dve.tensor_copy(sm[:, :, hf, 0, :, :],
                                        z[:, hf * HC:(hf + 1) * HC, :].rearrange("p c (g h) -> p g c h", h=GH)).then_inc(copied, 1)

                @block.sync
                def _(sp):
                    sp.wait_ge(sexp, 6)
                    sp.wait_ge(copied, 2)
                    sp.dma_start(D["small"], sm[:, :, :, :, :, :].rearrange("p g f k c h -> p (g f k c h)")).then_inc(stored, 16)
                    sp.dma_start(D["C"], CT).then_inc(stored, 16)
                    sp.wait_ge(stored, 32)

        a1, a2, a3 = (sb(f"si_a{i}", [NH, T], BF16) for i in range(3))
        rest = sb("si_rest", [NH, 2, CHUNK])
        Bt, CB = (raw[:, j, 0:T].rearrange("p (c n) -> p c n", n=P) for j in range(2))
        aprod, apart, apdone, acopy = g.sem("si_aprod"), g.sem("si_apart"), g.sem("si_apdone"), g.sem("si_acopy")
        bprod, bread, cprod, cread = g.sem("si_bprod"), g.sem("si_bread"), g.sem("si_cprod"), g.sem("si_cread")
        with ExitStack() as inner:
            ps = [inner.enter_context(nc.psum_tensor(f"si_at{b}", [P, 4, P], F32)) for b in range(8)]
            with nc.Block() as block:

                @block.tensor
                def _(pe):
                    for n in range(4):
                        for c in range(4):
                            mm = pe.matmul(ps[n][0:NH, c, :], dA[:, 4 * n + c, :], upto[:, :], start=True, stop=True)
                        mm.then_inc(aprod, 1)
                    for n in range(4):
                        if n >= 2:
                            pe.wait_ge(bread, n - 1)
                        for c in range(4):
                            i = 4 * n + c
                            mm = pe.transpose(ps[4 + n % 2][:, c, :], BT[:, i * P:(i + 1) * P], g.ident[:, :])
                        mm.then_inc(bprod, 1)
                        if n >= 2:
                            pe.wait_ge(cread, n - 1)
                        for c in range(4):
                            i = 4 * n + c
                            mm = pe.matmul(ps[6 + n % 2][:, c, :], BT[:, i * P:(i + 1) * P], CT[:, i * P:(i + 1) * P],
                                           start=True, stop=True)
                        mm.then_inc(cprod, 1)

                @block.scalar
                def _(act):
                    for n in range(4):
                        act.wait_ge(aprod, n + 1)
                        act.activation(a1[:, n * CHUNK:(n + 1) * CHUNK], ps[n][0:NH, :, :].rearrange("p c l -> p (c l)"),
                                       ACT.Copy).then_inc(acopy, 1)
                    for n in range(4):
                        act.wait_ge(bprod, n + 1)
                        act.activation(Bt[:, 4 * n:4 * n + 4, :], ps[4 + n % 2][:, :, :], ACT.Copy).then_inc(bread, 1)

                @block.vector
                def _(dve):
                    up = upto[:, :].unsqueeze(1).to_broadcast([P, 4, P])
                    for n in range(4):
                        sl = slice(n * CHUNK, (n + 1) * CHUNK)
                        dve.wait_ge(acopy, n + 1)
                        r = rest[:, n % 2, :]
                        dve.tensor_tensor(r, ps[n][0:NH, :, :].rearrange("p c l -> p (c l)"), a1[:, sl], ALU.subtract).then_inc(apart, 1)
                        dve.wait_ge(apart, 3 * n + 1)
                        dve.tensor_copy(a2[:, sl], r).then_inc(apart, 1)
                        dve.wait_ge(apart, 3 * n + 2)
                        dve.tensor_tensor(a3[:, sl], r, a2[:, sl], ALU.subtract).then_inc(apart, 1)
                    for n in range(4):
                        dve.wait_ge(cprod, n + 1)
                        dve.tensor_tensor(CB[:, 4 * n:4 * n + 4, :], ps[6 + n % 2][:, :, :], up, ALU.mult).then_inc(cread, 1)

                @block.sync
                def _(sp):
                    sp.wait_ge(apart, 12)
                    for n, a in enumerate((a1, a2, a3)):
                        sp.dma_start(D["sums"][n], a[:, :]).then_inc(apdone, 16)
                    sp.wait_ge(bread, 4)
                    sp.dma_start(D["B"], Bt).then_inc(apdone, 16)
                    sp.wait_ge(cread, 4)
                    sp.dma_start(D["CB"], CB).then_inc(apdone, 16)
                    sp.wait_ge(apdone, 80)


SLOTS = HC + 4
AK = 3 + 3 * GH


def scan_semaphores(g):
    names = ("xin w_raw w_high w_low wo_raw wo_scaled wo_high wo_low sums_in small_in state_in state_out "
             "ip ip_read hist conv_step conv silu coef dcoef arg exped decay xt xdt xdd y_prod s_prod y_scaled y_sum "
             "s_decayed s_next yt gate_sum gated g_high g_sq g_low sq_add sq_all op op_added setup acc_out").split()
    return {n: g.sem("sc_" + n) for n in names}


def scan_half(nc, g, hf, S, D, Wg, WoT, tables, hist, ssq_dram, acc_dram):
    NBK = HT // CHUNK
    CB4 = CHUNK // CL
    first = hf * GROUPS
    with ExitStack() as ctx:
        sb = lambda name, shape, dt=F32: ctx.enter_context(nc.sbuf_tensor(f"{name}_{hf}", shape, dt))
        pb = lambda name, shape: ctx.enter_context(nc.psum_tensor(f"{name}_{hf}", shape, F32))
        xh, xl = sb("sc_xh", [P, EK, HT], F32R), sb("sc_xl", [P, EK, HT], F32R)
        acc, ssq = sb("sc_acc", [P, HC, E]), sb("sc_ssq", [P, HT])
        Bt, Ct, CB = sb("sc_B", [P, HC, NS]), sb("sc_C", [P, HT]), sb("sc_CB", [P, HC, P])
        chan, dtab = sb("sc_chan", [P, 2 * GROUPS + 2, TAPS + 1]), sb("sc_dtab", [P, 2 * GROUPS, 2])
        coef, dcoef = sb("sc_coef", [P, GT, TAPS + 1]), sb("sc_dcoef", [P, GT, 2])
        ncoef = sb("sc_ncoef", [P, GT, 2])
        later = sb("sc_later", [P, GH, P], BF16)
        wr, wh, wl = sb("sc_wr", [P, EK, CHUNK]), sb("sc_wh", [P, 4, EK, P], F32R), sb("sc_wl", [P, 4, EK, P], F32R)
        wor = sb("sc_wor", [P, GT, E])
        woh, wol = sb("sc_woh", [P, GT, E], F32R), sb("sc_wol", [P, GT, E], F32R)
        arhs, alhs = sb("sc_arhs", [AK, HC, GH, CL], BF16), sb("sc_alhs", [AK, HT], BF16)
        small = sb("sc_small", [P, KINDS, HC, GH])
        xr = [[sb(f"sc_xr{j}{b}", [P, TAPS - 1 + CHUNK]) for b in range(NBK)] for j in range(GT)]
        ca = sb("sc_ca", [P, GT, CHUNK])
        xT, zT = sb("sc_xT", [P, NBK, GT, CHUNK]), sb("sc_zT", [P, NBK, GT, CHUNK])
        M = [sb(f"sc_M{b}", [P, GH, CL]) for b in range(2)]
        xdt = [sb(f"sc_xdt{b}", [P, GH, HP]) for b in range(2)]
        xdd = [sb(f"sc_xdd{b}", [P, GH, HP]) for b in range(2)]
        ya = [sb(f"sc_y{b}", [P, GC]) for b in range(2)]
        st = [sb(f"sc_s{b}", [P, GC]) for b in range(2)]
        sd = sb("sc_sd", [P, GC])
        gx, sq = sb("sc_gx", [P, GT, 2 * CL]), sb("sc_sq", [P, GT, 2 * CL])
        gh = [sb(f"sc_gh{b}", [P, GT, 2 * CL], F32R) for b in range(2)]
        gl = [sb(f"sc_gl{b}", [P, GT, 2 * CL], F32R) for b in range(2)]
        p_ip = [pb(f"sc_pip{b}", [P, CHUNK]) for b in range(2)]
        p_arg, p_xt, p_y, p_s = pb("sc_parg", [P, GH, CL]), pb("sc_pxt", [P, GC]), pb("sc_py", [P, 2, GC]), pb("sc_ps", [P, GC])
        p_yt, p_op = pb("sc_pyt", [P, GT, 2, CL]), pb("sc_pop", [P, E])

        def wait(e, name, value):
            if not (isinstance(value, int) and value <= 0):
                e.wait_ge(S[name], value)

        q_ip = lambda G, blk, m: G * 8 + hf * 4 + blk * 4 + m
        q_cv = lambda G, blk, j: G * 4 + hf * 2 + blk * 2 + j
        q_st = lambda G, s: G * HC + s - GROUPS if hf else G * (HC - 1) + s - 1
        q_w = lambda G, m: G * 4 + hf * 4 + m

        def bc(kind, c):
            return small[:, kind, c, :].unsqueeze(2).to_broadcast([P, GH, HP])

        heads = lambda a: a.rearrange("p (h d) -> p h d", d=HP)
        n_setup = 9
        with nc.Block() as block:

            @block.sync
            def _(sp):
                for src, dst in ((D["xT"][0], xh), (D["xT"][1], xl)):
                    sp.dma_start(dst[:, :, :].bitcast(F32), src[:, :, hf * HT:(hf + 1) * HT]).then_inc(S["xin"], 16)
                sp.dma_start(Bt[:, :, :], D["B"][:, hf * HC:(hf + 1) * HC, :]).then_inc(S["xin"], 16)
                sp.dma_start(Ct[:, :], D["C"][:, hf * HT:(hf + 1) * HT]).then_inc(S["xin"], 16)
                sp.dma_start(CB[:, :, :], D["CB"][:, hf * HC:(hf + 1) * HC, :]).then_inc(S["xin"], 16)
                sp.dma_start(chan[:, :, :], tables[0]).then_inc(S["xin"], 16)
                sp.dma_start(dtab[:, :, :], tables[1]).then_inc(S["xin"], 16)

                def load_w(grp):
                    sp.dma_start(wr[:, :, :], Wg[ds(grp, 1), :, :].rearrange("o (k p) n -> p (o k) n", p=P)).then_inc(S["w_raw"], 16)

                def load_wo(grp):
                    sp.dma_start(wor[:, :, :], WoT[ds(grp * GC, GC), :].rearrange("(j p) n -> p j n", p=P)).then_inc(S["wo_raw"], 16)

                def load_sums(grp):
                    for n in range(3):
                        src = D["sums"][n, ds(grp * GH, GH), hf * HT:(hf + 1) * HT]
                        sp.dma_start(arhs[n:n + 1, :, :, :], src.rearrange("h (c l) -> c h l", l=CL).unsqueeze(0)).then_inc(S["sums_in"], 16)
                        sp.dma_start(alhs[3 + GH * n:3 + GH * (n + 1), :], src).then_inc(S["sums_in"], 16)

                def load_small(grp):
                    sp.dma_start(small[:, :, :, :].rearrange("p k c h -> p (k c h)"),
                                 D["small"][:, ds((grp * HALVES + hf) * KINDS * HC * GH, KINDS * HC * GH)]).then_inc(S["small_in"], 16)

                def load_state(grp):
                    if hf == 1:
                        sp.dma_start(st[0][:, :], D["state"][ds(grp, 1), :, :].rearrange("o p n -> p (o n)")).then_inc(S["state_in"], 16)

                load_w(0)
                sp.wait_ge(S["setup"], n_setup * (hf + 1))
                load_wo(0)
                load_sums(0)
                load_small(0)
                load_state(0)

                def after_group(G, grp, last):
                    sp.wait_ge(S["w_low"], q_w(G, 4))
                    load_w(grp if last else grp + 1)
                    sp.wait_ge(S["wo_low"], G + 1)
                    if not last:
                        load_wo(grp + 1)
                    sp.wait_ge(S["arg"], G * HC + HC)
                    if not last:
                        load_sums(grp + 1)
                    sp.wait_ge(S["s_next"], G * HC + HC)
                    sp.wait_ge(S["y_sum"], G * HC + HC)
                    sp.wait_ge(S["xdd"], G * HC + HC)
                    if not last:
                        load_small(grp + 1)
                    if hf == 0:
                        sp.dma_start(D["state"][ds(grp, 1), :, :].rearrange("o p n -> p (o n)"), st[0][:, :]).then_inc(S["state_out"], 16)
                    elif not last:
                        load_state(grp + 1)

                with sp.Fori(first, first + GROUPS - 1) as G:
                    after_group(G, G - first, False)
                after_group(first + GROUPS - 1, GROUPS - 1, True)
                if hf == 0:
                    sp.wait_ge(S["state_out"], 16 * GROUPS)
                sp.wait_ge(S["op_added"], (first + GROUPS) * HC)
                sp.dma_start(acc_dram[:, hf * HC:(hf + 1) * HC, :], acc[:, :, :]).then_inc(S["acc_out"], 16)
                sp.wait_ge(S["sq_add"], (first + GROUPS) * 8)
                sp.dma_start(ssq_dram[:, hf * HT:(hf + 1) * HT], ssq[:, :]).then_inc(S["acc_out"], 16)
                sp.wait_ge(S["acc_out"], 32 * (hf + 1))
                sp.wait_ge(S["w_raw"], 16 * (GROUPS + 1) * (hf + 1))

            @block.gpsimd
            def _(pool):
                s0 = n_setup * hf
                pool.memset(later[:, :, :], 0.0).then_inc(S["setup"], 1)
                pool.memset(arhs[:, :, :, :], 0.0).then_inc(S["setup"], 1)
                pool.memset(alhs[:, :], 1.0).then_inc(S["setup"], 1)
                pool.memset(acc[:, :, :], 0.0).then_inc(S["setup"], 1)
                pool.memset(ssq[:, :], 0.0).then_inc(S["setup"], 1)
                pool.wait_ge(S["setup"], s0 + 5)
                pool.affine_select(out=later[:, :, :], in_=later[:, :, :], compare_op=ALU.is_ge, fill=NEG, base=0,
                                   pattern=[[0, GH], [1, CL]], channel_multiplier=-1).then_inc(S["setup"], 1)
                for n in range(3):
                    pool.affine_select(out=arhs[:, :, :, :], in_=arhs[:, :, :, :], compare_op=ALU.not_equal, fill=-1.0,
                                       base=-3 - GH * n, pattern=[[0, HC], [-1, GH], [0, CL]],
                                       channel_multiplier=1).then_inc(S["setup"], 1)
                    pool.wait_ge(S["setup"], s0 + 7 + n)

                for m in range(4):
                    src = wr[:, :, m * P:(m + 1) * P]
                    pool.wait_ge(S["w_high"], q_w(first, m) + 1)
                    pool.tensor_tensor(wl[:, m, :, :], src, wh[:, m, :, :].bitcast(F32), ALU.subtract).then_inc(S["w_low"], 1)
                with pool.Fori(first, first + GROUPS) as G:
                    for s in range(-1, SLOTS):
                        c = s + 1
                        if c < HC:
                            pool.wait_ge(S["xdt"], G * HC + c + 1)
                            pool.wait_ge(S["s_prod"], G * HC + max(c - 1, 0))
                            pool.tensor_tensor(xdd[c % 2][:, :, :], xdt[c % 2][:, :, :], bc(2, c), ALU.mult).then_inc(S["xdd"], 1)
                        if s == -1:
                            pool.wait_ge(S["wo_high"], G + 1)
                            pool.tensor_tensor(wol[:, :, :], wor[:, :, :], woh[:, :, :].bitcast(F32), ALU.subtract).then_inc(S["wo_low"], 1)
                        if 0 <= s < HC:
                            if s == 0:
                                if hf == 0:
                                    continue
                                pool.wait_ge(S["small_in"], (G + 1) * 16)
                                pool.wait_ge(S["state_in"], (G - first + 1) * 16)
                            pool.wait_ge(S["s_next"], G * HC + s)
                            pool.tensor_tensor(heads(sd[:, :]), heads(st[s % 2][:, :]), bc(3, s), ALU.mult).then_inc(S["s_decayed"], 1)
                        if s in (2, 4, 6, 8):
                            p = s // 2 - 1
                            pool.wait_ge(S["g_sq"], G * 4 + p + 1)
                            for j in range(GT):
                                pool.wait_ge(S["sq_add"], (G * 4 + p) * 2 + j)
                                part = ssq[:, p * 2 * CL:(p + 1) * 2 * CL]
                                pool.tensor_tensor(part, part, sq[:, j, :], ALU.add).then_inc(S["sq_add"], 1)
                        if 3 <= s < 7:
                            m = s - 3
                            src = wr[:, :, m * P:(m + 1) * P]
                            pool.wait_ge(S["w_high"], q_w(G, m) + 5)
                            pool.tensor_tensor(wl[:, m, :, :], src, wh[:, m, :, :].bitcast(F32), ALU.subtract).then_inc(S["w_low"], 1)

            @block.tensor
            def _(pe):
                def ip(G, blk, m):
                    wait(pe, "w_low", q_w(G, m) + 1)
                    wait(pe, "ip_read", q_ip(G, blk, m) - 1)
                    for k in range(EK):
                        mm = product3(pe, p_ip[m % 2][:, :], (wh[:, m, k, :], wl[:, m, k, :]),
                                      (xh[:, k, blk * CHUNK:(blk + 1) * CHUNK], xl[:, k, blk * CHUNK:(blk + 1) * CHUNK]),
                                      start=(k == 0), stop=(k == EK - 1))
                    mm.then_inc(S["ip"], 1)

                pe.wait_ge(S["xin"], 7 * 16 * (hf + 1))
                pe.wait_ge(S["setup"], n_setup * (hf + 1))
                for m in range(4):
                    ip(first, 0, m)
                with pe.Fori(first, first + GROUPS) as G:
                    for s in range(-1, SLOTS):
                        if 0 <= s < 4:
                            ip(G, 1, s)
                        if s >= HC:
                            ip(G + 1, 0, s - HC)
                        c = s + 1
                        if c < HC:
                            if c == 0:
                                pe.wait_ge(S["sums_in"], (G + 1) * 96)
                            pe.wait_ge(S["exped"], G * HC + c)
                            pe.matmul(p_arg[:, :, :], alhs[:, c * CL:(c + 1) * CL], arhs[:, c, :, :], start=True, stop=False)
                            pe.matmul(p_arg[:, :, :], g.identb[:, :], later[:, :, :], start=False, stop=True).then_inc(S["arg"], 1)
                            pe.wait_ge(S["silu"], q_cv(G, c // CB4, 1) + 1)
                            pe.wait_ge(S["xdt"], G * HC + c)
                            for j in range(GT):
                                mm = pe.transpose(p_xt[:, j * P:(j + 1) * P], xT[:, c // CB4, j, (c % CB4) * CL:(c % CB4 + 1) * CL],
                                                  g.ident[:, :])
                            mm.then_inc(S["xt"], 1)
                        if 0 <= s < HC:
                            pe.wait_ge(S["decay"], G * HC + s + 1)
                            pe.wait_ge(S["xdt"], G * HC + s + 1)
                            pe.wait_ge(S["y_sum"], G * HC + s)
                            for h in range(GH):
                                mm = pe.matmul(p_y[:, 0, h * HP:(h + 1) * HP], M[s % 2][:, h, :], xdt[s % 2][:, h, :], start=True, stop=True)
                            if s == 0 and hf == 1:
                                pe.wait_ge(S["state_in"], (G - first + 1) * 16)
                            pe.wait_ge(S["s_next"], G * HC + s)
                            if s or hf:
                                mm = pe.matmul(p_y[:, 1, :], Ct[:, s * CL:(s + 1) * CL], st[s % 2][:, :], start=True, stop=True)
                            mm.then_inc(S["y_prod"], 1)
                            pe.wait_ge(S["xdd"], G * HC + s + 1)
                            pe.matmul(p_s[:, :], Bt[:, s, :], xdd[s % 2][:, :, :], start=True, stop=True).then_inc(S["s_prod"], 1)
                        if 1 <= s <= HC:
                            c = s - 1
                            pe.wait_ge(S["y_sum"], G * HC + c + 1)
                            if c % 2 == 0:
                                pe.wait_ge(S["gate_sum"], (G * 4 + c // 2) * 2)
                            for j in range(GT):
                                mm = pe.transpose(p_yt[:, j, c % 2, :], ya[c % 2][:, j * P:(j + 1) * P], g.ident[:, :])
                            mm.then_inc(S["yt"], 1)
                        if s >= 4:
                            c = s - 4
                            if c == 0:
                                pe.wait_ge(S["wo_low"], G + 1)
                            pe.wait_ge(S["g_low"], G * 4 + c // 2 + 1)
                            pe.wait_ge(S["op_added"], G * HC + c)
                            b = (c // 2) % 2
                            for j in range(GT):
                                mm = product3(pe, p_op[:, :], (gh[b][:, j, (c % 2) * CL:(c % 2 + 1) * CL], gl[b][:, j, (c % 2) * CL:(c % 2 + 1) * CL]),
                                              (woh[:, j, :], wol[:, j, :]), start=(j == 0), stop=(j == GT - 1))
                            mm.then_inc(S["op"], 1)

            @block.scalar
            def _(act):
                def ip_read(G, blk, m):
                    act.wait_ge(S["ip"], q_ip(G, blk, m) + 1)
                    if m < GT:
                        wait(act, "conv", q_cv(G, blk, m) - 1)
                        act.activation(xr[m][blk][:, TAPS - 1:], p_ip[m % 2][:, :], ACT.Copy).then_inc(S["ip_read"], 1)
                    else:
                        wait(act, "gated", G * 4 + 2 * blk - 2)
                        act.activation(zT[:, blk, m - GT, :], p_ip[m % 2][:, :], ACT.Silu).then_inc(S["ip_read"], 1)

                def silu(G, blk, j):
                    act.wait_ge(S["conv"], q_cv(G, blk, j) + 1)
                    wait(act, "gated", G * 4 + 2 * blk - 2)
                    wait(act, "xt", G * HC + (blk + 1) * CB4 - HC)
                    act.activation(xT[:, blk, j, :], ca[:, j, :], ACT.Silu).then_inc(S["silu"], 1)

                def w_high(m):
                    act.activation(wh[:, m, :, :], wr[:, :, m * P:(m + 1) * P], ACT.Copy).then_inc(S["w_high"], 1)

                act.wait_ge(S["w_raw"], ((GROUPS + 1) * hf + 1) * 16)
                for m in range(4):
                    w_high(m)
                for m in range(4):
                    ip_read(first, 0, m)
                    if m >= 1 and m - 1 < GT:
                        silu(first, 0, m - 1)
                with act.Fori(first, first + GROUPS) as G:
                    for s in range(-1, SLOTS):
                        c = s + 1
                        if c < HC:
                            act.wait_ge(S["arg"], G * HC + c + 1)
                            act.wait_ge(S["y_prod"], G * HC + max(c - 1, 0))
                            act.activation(M[c % 2][:, :, :], p_arg[:, :, :], ACT.Exp).then_inc(S["exped"], 1)
                        for at, Gn, blk in ((0, G, 1), (HC, G + 1, 0)):
                            if at <= s < at + 4:
                                ip_read(Gn, blk, s - at)
                            if at + 1 <= s < at + 1 + GT:
                                silu(Gn, blk, s - at - 1)
                        if s in (2, 4, 6, 8):
                            p = s // 2 - 1
                            act.wait_ge(S["gated"], G * 4 + p + 1)
                            act.wait_ge(S["op"], G * HC + max(2 * p - 2, 0))
                            act.activation(gh[p % 2][:, :, :], gx[:, :, :], ACT.Copy).then_inc(S["g_high"], 1)
                            act.wait_ge(S["sq_add"], (G * 4 + p) * 2)
                            act.activation(sq[:, :, :], gx[:, :, :], ACT.Square).then_inc(S["g_sq"], 1)
                        if s == 0:
                            act.wait_ge(S["wo_raw"], (G + 1) * 16)
                            act.wait_ge(S["dcoef"], G + 1)
                            act.wait_ge(S["op"], G * HC)
                            for j in range(GT):
                                act.activation(wor[:, j, :], wor[:, j, :], ACT.Copy, scale=ncoef[:, j, 1:2]).then_inc(S["wo_scaled"], 1)
                            act.wait_ge(S["wo_scaled"], (G + 1) * GT)
                            act.activation(woh[:, :, :], wor[:, :, :], ACT.Copy).then_inc(S["wo_high"], 1)
                        if 3 <= s < 7:
                            m = s - 3
                            act.wait_ge(S["w_raw"], (G + hf + 2) * 16)
                            act.wait_ge(S["ip"], q_ip(G, 1, m) + 1)
                            w_high(m)

            @block.vector
            def _(dve):
                def conv(G, blk, j):
                    grp = G - first
                    n = 4 * q_cv(G, blk, j)
                    dve.wait_ge(S["ip_read"], q_ip(G, blk, j) + 1)
                    if blk == 0:
                        before = hist[:, ds(grp * GT + j, 1), :].rearrange("p o k -> p (o k)")
                    else:
                        before = xr[j][0][:, CHUNK:CHUNK + TAPS - 1]
                    dve.tensor_copy(xr[j][blk][:, 0:TAPS - 1], before).then_inc(S["conv_step"], 1)
                    dve.wait_ge(S["conv_step"], n + 1)
                    if blk == NBK - 1:
                        dve.tensor_copy(hist[:, ds(grp * GT + j, 1), :].rearrange("p o k -> p (o k)"),
                                        xr[j][blk][:, CHUNK:CHUNK + TAPS - 1]).then_inc(S["hist"], 1)
                    wait(dve, "silu", q_cv(G, blk, j) - 1)
                    for tap in range(TAPS):
                        src = xr[j][blk][:, tap:tap + CHUNK]
                        w = coef[:, j, tap:tap + 1]
                        if tap == 0:
                            dve.tensor_scalar(ca[:, j, :], src, w, coef[:, j, TAPS:TAPS + 1], ALU.mult,
                                              ALU.add).then_inc(S["conv_step"], 1)
                        else:
                            dve.wait_ge(S["conv_step"], n + 1 + tap)
                            last = tap == TAPS - 1
                            dve.scalar_tensor_tensor(out=ca[:, j, :], in0=src, scalar=w, in1=ca[:, j, :], op0=ALU.mult,
                                                     op1=ALU.add).then_inc(S["conv" if last else "conv_step"], 1)

                def coefficients(G):
                    dve.tensor_copy(coef[:, :, :], chan[:, ds((G - first) * GT, GT), :]).then_inc(S["coef"], 1)
                    dve.wait_ge(S["coef"], G + hf + 1)

                dve.wait_ge(S["xin"], 7 * 16 * (hf + 1))
                coefficients(first)
                for j in range(GT):
                    conv(first, 0, j)
                with dve.Fori(first, first + GROUPS) as G:
                    for s in range(-1, SLOTS):
                        if s == -1:
                            dve.wait_ge(S["wo_scaled"], G * GT)
                            dve.tensor_copy(dcoef[:, :, :], dtab[:, ds((G - first) * GT, GT), :])
                            dve.tensor_copy(ncoef[:, :, :], dtab[:, ds((G - first) * GT, GT), :]).then_inc(S["dcoef"], 1)
                            dve.wait_ge(S["dcoef"], G + 1)
                            dve.wait_ge(S["small_in"], (G + 1) * 16)
                        if 1 <= s < 1 + GT:
                            conv(G, 1, s - 1)
                        c = s + 1
                        if c < HC:
                            dve.wait_ge(S["xt"], G * HC + c + 1)
                            dve.wait_ge(S["y_prod"], G * HC + max(c - 1, 0))
                            dve.wait_ge(S["xdd"], G * HC + max(c - 1, 0))
                            dve.tensor_tensor(xdt[c % 2][:, :, :], heads(p_xt[:, :]), bc(0, c), ALU.mult).then_inc(S["xdt"], 1)
                            dve.wait_ge(S["exped"], G * HC + c + 1)
                            dve.tensor_tensor(M[c % 2][:, :, :], M[c % 2][:, :, :],
                                              CB[:, c, :].unsqueeze(1).to_broadcast([P, GH, CL]), ALU.mult).then_inc(S["decay"], 1)
                        if 0 <= s < HC:
                            dve.wait_ge(S["y_prod"], G * HC + s + 1)
                            dve.wait_ge(S["yt"], G * HC + max(s - 1, 0))
                            if s == 0 and hf == 0:
                                dve.tensor_copy(ya[0][:, :], p_y[:, 0, :]).then_inc(S["y_sum"], 1)
                                dve.wait_ge(S["s_prod"], G * HC + 1)
                                dve.tensor_copy(st[1][:, :], p_s[:, :]).then_inc(S["s_next"], 1)
                            else:
                                dve.tensor_tensor(heads(ya[s % 2][:, :]), heads(p_y[:, 1, :]), bc(1, s), ALU.mult).then_inc(S["y_scaled"], 1)
                                dve.wait_ge(S["y_scaled"], q_st(G, s) + 1)
                                dve.tensor_tensor(ya[s % 2][:, :], ya[s % 2][:, :], p_y[:, 0, :], ALU.add).then_inc(S["y_sum"], 1)
                                dve.wait_ge(S["s_prod"], G * HC + s + 1)
                                dve.wait_ge(S["s_decayed"], q_st(G, s) + 1)
                                if s == 1 and hf == 0:
                                    dve.wait_ge(S["state_out"], G * 16)
                                dve.tensor_tensor(st[(s + 1) % 2][:, :], sd[:, :], p_s[:, :], ALU.add).then_inc(S["s_next"], 1)
                        if s == HC:
                            coefficients(G + 1)
                        if HC + 1 <= s < HC + 1 + GT:
                            conv(G + 1, 0, s - HC - 1)
                        if s in (2, 4, 6, 8):
                            p = s // 2 - 1
                            blk, at = p // 2, (p % 2) * 2 * CL
                            dve.wait_ge(S["yt"], G * HC + 2 * p + 2)
                            dve.wait_ge(S["g_sq"], G * 4 + p)
                            dve.wait_ge(S["g_low"], G * 4 + p)
                            for j in range(GT):
                                dve.scalar_tensor_tensor(out=gx[:, j, :], in0=xT[:, blk, j, at:at + 2 * CL], scalar=dcoef[:, j, 0:1],
                                                         in1=p_yt[:, j, :, :].rearrange("p a l -> p (a l)"), op0=ALU.mult,
                                                         op1=ALU.add).then_inc(S["gate_sum"], 1)
                            dve.wait_ge(S["ip_read"], q_ip(G, blk, 3) + 1)
                            dve.wait_ge(S["gate_sum"], (G * 4 + p + 1) * 2)
                            dve.tensor_tensor(gx[:, :, :], gx[:, :, :], zT[:, blk, :, at:at + 2 * CL], ALU.mult).then_inc(S["gated"], 1)
                            dve.wait_ge(S["g_high"], G * 4 + p + 1)
                            dve.tensor_tensor(gl[p % 2][:, :, :], gx[:, :, :], gh[p % 2][:, :, :].bitcast(F32), ALU.subtract).then_inc(S["g_low"], 1)
                        if s >= 4:
                            c = s - 4
                            dve.wait_ge(S["op"], G * HC + c + 1)
                            dve.tensor_tensor(acc[:, c, :], acc[:, c, :], p_op[:, :], ALU.add).then_inc(S["op_added"], 1)


def scan_end(nc, g, X, x_dram, acc_dram, ssq_dram, mv):
    with ExitStack() as ctx:
        sb = lambda name, shape, dt=F32: ctx.enter_context(nc.sbuf_tensor(name, shape, dt))
        ssq, ones = sb("se_ssq", [P, T]), sb("se_ones", [P, 1])
        acc = sb("se_acc", [P, 4, E])
        rstd = sb("se_rstd", [P, TT])
        stt = sb("se_stats", [P, 2, 6])
        ps = ctx.enter_context(nc.psum_tensor("se_ps", [P, TT], F32))
        x_in, ss_in, a_in = g.sem("se_x"), g.sem("se_ss"), [g.sem(f"se_a{b}") for b in range(4)]
        made, summed, step, root = g.sem("se_made"), g.sem("se_summed"), g.sem("se_step"), g.sem("se_root")
        added, stats, aggr = g.sem("se_added"), g.sem("se_stats"), g.sem("se_aggr")
        with nc.Block() as block:

            @block.gpsimd
            def _(pool):
                pool.memset(ones[:, :], 1.0).then_inc(made, 1)

            @block.sync
            def _(sp):
                sp.dma_start(ssq[:, :], ssq_dram).then_inc(ss_in, 16)
                sp.dma_start(X[:, :, :], x_dram.rearrange("(i p) n -> p i n", p=P)).then_inc(x_in, 16)
                for i in range(TT):
                    if i >= 4:
                        sp.wait_ge(added, i - 3)
                    sp.dma_start(acc[:, i % 4, :], acc_dram[:, i, :]).then_inc(a_in[i % 4], 16)

            @block.tensor
            def _(pe):
                pe.wait_ge(made, 1)
                pe.wait_ge(ss_in, 16)
                for i in range(TT):
                    mm = pe.matmul(ps[:, i:i + 1], ssq[:, i * P:(i + 1) * P], ones[:, :], start=True, stop=True)
                mm.then_inc(summed, 1)

            @block.scalar
            def _(act):
                act.wait_ge(step, 1)
                act.activation(rstd[:, :], rstd[:, :], ACT.Sqrt).then_inc(root, 1)

            @block.vector
            def _(dve):
                dve.wait_ge(summed, 1)
                dve.tensor_scalar(rstd[:, :], ps[:, :], 1.0 / DI, LN_EPS, ALU.mult, ALU.add).then_inc(step, 1)
                dve.wait_ge(root, 1)
                dve.reciprocal(rstd[:, :], rstd[:, :]).then_inc(step, 1)
                dve.wait_ge(step, 2)
                dve.wait_ge(x_in, 16)
                for i in range(TT):
                    dve.wait_ge(a_in[i % 4], 16 * (i // 4 + 1))
                    dve.scalar_tensor_tensor(out=X[:, i, :], in0=acc[:, i % 4, :], scalar=rstd[:, i:i + 1], in1=X[:, i, :],
                                             op0=ALU.mult, op1=ALU.add).then_inc(added, 1)
                    dve.wait_ge(added, i + 1)
                    dve.bn_stats(stt[:, i % 2, :], X[:, i, :]).then_inc(stats, 1)
                    dve.wait_ge(stats, i + 1)
                    dve.bn_aggr(mv[:, i, :], stt[:, i % 2, :]).then_inc(aggr, 1)


FF = 2048
FT = FF // P


def ffn(nc, g, X, xT_dram, Wgate, Wup, Wdown, scales, s_down, st_all):
    with ExitStack() as ctx:
        sb = lambda name, shape, dt=F32: ctx.enter_context(nc.sbuf_tensor(name, shape, dt))
        pb = lambda name: ctx.enter_context(nc.psum_tensor(name, [P, CHUNK], F32))
        w32 = sb("ff_w8", [P, 3, FF // 4], mybir.dt.int32)
        w8 = lambda slot: w32[:, slot, :].bitcast(mybir.dt.int8)
        wg, wu, wd = sb("ff_wg", [P, EK, FF], F32R), sb("ff_wu", [P, EK, FF], F32R), sb("ff_wd", [P, FT, E], F32R)
        sc, sdn = sb("ff_sc", [P, 2, FT]), sb("ff_sdn", [P, E])
        xb = [[sb(f"ff_x{p}{b}", [P, EK, CHUNK], F32R) for b in range(2)] for p in range(2)]
        sg, fz = sb("ff_sg", [P, 2, CHUNK]), sb("ff_fz", [P, 2, CHUNK])
        fh, fl = sb("ff_fh", [P, 2, CHUNK], F32R), sb("ff_fl", [P, 2, CHUNK], F32R)
        tmp = sb("ff_tmp", [P, E])
        res, stt = sb("ff_res", [P, 2, E]), sb("ff_stats", [P, 2, 6])
        pg, pu = [pb(f"ff_pg{b}") for b in range(2)], [pb(f"ff_pu{b}") for b in range(2)]
        pd = [pb(f"ff_pd{b}") for b in range(4)]
        w_in, vec_in = [g.sem(f"ff_w{b}") for b in range(3)], g.sem("ff_vec")
        x_in = [g.sem(f"ff_x{b}") for b in range(2)]
        made_a, made_d = g.sem("ff_made_a"), g.sem("ff_made_d")
        gate, up, silu, fused, high, low = (g.sem("ff_" + n) for n in ("gate", "up", "silu", "fused", "high", "low"))
        down, scaled, added, stats, kept = (g.sem("ff_" + n) for n in ("down", "scaled", "added", "stats", "kept"))
        rows = [(W[k * P:(k + 1) * P, :], w[:, k, :]) for W, w in ((Wgate, wg), (Wup, wu)) for k in range(EK)]
        rows += [(Wdown[4 * k * P:4 * (k + 1) * P, :].rearrange("(k p) n -> p k n", p=P), wd[:, 4 * k:4 * k + 4, :].rearrange("p k n -> p (k n)"))
                 for k in range(FT // 4)]
        NW = len(rows)
        ITER, PER = 2, 2 * FT
        with nc.Block() as block:

            @block.sync
            def _(sp):
                for n, (src, dst) in enumerate(rows):
                    if n >= 3:
                        sp.wait_ge((made_a, made_d)[(n - 3) % 2], (n - 3) // 2 + 1)
                    to = w32[:, n % 3, :]
                    if n >= 2 * EK:
                        to = to.rearrange("p (k n) -> p k n", k=4)
                    sp.dma_start(to, src).then_inc(w_in[n % 3], 16)
                    if n == 0:
                        sp.dma_start(sc[:, :, :], scales).then_inc(vec_in, 16)
                        sp.dma_start(sdn[:, :], s_down.partition_broadcast(P)).then_inc(vec_in, 16)
                        for b in range(2):
                            for p in range(2):
                                sp.dma_start(xb[p][b][:, :, :].bitcast(F32), xT_dram[p][:, :, b * CHUNK:(b + 1) * CHUNK]).then_inc(x_in[b], 16)
                for b in range(2):
                    sp.wait_ge(up, (b + 1) * FT)
                    for p in range(2):
                        sp.dma_start(xb[p][b][:, :, :].bitcast(F32), xT_dram[p][:, :, (2 + b) * CHUNK:(3 + b) * CHUNK]).then_inc(x_in[b], 16)

            @block.tensor
            def _(pe):
                pe.wait_ge(made_a, NW // 2)
                pe.wait_ge(made_d, NW // 2)
                with pe.Fori(0, ITER) as it:
                    for t in range(PER + 1):
                        if t < PER:
                            b, f = t // FT, t % FT
                            if f == 0:
                                pe.wait_ge(x_in[b], (it + 1) * 32)
                            pe.wait_ge(fused, it * PER + max(t - 1, 0))
                            for w, ps, s in ((wg, pg, gate), (wu, pu, up)):
                                for k in range(EK):
                                    for part in (1, 0):
                                        mm = pe.matmul(ps[t % 2][:, :], w[:, k, f * P:(f + 1) * P], xb[part][b][:, k, :],
                                                       start=(k == 0 and part == 1), stop=(k == EK - 1 and part == 0))
                                mm.then_inc(s, 1)
                        if t >= 1:
                            n = t - 1
                            f = n % FT
                            pe.wait_ge(low, it * PER + n + 1)
                            for i in range(4):
                                if f == 0:
                                    blk = it * 2 + n // FT
                                    if n // FT == 0:
                                        pe.wait_ge(scaled, blk * 4)
                                    else:
                                        pe.wait_ge(scaled, blk * 4 - 3 + i)
                                sl = slice(i * P, (i + 1) * P)
                                pe.matmul(pd[i][:, :], fl[:, n % 2, sl], wd[:, f, :], start=(f == 0), stop=False)
                                mm = pe.matmul(pd[i][:, :], fh[:, n % 2, sl], wd[:, f, :], start=False, stop=(f == FT - 1))
                            mm.then_inc(down, 1)

            @block.scalar
            def _(act):
                for n in range(0, NW, 2):
                    act.wait_ge(w_in[n % 3], 16 * (n // 3 + 1))
                    act.activation(rows[n][1], w8(n % 3), ACT.Copy).then_inc(made_a, 1)
                act.wait_ge(vec_in, 32)
                with act.Fori(0, ITER) as it:
                    for t in range(PER + 1):
                        f = t % FT
                        if t < PER:
                            act.wait_ge(gate, it * PER + t + 1)
                            act.activation(sg[:, t % 2, :], pg[t % 2][:, :], ACT.Silu, scale=sc[:, 0, f:f + 1]).then_inc(silu, 1)
                            act.wait_ge(fused, it * PER + t + 1)
                            act.wait_ge(down, it * PER + max(t - 1, 0))
                            act.activation(fh[:, t % 2, :], fz[:, t % 2, :], ACT.Copy).then_inc(high, 1)
                        if t >= 1 and f == 0:
                            for i in range(4):
                                n = (it * 2 + t // FT - 1) * 4 + i
                                act.wait_ge(added, n + 1)
                                act.activation(X[:, ds(n, 1), :].rearrange("p o n -> p (o n)"), res[:, i % 2, :], ACT.Copy).then_inc(kept, 1)
                                act.wait_ge(stats, n + 1)
                                act.activation(st_all[:, ds(n, 1), :].rearrange("p o n -> p (o n)"), stt[:, i % 2, :], ACT.Copy).then_inc(kept, 1)

            @block.vector
            def _(dve):
                for n in range(1, NW, 2):
                    dve.wait_ge(w_in[n % 3], 16 * (n // 3 + 1))
                    dve.tensor_copy(rows[n][1], w8(n % 3)).then_inc(made_d, 1)
                dve.wait_ge(vec_in, 32)
                with dve.Fori(0, ITER) as it:
                    for t in range(PER + 1):
                        if t < PER:
                            f = t % FT
                            dve.wait_ge(silu, it * PER + t + 1)
                            dve.wait_ge(up, it * PER + t + 1)
                            dve.wait_ge(low, it * PER + max(t - 1, 0))
                            dve.scalar_tensor_tensor(out=fz[:, t % 2, :], in0=pu[t % 2][:, :], scalar=sc[:, 1, f:f + 1],
                                                     in1=sg[:, t % 2, :], op0=ALU.mult, op1=ALU.mult).then_inc(fused, 1)
                            dve.wait_ge(high, it * PER + t + 1)
                            dve.tensor_tensor(fl[:, t % 2, :], fz[:, t % 2, :], fh[:, t % 2, :].bitcast(F32), ALU.subtract).then_inc(low, 1)
                        if t >= 1 and t % FT == 0:
                            b = t // FT - 1
                            dve.wait_ge(down, it * PER + t)
                            for i in range(4):
                                n = (it * 2 + b) * 4 + i
                                dve.wait_ge(added, n)
                                dve.tensor_tensor(tmp[:, :], pd[i][:, :], sdn[:, :], ALU.mult).then_inc(scaled, 1)
                                dve.wait_ge(scaled, n + 1)
                                row = X[:, ds(n, 1), :].rearrange("p o n -> p (o n)")
                                dve.wait_ge(kept, 2 * (it * 8 + max(b * 4 + i - 1, 0)))
                                dve.tensor_tensor(res[:, i % 2, :], row, tmp[:, :], ALU.add).then_inc(added, 1)
                                dve.wait_ge(added, n + 1)
                                dve.bn_stats(stt[:, i % 2, :], res[:, i % 2, :]).then_inc(stats, 1)


def norm_out(nc, g, X, st_all, out):
    with ExitStack() as ctx:
        mv = ctx.enter_context(nc.sbuf_tensor("no_mv", [P, TT, 2], F32))
        rstd = ctx.enter_context(nc.sbuf_tensor("no_rstd", [P, TT], F32))
        eps, root, inv, normed, stored = (g.sem("no_" + n) for n in ("eps", "root", "inv", "normed", "stored"))
        aggr = g.sem("no_aggr")
        with nc.Block() as block:

            @block.scalar
            def _(act):
                act.wait_ge(eps, 1)
                act.activation(rstd[:, :], rstd[:, :], ACT.Sqrt).then_inc(root, 1)

            @block.vector
            def _(dve):
                for i in range(TT):
                    dve.bn_aggr(mv[:, i, :], st_all[:, i, :]).then_inc(aggr, 1)
                dve.wait_ge(aggr, TT)
                dve.tensor_scalar(rstd[:, :], mv[:, :, 1], LN_EPS, None, ALU.add).then_inc(eps, 1)
                dve.wait_ge(root, 1)
                dve.reciprocal(rstd[:, :], rstd[:, :]).then_inc(inv, 1)
                dve.wait_ge(inv, 1)
                for i in range(TT):
                    dve.tensor_scalar(X[:, i, :], X[:, i, :], mv[:, i, 0:1], rstd[:, i:i + 1], ALU.subtract,
                                      ALU.mult).then_inc(normed, 1)

            @block.sync
            def _(sp):
                for i in range(0, TT, 2):
                    sp.wait_ge(normed, i + 2)
                    sp.dma_start(out[i * P:(i + 2) * P, :].rearrange("(i p) n -> p i n", p=P), X[:, i:i + 2, :]).then_inc(stored, 16)
                sp.wait_ge(stored, 16 * TT // 2)


class Shared:

    def __init__(self, nc, ctx):
        self.nc, self.ctx, self.turns, self.sems = nc, ctx, 0, []
        self.ident = self.sbuf("ident", [P, P])
        self.identb = self.sbuf("identb", [P, P], BF16)
        self.causal = self.sbuf("causal", [P, P], BF16)
        self.neg_lam = self.sbuf("neg_lam", [P, 1])

    def sbuf(self, name, shape, dt=F32):
        return self.ctx.enter_context(self.nc.sbuf_tensor(name, shape, dt))

    def sem(self, name):
        self.sems.append(self.nc.alloc_semaphore(name=name))
        return self.sems[-1]

    def end_stage(self):
        self.nc.clear_and_free_semaphores(self.sems)
        self.nc.all_engine_barrier()
        self.sems = []

    def tag(self):
        self.turns += 1
        return str(self.turns)


def keep(nc, g, name, pairs):
    stored = g.sem("kept_" + name)
    with nc.Block() as block:

        @block.sync
        def _(sp):
            for src, dst in pairs:
                sp.dma_start(dst, src).then_inc(stored, 16)
            sp.wait_ge(stored, 16 * len(pairs))


def two_layers(nc, x, xT, Wq, Wk, Wv, Wo, lq1, lk1, lq2, lk2, first, gate, up, down, lora_b, scan_first, chan_table,
               dt_bias, A_log, Wg, WoT, norm_table, w_gate, w_up, w_down, scales, s_down, out):
    def dram(name, shape, dt=F32):
        return nc.dram_tensor(name, shape, dt, kind="Internal").ap()

    by_row = lambda a: a.rearrange("(k p) n -> p k n", p=P)
    with ExitStack() as ctx:
        g = Shared(nc, ctx)
        QD, KD = dram("q_parts", [2, E, T]), dram("k_parts", [2, E, T])
        x2 = dram("x2", [T, E])
        D = dict(small=dram("scan_small", [P, GROUPS * HALVES * KINDS * HC * GH]), sums=dram("scan_sums", [3, NH, T], BF16),
                 B=dram("scan_B", [P, TT, NS]), C=dram("scan_C", [P, T]), CB=dram("scan_CB", [P, TT, P]),
                 state=dram("scan_state", [GROUPS, P, GC]), xT=[dram("x2_high", [P, EK, T]), dram("x2_low", [P, EK, T])])
        x3_parts = [dram("x3_high", [P, EK, T]), dram("x3_low", [P, EK, T])]
        acc_dram, ssq_dram = dram("scan_acc", [P, TT, E]), dram("scan_ssq", [P, T])
        mv = g.sbuf("row_stats", [P, TT, 2])
        hist = g.sbuf("conv_history", [P, 2 * GROUPS + 2, TAPS - 1])
        constants(nc, g)

        def split(c, name, src, rows, cols, raw):
            hi, lo = parts(nc, c, name, [P, rows, cols])
            slot = raw[:, 0:rows * cols].rearrange("p (k n) -> p k n", k=rows)
            return (by_row(src), slot, hi[:, :, :], lo[:, :, :]), (hi, lo)

        with nc.sbuf_tensor("V_then_X", [P, TT, E], F32) as X:
            g.V = X
            with nc.sbuf_tensor("xh", [P, EK, T], F32R) as g.xh, nc.sbuf_tensor("xl", [P, EK, T], F32R) as g.xl:
                qkv(nc, g, xT, Wq, Wk, Wv, QD, KD)
            with nc.sbuf_tensor("A", [P, TT, E], F32) as g.A:
                attention(nc, g, QD, KD, (lq1, lk1, lq2, lk2))
                g.end_stage()
                with ExitStack() as c:
                    ah, al = parts(nc, c, "aT", [P, EK, T])
                    raw = c.enter_context(nc.sbuf_tensor("wo_raw", [P, EK * E], F32))
                    item, wo = split(c, "wo", Wo, EK, E, raw)
                    split_weights(nc, g, "o", [item])
                    rms_norm(nc, g, g.A)
                    turn(nc, g, g.A, ah, al)
                    project_out(nc, g, x, X, ah, al, wo[0], wo[1], mv)
            with ExitStack() as c:
                xh, xl = parts(nc, c, "xT", [P, EK, T])
                turn(nc, g, X, xh, xl, mv)
                with ExitStack() as c2:
                    raw = [c2.enter_context(nc.sbuf_tensor(f"moe_raw{b}", [P, EK * E], F32)) for b in range(2)]
                    items, W = [], {}
                    for n, (name, src, rows, cols) in enumerate((("first", first, EK, EX * RANK + EX), ("gate", gate, EK, E), ("up", up, EK, E),
                                                                 ("down", down, FK, E), ("lora_b", lora_b, 1, E))):
                        item, W[name] = split(c2, name, src, rows, cols, raw[n % 2])
                        items.append(item)
                    W["loraB"] = tuple(w[:, 0, :] for w in W["lora_b"])
                    split_weights(nc, g, "moe", items)
                    moe(nc, g, X, xh, xl, W, mv)
                turn(nc, g, X, xh, xl, mv)
                keep(nc, g, "x2", [(X[:, :, :], by_row(x2)), (xh[:, :, :].bitcast(F32), D["xT"][0]), (xl[:, :, :].bitcast(F32), D["xT"][1])])
                g.end_stage()
                with ExitStack() as c2:
                    raw = c2.enter_context(nc.sbuf_tensor("scan_raw", [P, EK * 2 * NS + EK * NH], F32))
                    item, W = split(c2, "scan_first", scan_first, EK, 2 * NS + NH, raw)
                    chan = c2.enter_context(nc.sbuf_tensor("chan", [P, 2 * GROUPS + 2, TAPS + 1], F32))
                    split_weights(nc, g, "scan", [item])
                    chan_in, hist_zero = g.sem("chan_in"), g.sem("hist_zero")
                    with nc.Block() as block:

                        @block.sync
                        def _(sp):
                            sp.dma_start(chan[:, :, :], chan_table).then_inc(chan_in, 16)
                            sp.wait_ge(chan_in, 16)

                        @block.vector
                        def _(dve):
                            dve.memset(hist[:, :, :], 0.0).then_inc(hist_zero, 1)
                    scan_inputs(nc, g, xh, xl, W, chan, dt_bias, A_log, D)
        g.end_stage()
        S = scan_semaphores(g)
        for half in range(HALVES):
            scan_half(nc, g, half, S, D, Wg, WoT, (chan_table, norm_table), hist, ssq_dram, acc_dram)
        g.end_stage()
        with nc.sbuf_tensor("X_1", [P, TT, E], F32) as X:
            scan_end(nc, g, X, x2, acc_dram, ssq_dram, mv)
            with ExitStack() as c:
                xh, xl = parts(nc, c, "x3T", [P, EK, T])
                turn(nc, g, X, xh, xl, mv)
                keep(nc, g, "x3", [(xh[:, :, :].bitcast(F32), x3_parts[0]), (xl[:, :, :].bitcast(F32), x3_parts[1])])
            with nc.sbuf_tensor("out_stats", [P, TT, 6], F32) as st_all:
                ffn(nc, g, X, x3_parts, w_gate, w_up, w_down, scales, s_down, st_all)
                norm_out(nc, g, X, st_all, out)


def kernel(**inputs):
    import numpy as np
    import concourse.bacc as bacc
    from concourse.bass_utils import run_bass_kernel_spmd

    c = np.ascontiguousarray
    i = {n: np.asarray(a) for n, a in inputs.items()}
    x = c(i["L0_attn_x"].reshape(T, E))
    wide = lambda w: c(w.reshape(-1, E).T)
    deep = lambda w: c(w.transpose(0, 2, 1).reshape(-1, E))
    w_in = i["L1_attn_W_in"].T
    grouped = lambda w: w.reshape(E, GROUPS, GC)
    by_channel = lambda a: c(a.reshape(-1, P, a.shape[1]).transpose(1, 0, 2))
    words = lambda a: c(a).view(np.int32)
    args = dict(
        x=x, xT=c(x.T), Wq=i["L0_attn_Wq"], Wk=i["L0_attn_Wk"], Wv=i["L0_attn_Wv"], Wo=i["L0_attn_Wo"],
        lq1=i["L0_attn_lq1"], lk1=i["L0_attn_lk1"], lq2=i["L0_attn_lq2"], lk2=i["L0_attn_lk2"],
        first=c(np.concatenate([i["L0_ffn_lora_A"].reshape(-1, E).T, i["L0_ffn_G"]], 1)),
        gate=wide(i["L0_ffn_gate_w"]), up=wide(i["L0_ffn_up_w"]), down=deep(i["L0_ffn_down_w"]), lora_b=deep(i["L0_ffn_lora_B"]),
        scan_first=c(w_in[:, 2 * DI:]),
        chan_table=by_channel(np.concatenate([i["L1_attn_conv_w"][:, 0, :], i["L1_attn_conv_b"][:, None]], 1)),
        dt_bias=i["L1_attn_dt_bias"], A_log=i["L1_attn_A_log"],
        Wg=c(np.concatenate([grouped(w_in[:, DI:2 * DI]), grouped(w_in[:, :DI])], 2).transpose(1, 0, 2)),
        WoT=c(i["L1_attn_W_out"].T),
        norm_table=by_channel(np.stack([np.repeat(i["L1_attn_D_param"], HP), i["L1_attn_norm_w"]], 1)),
        w_gate=words(i["L1_ffn_w_gate"]), w_up=words(i["L1_ffn_w_up"]), w_down=words(i["L1_ffn_w_down"]),
        scales=c(np.stack([i["L1_ffn_s_gate"].reshape(FT, P).T, i["L1_ffn_s_up"].reshape(FT, P).T], 1)),
        s_down=i["L1_ffn_s_down"])
    nc = bacc.Bacc("TRN2", target_bir_lowering=False, num_devices=1)
    arrays, aps = {}, []
    for name, a in args.items():
        arrays[f"in_{name}"] = c(a)
        aps.append(nc.dram_tensor(f"in_{name}", a.shape, mybir.dt.from_np(a.dtype), kind="ExternalInput").ap())
    aps.append(nc.dram_tensor("out", (T, E), F32, kind="ExternalOutput").ap())
    two_layers(nc, *aps)
    r = run_bass_kernel_spmd(nc, [arrays], core_ids=[0])
    return r.results[0]["out"].reshape(1, T, E)
```

```python
import math
from contextlib import ExitStack

import concourse.bass as bass
from concourse import mybir

F32 = mybir.dt.float32
F32R = mybir.dt.float32r
BF16 = mybir.dt.bfloat16
ALU = mybir.AluOpType
ACT = mybir.ActivationFunctionType
AX = mybir.AxisListType
ds = bass.ds

P = 128
T = 2048
E = 512
TT = T // P
EK = E // P
CHUNK = 512
NCH = T // CHUNK
LN_EPS = 1e-5
NEG = -3.0e38

HD = 16
PAIRS = 16
VD = 2 * HD
LAMBDA_INIT = 0.8 - 0.6 * math.exp(-0.3 * 12)


def constants(nc, g):
    made = g.sem("constants_made")
    with nc.Block() as block:

        @block.gpsimd
        def _(pool):
            pool.memset(g.ident[:, :], 0.0).then_inc(made, 1)
            pool.memset(g.identb[:, :], 0.0).then_inc(made, 1)
            pool.memset(g.causal[:, :], 0.0).then_inc(made, 1)
            pool.memset(g.causalT[:, :], 0.0).then_inc(made, 1)
            pool.wait_ge(made, 4)
            for m in (g.ident, g.identb):
                pool.affine_select(out=m[:, :], in_=m[:, :], compare_op=ALU.not_equal, fill=1.0, base=0,
                                   pattern=[[-1, P]], channel_multiplier=1).then_inc(made, 1)
            pool.affine_select(out=g.causal[:, :], in_=g.causal[:, :], compare_op=ALU.is_ge, fill=NEG, base=0,
                               pattern=[[-1, P]], channel_multiplier=1).then_inc(made, 1)
            pool.affine_select(out=g.causalT[:, :], in_=g.causalT[:, :], compare_op=ALU.is_ge, fill=NEG, base=0,
                               pattern=[[1, P]], channel_multiplier=-1).then_inc(made, 1)
            pool.wait_ge(made, 8)


def product3(pe, out, lhs, rhs, start=True, stop=True):
    (lh, ll), (rh, rl) = lhs, rhs
    pe.matmul(out, ll, rh, start=start, stop=False)
    pe.matmul(out, lh, rl, start=False, stop=False)
    return pe.matmul(out, lh, rh, start=False, stop=stop)


def qkv(nc, g, xT, Wq, Wk, Wv, QD, KD):
    with ExitStack() as ctx:
        sb = lambda name, shape, dt=F32: ctx.enter_context(nc.sbuf_tensor(name, shape, dt))
        wraw = [sb(f"wraw_{w}", [P, EK, E]) for w in "qkv"]
        wh = [sb(f"wh_{w}", [P, EK, E], F32R) for w in "qkv"]
        wl = [sb(f"wl_{w}", [P, EK, E], F32R) for w in "qkv"]
        xraw = sb("xraw", [P, 2, EK, CHUNK])
        NS = 4
        sh = sb("qk_high", [P, NS, CHUNK], F32R)
        sl = sb("qk_low", [P, NS, CHUNK], F32R)
        ps = [ctx.enter_context(nc.psum_tensor(f"qkv_ps{i}", [P, CHUNK], F32)) for i in range(8)]
        w_in = [g.sem(f"w_in_{w}") for w in "qkv"]
        x_in = [g.sem("x_in0"), g.sem("x_in1")]
        w_high, w_low = g.sem("w_high"), g.sem("w_low")
        x_high, x_low = g.sem("x_high"), g.sem("x_low")
        prod, high, low = g.sem("qk_prod"), g.sem("qk_high"), g.sem("qk_low")
        out = [g.sem(f"qk_out{i}") for i in range(NS)]
        v_prod, v_done = g.sem("v_prod"), g.sem("v_done")
        outs = [(w, m, c) for c in range(NCH) for w in range(2) for m in range(EK)]
        with nc.Block() as block:

            @block.sync
            def _(sp):
                def load_x(c):
                    src = xT[:, c * CHUNK:(c + 1) * CHUNK].rearrange("(k p) n -> p k n", p=P)
                    sp.dma_start(xraw[:, c % 2, :, :], src).then_inc(x_in[c % 2], 16)

                for w, W in enumerate((Wq, Wk, Wv)):
                    sp.dma_start(wraw[w][:, :, :], W.rearrange("(k p) n -> p k n", p=P)).then_inc(w_in[w], 16)
                    if w < 2:
                        load_x(w)
                for c in range(2, NCH):
                    sp.wait_ge(x_low, c - 1)
                    load_x(c)
                for n, (w, m, c) in enumerate(outs):
                    sp.wait_ge(low, n + 1)
                    for part, s in enumerate((sh, sl)):
                        sp.dma_start((QD, KD)[w][part, m * P:(m + 1) * P, c * CHUNK:(c + 1) * CHUNK],
                                     s[:, n % NS, :].bitcast(F32)).then_inc(out[n % NS], 16)
                for i in range(NS):
                    sp.wait_ge(out[i], 32 * (len(outs) // NS))

            @block.scalar
            def _(act):
                def x_part(c):
                    act.wait_ge(x_in[c % 2], 16 * (c // 2 + 1))
                    act.activation(g.xh[:, :, c * CHUNK:(c + 1) * CHUNK], xraw[:, c % 2, :, :], ACT.Copy).then_inc(x_high, 1)

                for w in range(3):
                    act.wait_ge(w_in[w], 16)
                    act.activation(wh[w][:, :, :], wraw[w][:, :, :], ACT.Copy).then_inc(w_high, 1)
                    if w < 2:
                        x_part(w)
                for n, (w, m, c) in enumerate(outs):
                    if n in (4, 8):
                        x_part(n // 4 + 1)
                    act.wait_ge(prod, n + 1)
                    if n >= NS:
                        act.wait_ge(out[n % NS], 32 * (n // NS))
                    act.activation(sh[:, n % NS, :], ps[n % 8][:, :], ACT.Copy,
                                   scale=(HD ** -0.5, 1.0)[w]).then_inc(high, 1)
                for i in range(TT):
                    act.wait_ge(v_prod, i + 1)
                    act.activation(g.V[:, i, :], ps[i % 8][:, :], ACT.Copy).then_inc(v_done, 1)

            @block.vector
            def _(dve):
                def x_rest(c):
                    at = slice(c * CHUNK, (c + 1) * CHUNK)
                    dve.wait_ge(x_high, c + 1)
                    dve.tensor_tensor(g.xl[:, :, at], xraw[:, c % 2, :, :], g.xh[:, :, at].bitcast(F32),
                                      ALU.subtract).then_inc(x_low, 1)

                for w in range(3):
                    dve.wait_ge(w_high, w + 1)
                    dve.tensor_tensor(wl[w][:, :, :], wraw[w][:, :, :], wh[w][:, :, :].bitcast(F32),
                                      ALU.subtract).then_inc(w_low, 1)
                    if w < 2:
                        x_rest(w)
                for n, (w, m, c) in enumerate(outs):
                    if n in (4, 8):
                        x_rest(n // 4 + 1)
                    dve.wait_ge(high, n + 1)
                    dve.scalar_tensor_tensor(out=sl[:, n % NS, :], in0=ps[n % 8][:, :], scalar=(HD ** -0.5, 1.0)[w],
                                             in1=sh[:, n % NS, :].bitcast(F32), op0=ALU.mult,
                                             op1=ALU.subtract).then_inc(low, 1)

            @block.tensor
            def _(pe):
                for n, (w, m, c) in enumerate(outs):
                    pe.wait_ge(w_low, w + 1)
                    pe.wait_ge(x_low, c + 1)
                    if n >= 8:
                        pe.wait_ge(low, n - 7)
                    for k in range(EK):
                        mm = product3(pe, ps[n % 8][:, :],
                                      (wh[w][:, k, m * P:(m + 1) * P], wl[w][:, k, m * P:(m + 1) * P]),
                                      (g.xh[:, k, c * CHUNK:(c + 1) * CHUNK], g.xl[:, k, c * CHUNK:(c + 1) * CHUNK]),
                                      start=(k == 0), stop=(k == EK - 1))
                    mm.then_inc(prod, 1)
                pe.wait_ge(w_low, 3)
                for i in range(TT):
                    if i < 8:
                        pe.wait_ge(low, len(outs) - 7 + i)
                    else:
                        pe.wait_ge(v_done, i - 7)
                    for k in range(EK):
                        mm = product3(pe, ps[i % 8][:, :],
                                      (g.xh[:, k, i * P:(i + 1) * P], g.xl[:, k, i * P:(i + 1) * P]),
                                      (wh[2][:, k, :], wl[2][:, k, :]), start=(k == 0), stop=(k == EK - 1))
                    mm.then_inc(v_prod, 1)


def attention(nc, g, QD, KD, lams):
    ITER = PAIRS // 2
    PARTS = 3 * HD
    FULL = PARTS + 2
    OUT = 64 + VD + 1
    units = [(c, j) for c in range(NCH) for j in range(4 * c + 4)]
    chunks = [(i, s, c) for i in range(TT) for s in range(2) for c in range(i // 4 + 1)]
    NU, NC = len(units), len(chunks)
    ends = [units.index((c, 4 * c + 3)) for c in range(NCH)]
    AHEAD, PER = 8, 3
    M_AT = NU - 3

    def width(u):
        c, j = units[u]
        return CHUNK - P * max(j - 4 * c, 0)

    def chunk_range(u):
        first = min(max(u - AHEAD, 0) * PER, NC)
        return range(first, min(first + PER, NC) if u >= AHEAD else first)

    assert chunk_range(M_AT - 2).stop == NC
    with ExitStack() as ctx:
        sb = lambda name, shape, dt=F32: ctx.enter_context(nc.sbuf_tensor(name, shape, dt))
        QS = [sb(f"QS{b}", [P, T], F32R) for b in range(2)]
        KS = [sb(f"KS{b}", [P, T], F32R) for b in range(2)]
        VS = [sb(f"VS{b}", [P, TT, 2, OUT]) for b in range(2)]
        PT = [sb(f"probs{b}", [P, 2, CHUNK]) for b in range(3)]
        OT = [sb(f"outT{b}", [P, CHUNK]) for b in range(2)]
        part = sb("part_max", [P, TT, 2, NCH])
        nm = sb("neg_max", [P, 2, TT])
        mp = sb("neg_max_parts", [P, P], F32R)
        mT = sb("neg_max_turned", [P, P], F32R)
        rL = sb("inv_sums", [P, 4, 2])
        r2 = sb("weight2", [P, 4])
        o1, o2 = sb("out1", [P, 4, VD]), sb("out2", [P, 4, VD])
        lv = sb("lambda_vecs", [P, 4, HD])
        lp = sb("lambda_products", [P, 2, HD])
        le = sb("lambda_sums", [P, 4])
        pa = [ctx.enter_context(nc.psum_tensor(f"max_scores{i}", [P, CHUNK], F32)) for i in range(2)]
        pb = [ctx.enter_context(nc.psum_tensor(f"prob_scores{i}", [P, 2, CHUNK], F32)) for i in range(2)]
        po = ctx.enter_context(nc.psum_tensor("times_v", [P, CHUNK], F32))
        tp = ctx.enter_context(nc.psum_tensor("turned_out", [P, 4, P], F32))
        setup, lam_in, lam, lam_sum, lam_exp = (g.sem("at_" + n) for n in ("setup", "lam_in", "lam", "lam_sum", "lam_exp"))
        loaded, max_in = [[g.sem(f"{n}{b}") for b in range(2)] for n in ("at_loaded", "at_max_in")]
        max_scored, max_part, max_all = g.sem("max_scored"), g.sem("max_part"), g.sem("max_all")
        max_high, max_low, max_turned, max_copied = (g.sem("max_" + n) for n in ("high", "low", "turned", "copied"))
        scored, exped, v_staged, pv = g.sem("scored"), g.sem("exped"), g.sem("v_staged"), g.sem("pv")
        out_copied, out_turned, out_inv, out_weight = (g.sem("out_" + n) for n in ("copied", "turned", "inv", "weight"))
        out_weighed, out_read, out_done = g.sem("out_weighed"), g.sem("out_read"), g.sem("out_done")

        def load(sp, b, pair):
            for s in range(2):
                for r in range(3):
                    at = 64 * s + HD * r
                    for dst, src, which in ((QS, QD, r // 2), (KS, KD, r % 2)):
                        sp.dma_start(dst[b][at:at + HD, :].bitcast(F32), src[which, ds(pair * VD + s * HD, HD), :]).then_inc(loaded[b], 16)

        def max_rows(sp, b, n):
            sp.wait_ge(max_copied, n)
            for k in range(2):
                for s in range(2):
                    at = (2 * k + s) * TT
                    sp.dma_start(QS[b][64 * s + PARTS + k:64 * s + PARTS + k + 1, :].bitcast(F32),
                                 mT[at:at + TT, :].bitcast(F32)).then_inc(max_in[b], 16)

        with nc.Block() as block:

            @block.gpsimd
            def _(pool):
                for b in range(2):
                    pool.memset(KS[b][:, :].bitcast(F32), 1.0).then_inc(setup, 1)
                for b in range(2):
                    pool.memset(VS[b][:, :, :, :], 0.0).then_inc(setup, 1)
                pool.memset(mp[:, :].bitcast(F32), 0.0).then_inc(setup, 1)
                pool.memset(part[:, :, :, :], NEG).then_inc(setup, 1)
                pool.wait_ge(setup, 6)
                for b in range(2):
                    for s in range(2):
                        pool.memset(VS[b][:, :, s, 64 * s + VD], 1.0).then_inc(setup, 1)

            @block.sync
            def _(sp):
                for n, v in enumerate(lams):
                    sp.dma_start(lv[:, n, :], v.partition_broadcast(P)).then_inc(lam_in, 16)
                sp.wait_ge(setup, 2)
                load(sp, 0, 0)
                max_rows(sp, 0, 1)

                def stage(it, b, last):
                    sp.wait_ge(scored, it * 2 * NU + b * NU)
                    load(sp, 1 - b, 2 * it + b if last and b else 2 * it + b + 1)
                    max_rows(sp, 1 - b, 2 * it + b + 2)

                with sp.Fori(0, ITER - 1) as it:
                    for b in range(2):
                        stage(it, b, False)
                for b in range(2):
                    stage(ITER - 1, b, True)
                sp.wait_ge(loaded[0], (ITER + 1) * 16 * 12)
                sp.wait_ge(max_in[0], (ITER + 1) * 64)

            @block.tensor
            def _(pe):
                def max_scores(b, base, n):
                    i, s, c = chunks[n]
                    w = min(CHUNK, (i + 1) * P - c * CHUNK)
                    pe.wait_ge(max_part, base + max(n - 1, 0))
                    rows = slice(64 * s, 64 * s + PARTS)
                    mm = pe.matmul(pa[n % 2][:, 0:w], QS[b][rows, i * P:(i + 1) * P], KS[b][rows, c * CHUNK:c * CHUNK + w],
                                   start=True, stop=True)
                    if c == i // 4:
                        mm = pe.matmul(pa[n % 2][:, w - P:w], g.identb[:, :], g.causal[:, :], start=False, stop=True,
                                       skip_group_check=True)
                    mm.then_inc(max_scored, 1)

                def turn_maxima(n):
                    pe.wait_ge(max_low, n)
                    pe.transpose(tp[:, 0, :], mp[:, :].bitcast(F32), g.ident[:, :]).then_inc(max_turned, 1)

                def scores(p, b, u):
                    c, j = units[u]
                    w = width(u)
                    pe.wait_ge(exped, p * NU + max(u - 1, 0))
                    for s in range(2):
                        rows = slice(64 * s, 64 * s + FULL)
                        mm = pe.matmul(pb[u % 2][:, s, 0:w], KS[b][rows, j * P:(j + 1) * P],
                                       QS[b][rows, (c + 1) * CHUNK - w:(c + 1) * CHUNK], start=True, stop=True)
                        if j >= 4 * c:
                            mm = pe.matmul(pb[u % 2][:, s, 0:P], g.identb[:, :], g.causalT[:, :], start=False, stop=True,
                                           skip_group_check=True)
                    mm.then_inc(scored, 1)

                def times_v(p, b, u, chunk=None):
                    c, j = units[u]
                    w = width(u)
                    pe.wait_ge(exped, p * NU + u + 1)
                    if u == 0:
                        pe.wait_ge(v_staged, (p + 1) * 2)
                    if j == 0:
                        pe.wait_ge(out_copied, p * NCH + c)
                    for s in range(2):
                        mm = pe.matmul(po[0:OUT, CHUNK - w:CHUNK], VS[b][:, j, s, :], PT[u % 3][:, s, 0:w],
                                       start=(j == 0 and s == 0), stop=(j == 4 * c + 3 and s == 1))
                        if s == 0 and chunk is not None:
                            max_scores(1 - b, (p + 1) * NC, chunk)
                    mm.then_inc(pv, 1)

                def turn_out(p, c):
                    pe.wait_ge(out_copied, p * NCH + c + 1)
                    pe.wait_ge(out_read, p * NCH + c)
                    if c == 0 or c == NCH - 1:
                        pe.wait_ge(max_copied, p + 1 + (c == NCH - 1))
                    for k in range(4):
                        mm = pe.transpose(tp[:, k, 0:OUT], OT[c % 2][0:OUT, k * P:(k + 1) * P], g.ident[0:OUT, 0:OUT])
                    mm.then_inc(out_turned, 1)

                pe.wait_ge(setup, 10)
                pe.wait_ge(loaded[0], 16 * 12)
                for n in range(NC):
                    max_scores(0, 0, n)
                turn_maxima(1)
                with pe.Fori(0, ITER) as it:
                    for b in range(2):
                        p = it * 2 + b
                        pe.wait_ge(max_in[b], (it + 1) * 64)
                        for u in range(NU):
                            scores(p, b, u)
                            if u == AHEAD:
                                pe.wait_ge(loaded[1 - b], (it + 1 + b) * 16 * 12)
                            mine = list(chunk_range(u)) + [None] * PER
                            if mine[0] is not None:
                                max_scores(1 - b, (p + 1) * NC, mine[0])
                            if u >= 1:
                                times_v(p, b, u - 1, mine[1])
                            if mine[2] is not None:
                                max_scores(1 - b, (p + 1) * NC, mine[2])
                            if u - 3 in ends:
                                turn_out(p, ends.index(u - 3))
                            if u == M_AT:
                                pe.wait_ge(out_read, p * NCH + NCH - 1)
                                turn_maxima(p + 2)
                        times_v(p, b, NU - 1)
                        turn_out(p, NCH - 1)

            @block.scalar
            def _(act):
                act.wait_ge(lam_sum, 2)
                act.activation(le[:, 2:4], le[:, 0:2], ACT.Exp).then_inc(lam_exp, 1)
                with act.Fori(0, ITER) as it:
                    for b in range(2):
                        p = it * 2 + b

                        def copy_out(c):
                            act.wait_ge(pv, p * NU + ends[c] + 1)
                            act.wait_ge(out_turned, p * NCH + c - 1 if c or b else it * 2 * NCH)
                            act.activation(OT[c % 2][0:OUT, :], po[0:OUT, :], ACT.Copy).then_inc(out_copied, 1)

                        for u in range(NU):
                            w = width(u)
                            act.wait_ge(scored, p * NU + u + 1)
                            act.wait_ge(pv, p * NU + max(u - 2, 0))
                            act.activation(PT[u % 3][:, :, 0:w], pb[u % 2][:, :, 0:w], ACT.Exp).then_inc(exped, 1)
                            if u - 1 in ends:
                                copy_out(ends.index(u - 1))
                        copy_out(NCH - 1)

            @block.vector
            def _(dve):
                def maxima(base, ns):
                    for n in ns:
                        i, s, c = chunks[n]
                        w = min(CHUNK, (i + 1) * P - c * CHUNK)
                        dve.wait_ge(max_scored, base + n + 1)
                        dve.tensor_reduce(part[:, i, s, c:c + 1], pa[n % 2][:, 0:w], AX.X, ALU.max).then_inc(max_part, 1)

                def split_maxima(n):
                    dve.wait_ge(max_part, n * NC)
                    dve.tensor_reduce(nm[:, :, :].rearrange("p s i -> p i s"), part[:, :, :, :], AX.X, ALU.max,
                                      negate=True).then_inc(max_all, 1)
                    dve.wait_ge(max_all, n)
                    flat = nm[:, :, :].rearrange("p s i -> p (s i)")
                    dve.wait_ge(max_turned, n - 1)
                    dve.tensor_copy(mp[:, 0:2 * TT], flat).then_inc(max_high, 1)
                    dve.wait_ge(max_high, n)
                    dve.tensor_tensor(mp[:, 2 * TT:4 * TT], flat, mp[:, 0:2 * TT].bitcast(F32), ALU.subtract).then_inc(max_low, 1)

                def copy_maxima(n):
                    dve.wait_ge(max_turned, n)
                    dve.tensor_copy(mT[:, :], tp[:, 0, :]).then_inc(max_copied, 1)

                def combine(p, c):
                    n = p * NCH + c
                    dve.wait_ge(out_turned, n + 1)
                    sums = tp[:, :, :].rearrange("p k (s n) -> p k s n", s=2)[:, :, :, VD]
                    dve.reciprocal(rL[:, :, :], sums).then_inc(out_inv, 1)
                    dve.wait_ge(out_inv, n + 1)
                    dve.tensor_scalar(r2[:, :], rL[:, :, 1], g.neg_lam[:, :], None, ALU.mult).then_inc(out_weight, 1)
                    dve.tensor_tensor(o1[:, :, :], tp[:, :, 0:VD], rL[:, :, 0].unsqueeze(2).to_broadcast([P, 4, VD]),
                                      ALU.mult).then_inc(out_weighed, 1)
                    dve.wait_ge(out_weight, n + 1)
                    dve.tensor_tensor(o2[:, :, :], tp[:, :, 64:64 + VD], r2[:, :].unsqueeze(2).to_broadcast([P, 4, VD]),
                                      ALU.mult).then_inc(out_read, 1)
                    dve.wait_ge(out_weighed, n + 1)
                    dve.wait_ge(out_read, n + 1)
                    dve.tensor_tensor(g.A[:, 4 * c:4 * c + 4, ds(p * VD, VD)], o1[:, :, :], o2[:, :, :], ALU.add).then_inc(out_done, 1)

                dve.wait_ge(lam_in, 64)
                for n in range(2):
                    dve.tensor_tensor(lp[:, n, :], lv[:, 2 * n, :], lv[:, 2 * n + 1, :], ALU.mult).then_inc(lam, 1)
                dve.wait_ge(lam, 2)
                for n in range(2):
                    dve.tensor_reduce(le[:, n:n + 1], lp[:, n, :], AX.X, ALU.add).then_inc(lam_sum, 1)
                dve.wait_ge(lam_exp, 1)
                dve.tensor_tensor(le[:, 0:1], le[:, 3:4], le[:, 2:3], ALU.subtract).then_inc(lam, 1)
                dve.wait_ge(lam, 3)
                dve.tensor_scalar(g.neg_lam[:, :], le[:, 0:1], -LAMBDA_INIT, None, ALU.add).then_inc(lam, 1)
                dve.wait_ge(lam, 4)
                dve.wait_ge(setup, 10)
                maxima(0, range(NC))
                split_maxima(1)
                copy_maxima(1)
                with dve.Fori(0, ITER) as it:
                    for b in range(2):
                        p = it * 2 + b
                        for s in range(2):
                            dve.tensor_copy(VS[b][:, :, s, 64 * s:64 * s + VD], g.V[:, :, ds(p * VD, VD)]).then_inc(v_staged, 1)
                        for u in range(NU):
                            maxima((p + 1) * NC, chunk_range(u))
                            if u - 4 in ends:
                                combine(p, ends.index(u - 4))
                            if u == M_AT - 1:
                                split_maxima(p + 2)
                            if u == M_AT:
                                dve.wait_ge(max_in[b], (it + 1) * 64)
                                copy_maxima(p + 2)
                        combine(p, NCH - 1)


LOADB = 4


class Weights:

    def __init__(self, g, what, items):
        self.items = items
        self.w_in = [g.sem(f"sw_{what}_in{b}") for b in range(2)]
        self.w_high, self.w_low = g.sem(f"sw_{what}_high"), g.sem(f"sw_{what}_low")

    def load_all(self, sp):
        for n, (src, raw, hi, lo) in enumerate(self.items):
            if n >= 2:
                sp.wait_ge(self.w_low, n - 1)
            sp.dma_start(raw, src).then_inc(self.w_in[n % 2], 16)

    def high(self, act, n):
        src, raw, hi, lo = self.items[n]
        act.wait_ge(self.w_in[n % 2], 16 * (n // 2 + 1))
        act.activation(hi, raw, ACT.Copy).then_inc(self.w_high, 1)

    def low(self, dve, n):
        src, raw, hi, lo = self.items[n]
        dve.wait_ge(self.w_high, n + 1)
        dve.tensor_tensor(lo, raw, hi.bitcast(F32), ALU.subtract).then_inc(self.w_low, 1)


def rms_norm(nc, g, A):
    with ExitStack() as ctx:
        sb = lambda name, shape, dt=F32: ctx.enter_context(nc.sbuf_tensor(name, shape, dt))
        sq = sb("rn_sq", [P, 2, E])
        ms = sb("rn_ms", [P, TT, PAIRS])
        squared, summed = g.sem("rn_squared"), g.sem("rn_summed")
        biased, rooted, inverted, scaled = g.sem("rn_biased"), g.sem("rn_rooted"), g.sem("rn_inv"), g.sem("rn_scaled")
        with nc.Block() as block:

            @block.scalar
            def _(act):
                for i in range(TT):
                    if i >= 2:
                        act.wait_ge(summed, i - 1)
                    act.activation(sq[:, i % 2, :], A[:, i, :], ACT.Square).then_inc(squared, 1)
                act.wait_ge(biased, 1)
                act.activation(ms[:, :, :], ms[:, :, :], ACT.Sqrt).then_inc(rooted, 1)

            @block.vector
            def _(dve):
                for i in range(TT):
                    dve.wait_ge(squared, i + 1)
                    dve.tensor_reduce(ms[:, i, :], sq[:, i % 2, :].rearrange("p (h d) -> p h d", d=VD), AX.X,
                                      ALU.add).then_inc(summed, 1)
                dve.wait_ge(summed, TT)
                c = 1.0 - LAMBDA_INIT
                dve.tensor_scalar(ms[:, :, :], ms[:, :, :], 1.0 / VD / c / c, LN_EPS / c / c, ALU.mult, ALU.add).then_inc(biased, 1)
                dve.wait_ge(rooted, 1)
                dve.reciprocal(ms[:, :, :], ms[:, :, :]).then_inc(inverted, 1)
                dve.wait_ge(inverted, 1)
                for i in range(TT):
                    a = A[:, i, :].rearrange("p (h d) -> p h d", d=VD)
                    dve.tensor_tensor(a, a, ms[:, i, :].unsqueeze(2).to_broadcast([P, PAIRS, VD]), ALU.mult).then_inc(scaled, 1)


def turn(nc, g, X, xh, xl, mv=None, weights=None):
    tag = g.tag()
    split_after = {} if weights is None else {3 * n + 2: n for n in range(len(weights.items))}
    with ExitStack() as ctx:
        rstd = ctx.enter_context(nc.sbuf_tensor(f"rstd{tag}", [P, TT], F32))
        tp = [ctx.enter_context(nc.psum_tensor(f"turn{tag}_{b}", [P, EK, P], F32)) for b in range(LOADB)]
        eps, root, inv, normed = (g.sem(f"{n}{tag}") for n in ("ln_eps", "ln_root", "ln_inv", "ln_normed"))
        turned, high, low = (g.sem(f"{n}{tag}") for n in ("turned", "turn_high", "turn_low"))
        with nc.Block() as block:

            @block.sync
            def _(sp):
                if weights is not None:
                    weights.load_all(sp)

            @block.scalar
            def _(act):
                if mv is not None:
                    act.wait_ge(eps, 1)
                    act.activation(rstd[:, :], rstd[:, :], ACT.Sqrt).then_inc(root, 1)
                for i in range(TT):
                    act.wait_ge(turned, i + 1)
                    act.activation(xh[:, :, i * P:(i + 1) * P], tp[i % LOADB][:, :, :], ACT.Copy).then_inc(high, 1)
                    if i in split_after:
                        weights.high(act, split_after[i])

            @block.vector
            def _(dve):
                if mv is not None:
                    dve.tensor_scalar(rstd[:, :], mv[:, :, 1], LN_EPS, None, ALU.add).then_inc(eps, 1)
                    dve.wait_ge(root, 1)
                    dve.reciprocal(rstd[:, :], rstd[:, :]).then_inc(inv, 1)
                    dve.wait_ge(inv, 1)
                ahead = 4 if mv is not None else 0
                for i in range(TT + ahead):
                    if mv is not None and i < TT:
                        dve.tensor_scalar(X[:, i, :], X[:, i, :], mv[:, i, 0:1], rstd[:, i:i + 1], ALU.subtract,
                                          ALU.mult).then_inc(normed, 1)
                    if i >= ahead:
                        n = i - ahead
                        dve.wait_ge(high, n + 1)
                        dve.tensor_tensor(xl[:, :, n * P:(n + 1) * P], tp[n % LOADB][:, :, :],
                                          xh[:, :, n * P:(n + 1) * P].bitcast(F32), ALU.subtract).then_inc(low, 1)
                        if n in split_after:
                            weights.low(dve, split_after[n])

            @block.tensor
            def _(pe):
                for i in range(TT):
                    if mv is not None:
                        pe.wait_ge(normed, i + 1)
                    if i >= LOADB:
                        pe.wait_ge(low, i - LOADB + 1)
                    for k in range(EK):
                        mm = pe.transpose(tp[i % LOADB][:, k, :], X[:, i, k * P:(k + 1) * P], g.ident[:, :])
                    mm.then_inc(turned, 1)


def project_out(nc, g, x_dram, X, ah, al, wh, wl, mv):
    NB = 4
    with ExitStack() as ctx:
        xin = ctx.enter_context(nc.sbuf_tensor("po_x", [P, NB, E], F32))
        st = ctx.enter_context(nc.sbuf_tensor("po_stats", [P, 2, 6], F32))
        ps = [ctx.enter_context(nc.psum_tensor(f"po_ps{b}", [P, E], F32)) for b in range(NB)]
        x_in = [g.sem(f"po_x{b}") for b in range(NB)]
        done, added, stats, aggr = g.sem("po_done"), g.sem("po_added"), g.sem("po_stats"), g.sem("po_aggr")
        with nc.Block() as block:

            @block.sync
            def _(sp):
                for i in range(TT):
                    if i >= NB:
                        sp.wait_ge(added, i - NB + 1)
                    sp.dma_start(xin[:, i % NB, :], x_dram[i * P:(i + 1) * P, :]).then_inc(x_in[i % NB], 16)

            @block.tensor
            def _(pe):
                for i in range(TT):
                    if i >= NB:
                        pe.wait_ge(added, i - NB + 1)
                    for k in range(EK):
                        mm = product3(pe, ps[i % NB][:, :], (ah[:, k, i * P:(i + 1) * P], al[:, k, i * P:(i + 1) * P]),
                                      (wh[:, k, :], wl[:, k, :]), start=(k == 0), stop=(k == EK - 1))
                    mm.then_inc(done, 1)

            @block.vector
            def _(dve):
                for i in range(TT):
                    dve.wait_ge(done, i + 1)
                    dve.wait_ge(x_in[i % NB], 16 * (i // NB + 1))
                    dve.tensor_tensor(X[:, i, :], ps[i % NB][:, :], xin[:, i % NB, :], ALU.add).then_inc(added, 1)
                    dve.wait_ge(added, i + 1)
                    dve.bn_stats(st[:, i % 2, :], X[:, i, :]).then_inc(stats, 1)
                    dve.wait_ge(stats, i + 1)
                    dve.bn_aggr(mv[:, i, :], st[:, i % 2, :]).then_inc(aggr, 1)


EX = 8
EF = 64
RANK = 16
FK = EX * EF // P


def moe(nc, g, X, xh, xl, W, mv):
    AR = EX * RANK + EX
    with ExitStack() as ctx:
        sb = lambda name, shape, dt=F32: ctx.enter_context(nc.sbuf_tensor(name, shape, dt))
        lr = sb("moe_lr", [P, TT, EX * RANK])
        ex = sb("moe_exp", [P, TT, EX])
        m = sb("moe_max", [P, TT])
        beats = sb("moe_beats", [P, TT, EX, EX])
        ties = sb("moe_ties", [P, TT, EX, EX])
        lower = sb("moe_lower", [P, EX, EX])
        rank = sb("moe_rank", [P, TT, EX])
        w = sb("moe_w", [P, TT, EX])
        with ExitStack() as inner:
            ps = [inner.enter_context(nc.psum_tensor(f"moe_ar{b}", [P, AR], F32)) for b in range(4)]
            made, prod, read_l, read_r = g.sem("moe_made"), g.sem("moe_prod"), g.sem("moe_read_l"), g.sem("moe_read_r")
            step, exped = g.sem("moe_step"), g.sem("moe_exped")
            with nc.Block() as block:

                @block.gpsimd
                def _(pool):
                    pool.memset(lower[:, :, :], 1.0).then_inc(made, 1)
                    pool.wait_ge(made, 1)
                    pool.affine_select(out=lower[:, :, :], in_=lower[:, :, :], compare_op=ALU.is_gt, fill=0.0, base=0,
                                       pattern=[[1, EX], [-1, EX]], channel_multiplier=0).then_inc(made, 1)

                @block.tensor
                def _(pe):
                    for i in range(TT):
                        if i >= 4:
                            pe.wait_ge(read_r, i - 3)
                        for k in range(EK):
                            mm = product3(pe, ps[i % 4][:, :], (xh[:, k, i * P:(i + 1) * P], xl[:, k, i * P:(i + 1) * P]),
                                          (W["first"][0][:, k, :], W["first"][1][:, k, :]), start=(k == 0), stop=(k == EK - 1))
                        mm.then_inc(prod, 1)

                @block.scalar
                def _(act):
                    for i in range(TT):
                        act.wait_ge(prod, i + 1)
                        act.activation(lr[:, i, :], ps[i % 4][:, 0:EX * RANK], ACT.Copy).then_inc(read_l, 1)
                    act.wait_ge(step, 2)
                    act.activation(ex[:, :, :], ex[:, :, :], ACT.Exp).then_inc(exped, 1)

                @block.vector
                def _(dve):
                    for i in range(TT):
                        dve.wait_ge(read_l, i + 1)
                        dve.tensor_copy(ex[:, i, :], ps[i % 4][:, EX * RANK:AR]).then_inc(read_r, 1)
                    dve.wait_ge(read_r, TT)
                    bc = lambda a: a.unsqueeze(2).to_broadcast([P, TT, EX])
                    dve.tensor_reduce(m[:, :], ex[:, :, :], AX.X, ALU.max).then_inc(step, 1)
                    dve.wait_ge(step, 1)
                    dve.tensor_tensor(ex[:, :, :], ex[:, :, :], bc(m[:, :]), ALU.subtract).then_inc(step, 1)
                    dve.wait_ge(exped, 1)
                    dve.tensor_reduce(m[:, :], ex[:, :, :], AX.X, ALU.add).then_inc(step, 1)
                    dve.wait_ge(step, 3)
                    dve.reciprocal(m[:, :], m[:, :]).then_inc(step, 1)
                    dve.wait_ge(step, 4)
                    dve.tensor_tensor(ex[:, :, :], ex[:, :, :], bc(m[:, :]), ALU.mult).then_inc(step, 1)
                    dve.wait_ge(step, 5)
                    dve.wait_ge(made, 2)
                    si = ex[:, :, :].unsqueeze(3).to_broadcast([P, TT, EX, EX])
                    sj = ex[:, :, :].unsqueeze(2).to_broadcast([P, TT, EX, EX])
                    dve.tensor_tensor(beats[:, :, :, :], sj, si, ALU.is_gt).then_inc(step, 1)
                    dve.tensor_tensor(ties[:, :, :, :], sj, si, ALU.is_equal).then_inc(step, 1)
                    dve.wait_ge(step, 7)
                    dve.tensor_tensor(ties[:, :, :, :], ties[:, :, :, :],
                                      lower[:, :, :].unsqueeze(1).to_broadcast([P, TT, EX, EX]), ALU.mult).then_inc(step, 1)
                    dve.wait_ge(step, 8)
                    dve.tensor_tensor(beats[:, :, :, :], beats[:, :, :, :], ties[:, :, :, :], ALU.add).then_inc(step, 1)
                    dve.wait_ge(step, 9)
                    dve.tensor_reduce(rank[:, :, :], beats[:, :, :, :], AX.X, ALU.add).then_inc(step, 1)
                    dve.wait_ge(step, 10)
                    dve.scalar_tensor_tensor(out=w[:, :, :], in0=rank[:, :, :], scalar=1.5, in1=ex[:, :, :],
                                             op0=ALU.is_lt, op1=ALU.mult).then_inc(step, 1)
                    dve.wait_ge(step, 11)

        sg = sb("moe_silu", [P, 2, E])
        gt = sb("moe_gated", [P, 2, E])
        lw = sb("moe_lw", [P, 2, EX * RANK])
        gh, gl = sb("moe_gh", [P, 2, FK, P], F32R), sb("moe_gl", [P, 2, FK, P], F32R)
        lh, ll = sb("moe_lh", [P, 2, P], F32R), sb("moe_ll", [P, 2, P], F32R)
        st = sb("moe_stats", [P, 2, 6])
        pb = lambda n, s: ctx.enter_context(nc.psum_tensor(n, s, F32))
        pg, pu = [pb(f"moe_g{b}", [P, E]) for b in range(2)], [pb(f"moe_u{b}", [P, E]) for b in range(2)]
        pt, pl, pd = pb("moe_t", [P, FK, P]), pb("moe_l", [P, P]), [pb(f"moe_d{b}", [P, E]) for b in range(2)]
        gate, up, silu, mul, gated = g.sem("moe_gate"), g.sem("moe_up"), g.sem("moe_silu"), g.sem("moe_mul"), g.sem("moe_gated")
        turned, high, low, down = g.sem("moe_turned"), g.sem("moe_high"), g.sem("moe_low"), g.sem("moe_down")
        lweighed, added, stats, aggr = g.sem("moe_lweighed"), g.sem("moe_added"), g.sem("moe_stats"), g.sem("moe_aggr")
        with nc.Block() as block:

            @block.tensor
            def _(pe):
                for i in range(TT + 2):
                    if i < TT:
                        a = lambda k: (xh[:, k, i * P:(i + 1) * P], xl[:, k, i * P:(i + 1) * P])
                        if i >= 2:
                            pe.wait_ge(mul, i - 1)
                        for k in range(EK):
                            mm = product3(pe, pg[i % 2][:, :], a(k), (W["gate"][0][:, k, :], W["gate"][1][:, k, :]),
                                          start=(k == 0), stop=(k == EK - 1))
                        mm.then_inc(gate, 1)
                        for k in range(EK):
                            mm = product3(pe, pu[i % 2][:, :], a(k), (W["up"][0][:, k, :], W["up"][1][:, k, :]),
                                          start=(k == 0), stop=(k == EK - 1))
                        mm.then_inc(up, 1)
                    if 1 <= i <= TT:
                        n = i - 1
                        pe.wait_ge(gated, n + 1)
                        pe.wait_ge(lweighed, n + 1)
                        pe.wait_ge(low, 2 * n)
                        for f in range(FK):
                            pe.transpose(pt[:, f, :], gt[:, n % 2, f * P:(f + 1) * P], g.ident[:, :])
                        pe.transpose(pl[:, :], lw[:, n % 2, :], g.ident[:, :]).then_inc(turned, 1)
                    if i >= 2:
                        n = i - 2
                        pe.wait_ge(low, 2 * n + 2)
                        if n >= 2:
                            pe.wait_ge(added, n - 1)
                        for f in range(FK):
                            product3(pe, pd[n % 2][:, :], (gh[:, n % 2, f, :], gl[:, n % 2, f, :]),
                                     (W["down"][0][:, f, :], W["down"][1][:, f, :]), start=(f == 0), stop=False)
                        product3(pe, pd[n % 2][:, :], (lh[:, n % 2, :], ll[:, n % 2, :]),
                                 (W["loraB"][0], W["loraB"][1]), start=False, stop=True).then_inc(down, 1)

            @block.scalar
            def _(act):
                for i in range(TT + 1):
                    if i < TT:
                        act.wait_ge(gate, i + 1)
                        if i >= 2:
                            act.wait_ge(mul, i - 1)
                        act.activation(sg[:, i % 2, :], pg[i % 2][:, :], ACT.Silu).then_inc(silu, 1)
                    if i >= 1:
                        n = i - 1
                        act.wait_ge(turned, n + 1)
                        if n >= 2:
                            act.wait_ge(down, n - 1)
                        act.activation(gh[:, n % 2, :, :], pt[:, :, :], ACT.Copy).then_inc(high, 1)
                        act.activation(lh[:, n % 2, :], pl[:, :], ACT.Copy).then_inc(high, 1)

            @block.vector
            def _(dve):
                for i in range(TT + 2):
                    if i < TT:
                        dve.wait_ge(silu, i + 1)
                        dve.wait_ge(up, i + 1)
                        dve.tensor_tensor(sg[:, i % 2, :], sg[:, i % 2, :], pu[i % 2][:, :], ALU.mult).then_inc(mul, 1)
                        if i >= 2:
                            dve.wait_ge(turned, i - 1)
                        dve.tensor_tensor(lw[:, i % 2, :].rearrange("p (e r) -> p e r", r=RANK),
                                          lr[:, i, :].rearrange("p (e r) -> p e r", r=RANK),
                                          w[:, i, :].unsqueeze(2).to_broadcast([P, EX, RANK]), ALU.mult).then_inc(lweighed, 1)
                        dve.wait_ge(mul, i + 1)
                        dve.tensor_tensor(gt[:, i % 2, :].rearrange("p (e f) -> p e f", f=EF),
                                          sg[:, i % 2, :].rearrange("p (e f) -> p e f", f=EF),
                                          w[:, i, :].unsqueeze(2).to_broadcast([P, EX, EF]), ALU.mult).then_inc(gated, 1)
                    if 1 <= i <= TT:
                        n = i - 1
                        if n >= 2:
                            dve.wait_ge(down, n - 1)
                        dve.wait_ge(high, 2 * n + 2)
                        dve.tensor_tensor(gl[:, n % 2, :, :], pt[:, :, :], gh[:, n % 2, :, :].bitcast(F32), ALU.subtract).then_inc(low, 1)
                        dve.tensor_tensor(ll[:, n % 2, :], pl[:, :], lh[:, n % 2, :].bitcast(F32), ALU.subtract).then_inc(low, 1)
                    if i >= 2:
                        n = i - 2
                        dve.wait_ge(down, n + 1)
                        dve.tensor_tensor(X[:, n, :], pd[n % 2][:, :], X[:, n, :], ALU.add).then_inc(added, 1)
                        dve.wait_ge(added, n + 1)
                        dve.bn_stats(st[:, n % 2, :], X[:, n, :]).then_inc(stats, 1)
                        dve.wait_ge(stats, n + 1)
                        dve.bn_aggr(mv[:, n, :], st[:, n % 2, :]).then_inc(aggr, 1)


def parts(nc, ctx, name, shape):
    return tuple(ctx.enter_context(nc.sbuf_tensor(f"{name}_{s}", shape, F32R)) for s in ("high", "low"))


NH = 64
HP = 64
DI = NH * HP
NS = 128
TAPS = 4
CL = P
GH = 4
GROUPS = NH // GH
GC = GH * HP
GT = GC // P
HALVES = 2
HC = TT // HALVES
HT = HC * CL
KINDS = 4


def scan_inputs(nc, g, xh, xl, W, ch, dt_bias, A_log, D):
    with ExitStack() as ctx:
        sb = lambda name, shape, dt=F32: ctx.enter_context(nc.sbuf_tensor(name, shape, dt))
        raw = sb("si_raw", [P, 2, TAPS - 1 + T])
        acc = sb("si_acc", [P, 2, T])
        BT, CT = acc[:, 0, :], acc[:, 1, :]
        z = sb("si_z", [P, TT, NH])
        bias = sb("si_bias", [P, NH])
        eA = sb("si_eA", [P, NH])
        dA = sb("si_dA", [P, TT, NH])
        vec_in, hist = g.sem("si_vec"), g.sem("si_hist")
        prod, read, dprod, dread = g.sem("si_prod"), g.sem("si_read"), g.sem("si_dprod"), g.sem("si_dread")
        conv, silu = g.sem("si_conv"), g.sem("si_silu")
        with ExitStack() as inner:
            ps = [inner.enter_context(nc.psum_tensor(f"si_ps{b}", [P, CHUNK], F32)) for b in range(8)]
            with nc.Block() as block:

                @block.sync
                def _(sp):
                    sp.dma_start(bias[:, :], dt_bias.partition_broadcast(P)).then_inc(vec_in, 16)
                    sp.dma_start(eA[:, :], A_log.partition_broadcast(P)).then_inc(vec_in, 16)

                @block.tensor
                def _(pe):
                    for n in range(2 * NCH):
                        j, c = n % 2, n // 2
                        for k in range(EK):
                            mm = product3(pe, ps[n][:, :], (W[0][:, k, j * P:(j + 1) * P], W[1][:, k, j * P:(j + 1) * P]),
                                          (xh[:, k, c * CHUNK:(c + 1) * CHUNK], xl[:, k, c * CHUNK:(c + 1) * CHUNK]),
                                          start=(k == 0), stop=(k == EK - 1))
                        mm.then_inc(prod, 1)
                    for i in range(TT):
                        if i < 8:
                            pe.wait_ge(read, i + 1)
                        else:
                            pe.wait_ge(dread, i - 7)
                        for k in range(EK):
                            mm = product3(pe, ps[i % 8][:, 0:NH], (xh[:, k, i * P:(i + 1) * P], xl[:, k, i * P:(i + 1) * P]),
                                          (W[0][:, k, 2 * NS:], W[1][:, k, 2 * NS:]), start=(k == 0), stop=(k == EK - 1))
                        mm.then_inc(dprod, 1)

                @block.scalar
                def _(act):
                    for n in range(2 * NCH):
                        j, c = n % 2, n // 2
                        act.wait_ge(prod, n + 1)
                        act.activation(raw[:, j, TAPS - 1 + c * CHUNK:TAPS - 1 + (c + 1) * CHUNK], ps[n][:, :],
                                       ACT.Copy).then_inc(read, 1)
                    for i in range(TT):
                        act.wait_ge(dprod, i + 1)
                        act.activation(z[:, i, :], ps[i % 8][:, 0:NH], ACT.Copy).then_inc(dread, 1)
                    act.wait_ge(conv, 8)
                    for j in range(2):
                        act.activation(acc[:, j, :], acc[:, j, :], ACT.Silu).then_inc(silu, 1)
                    act.wait_ge(vec_in, 32)
                    act.activation(eA[:, :], eA[:, :], ACT.Exp).then_inc(silu, 1)
                    act.wait_ge(silu, 3)

                @block.vector
                def _(dve):
                    for j in range(2):
                        dve.memset(raw[:, j, 0:TAPS - 1], 0.0).then_inc(hist, 1)
                    dve.wait_ge(hist, 2)
                    dve.wait_ge(read, 2 * NCH)
                    for tap in range(TAPS):
                        for j in range(2):
                            src = raw[:, j, tap:tap + T]
                            w = ch[:, DI // P + j, tap:tap + 1]
                            if tap == 0:
                                dve.tensor_scalar(acc[:, j, :], src, w, ch[:, DI // P + j, TAPS:TAPS + 1], ALU.mult,
                                                  ALU.add).then_inc(conv, 1)
                            else:
                                dve.wait_ge(conv, 2 * tap + j - 1)
                                dve.scalar_tensor_tensor(out=acc[:, j, :], in0=src, scalar=w, in1=acc[:, j, :],
                                                         op0=ALU.mult, op1=ALU.add).then_inc(conv, 1)

        u, s, s2, q = (raw[:, j, h * TT * NH:(h + 1) * TT * NH] for j in range(2) for h in range(2))
        step, exped = g.sem("si_step"), g.sem("si_exped")
        zf = z[:, :, :].rearrange("p c h -> p (c h)")
        with nc.Block() as block:

            @block.scalar
            def _(act):
                act.wait_ge(step, 2)
                act.activation(u, u, ACT.Exp, scale=-1.0).then_inc(exped, 1)

            @block.vector
            def _(dve):
                n = [0]

                def then(ins):
                    ins.then_inc(step, 1)
                    n[0] += 1
                    dve.wait_ge(step, n[0])

                then(dve.tensor_tensor(z[:, :, :], z[:, :, :], bias[:, :].unsqueeze(1).to_broadcast([P, TT, NH]), ALU.add))
                then(dve.scalar_tensor_tensor(out=u, in0=zf, scalar=-1.0, in1=zf, op0=ALU.mult, op1=ALU.max))
                dve.wait_ge(exped, 1)
                then(dve.tensor_scalar(s, u, 2.0, None, ALU.add))
                then(dve.reciprocal(s, s))
                then(dve.tensor_tensor(s, s, u, ALU.mult))
                then(dve.tensor_tensor(s2, s, s, ALU.mult))
                then(dve.tensor_scalar(q, s2, 1.0 / 15, None, ALU.mult))
                for k in (13, 11, 9, 7, 5, 3):
                    then(dve.scalar_tensor_tensor(out=q, in0=q, scalar=1.0 / k, in1=s2, op0=ALU.add,
                                                  op1=ALU.mult))
                then(dve.scalar_tensor_tensor(out=q, in0=q, scalar=1.0, in1=s, op0=ALU.add, op1=ALU.mult))
                then(dve.tensor_scalar(zf, zf, 0.0, None, ALU.max))
                then(dve.scalar_tensor_tensor(out=zf, in0=q, scalar=2.0, in1=zf, op0=ALU.mult, op1=ALU.add))
                then(dve.scalar_tensor_tensor(out=dA[:, :, :], in0=z[:, :, :], scalar=-1.0,
                                              in1=eA[:, :].unsqueeze(1).to_broadcast([P, TT, NH]), op0=ALU.mult, op1=ALU.mult))

        sm = sb("si_small", [P, GROUPS, HALVES, KINDS, HC, GH])
        upto, after, ones = sb("si_upto", [P, P]), sb("si_after", [P, P]), sb("si_ones", [P, P])
        made, summed, sexp, copied = g.sem("si_made"), g.sem("si_summed"), g.sem("si_sexp"), g.sem("si_copied")
        stored = g.sem("si_stored")
        with ExitStack() as inner:
            ps = [inner.enter_context(nc.psum_tensor(f"si_sum{b}", [P, HC, NH], F32)) for b in range(6)]
            with nc.Block() as block:

                @block.gpsimd
                def _(pool):
                    for m in (upto, after, ones):
                        pool.memset(m[:, :], 1.0).then_inc(made, 1)
                    pool.wait_ge(made, 3)
                    pool.affine_select(out=upto[:, :], in_=upto[:, :], compare_op=ALU.is_ge, fill=0.0, base=0,
                                       pattern=[[1, P]], channel_multiplier=-1).then_inc(made, 1)
                    pool.affine_select(out=after[:, :], in_=after[:, :], compare_op=ALU.is_gt, fill=0.0, base=0,
                                       pattern=[[-1, P]], channel_multiplier=1).then_inc(made, 1)

                @block.tensor
                def _(pe):
                    pe.wait_ge(made, 5)
                    for q, m in enumerate((upto, after, ones)):
                        for hf in range(HALVES):
                            pe.matmul(ps[2 * q + hf][:, :, :], m[:, :], dA[:, hf * HC:(hf + 1) * HC, :],
                                      start=True, stop=True).then_inc(summed, 1)

                @block.scalar
                def _(act):
                    for q in range(3):
                        for hf in range(HALVES):
                            act.wait_ge(summed, 2 * q + hf + 1)
                            act.activation(sm[:, :, hf, q + 1, :, :],
                                           ps[2 * q + hf][:, :, :].rearrange("p c (g h) -> p g c h", h=GH), ACT.Exp).then_inc(sexp, 1)

                @block.vector
                def _(dve):
                    for hf in range(HALVES):
                        dve.tensor_copy(sm[:, :, hf, 0, :, :],
                                        z[:, hf * HC:(hf + 1) * HC, :].rearrange("p c (g h) -> p g c h", h=GH)).then_inc(copied, 1)

                @block.sync
                def _(sp):
                    sp.wait_ge(sexp, 6)
                    sp.wait_ge(copied, 2)
                    sp.dma_start(D["small"], sm[:, :, :, :, :, :].rearrange("p g f k c h -> p (g f k c h)")).then_inc(stored, 16)
                    sp.dma_start(D["C"], CT).then_inc(stored, 16)
                    sp.wait_ge(stored, 32)

        a1, a2, a3 = (sb(f"si_a{i}", [NH, T], BF16) for i in range(3))
        rest = sb("si_rest", [NH, 2, CHUNK])
        Bt, CB = (raw[:, j, 0:T].rearrange("p (c n) -> p c n", n=P) for j in range(2))
        aprod, apart, apdone, acopy = g.sem("si_aprod"), g.sem("si_apart"), g.sem("si_apdone"), g.sem("si_acopy")
        bprod, bread, cprod, cread = g.sem("si_bprod"), g.sem("si_bread"), g.sem("si_cprod"), g.sem("si_cread")
        with ExitStack() as inner:
            ps = [inner.enter_context(nc.psum_tensor(f"si_at{b}", [P, 4, P], F32)) for b in range(8)]
            with nc.Block() as block:

                @block.tensor
                def _(pe):
                    for n in range(4):
                        for c in range(4):
                            mm = pe.matmul(ps[n][0:NH, c, :], dA[:, 4 * n + c, :], upto[:, :], start=True, stop=True)
                        mm.then_inc(aprod, 1)
                    for n in range(4):
                        if n >= 2:
                            pe.wait_ge(bread, n - 1)
                        for c in range(4):
                            i = 4 * n + c
                            mm = pe.transpose(ps[4 + n % 2][:, c, :], BT[:, i * P:(i + 1) * P], g.ident[:, :])
                        mm.then_inc(bprod, 1)
                        if n >= 2:
                            pe.wait_ge(cread, n - 1)
                        for c in range(4):
                            i = 4 * n + c
                            mm = pe.matmul(ps[6 + n % 2][:, c, :], BT[:, i * P:(i + 1) * P], CT[:, i * P:(i + 1) * P],
                                           start=True, stop=True)
                        mm.then_inc(cprod, 1)

                @block.scalar
                def _(act):
                    for n in range(4):
                        act.wait_ge(aprod, n + 1)
                        act.activation(a1[:, n * CHUNK:(n + 1) * CHUNK], ps[n][0:NH, :, :].rearrange("p c l -> p (c l)"),
                                       ACT.Copy).then_inc(acopy, 1)
                    for n in range(4):
                        act.wait_ge(bprod, n + 1)
                        act.activation(Bt[:, 4 * n:4 * n + 4, :], ps[4 + n % 2][:, :, :], ACT.Copy).then_inc(bread, 1)

                @block.vector
                def _(dve):
                    up = upto[:, :].unsqueeze(1).to_broadcast([P, 4, P])
                    for n in range(4):
                        sl = slice(n * CHUNK, (n + 1) * CHUNK)
                        dve.wait_ge(acopy, n + 1)
                        r = rest[:, n % 2, :]
                        dve.tensor_tensor(r, ps[n][0:NH, :, :].rearrange("p c l -> p (c l)"), a1[:, sl], ALU.subtract).then_inc(apart, 1)
                        dve.wait_ge(apart, 3 * n + 1)
                        dve.tensor_copy(a2[:, sl], r).then_inc(apart, 1)
                        dve.wait_ge(apart, 3 * n + 2)
                        dve.tensor_tensor(a3[:, sl], r, a2[:, sl], ALU.subtract).then_inc(apart, 1)
                    for n in range(4):
                        dve.wait_ge(cprod, n + 1)
                        dve.tensor_tensor(CB[:, 4 * n:4 * n + 4, :], ps[6 + n % 2][:, :, :], up, ALU.mult).then_inc(cread, 1)

                @block.sync
                def _(sp):
                    sp.wait_ge(apart, 12)
                    for n, a in enumerate((a1, a2, a3)):
                        sp.dma_start(D["sums"][n], a[:, :]).then_inc(apdone, 16)
                    sp.wait_ge(bread, 4)
                    sp.dma_start(D["B"], Bt).then_inc(apdone, 16)
                    sp.wait_ge(cread, 4)
                    sp.dma_start(D["CB"], CB).then_inc(apdone, 16)
                    sp.wait_ge(apdone, 80)


SLOTS = HC + 4
AK = 3 + 3 * GH


def scan_semaphores(g):
    names = ("x_first xin w_raw w_high w_low wo_raw wo_scaled wo_high wo_low sums_in small_in state_in state_out "
             "ip ip_read hist conv_step conv silu coef dcoef arg exped decay xt xdt xdd y_prod s_prod y_scaled y_sum "
             "s_decayed s_next yt gate_sum gated g_high g_sq g_low sq_add op op_added cleared setup acc_out").split()
    return {n: g.sem("sc_" + n) for n in names}


def scan_half(nc, g, hf, S, D, Wg, WoT, tables, hist, ssq_dram, acc_dram):
    NBK = HT // CHUNK
    CB4 = CHUNK // CL
    first = hf * GROUPS
    with ExitStack() as ctx:
        sb = lambda name, shape, dt=F32: ctx.enter_context(nc.sbuf_tensor(f"{name}_{hf}", shape, dt))
        pb = lambda name, shape: ctx.enter_context(nc.psum_tensor(f"{name}_{hf}", shape, F32))
        xh, xl = sb("sc_xh", [P, EK, HT], F32R), sb("sc_xl", [P, EK, HT], F32R)
        acc, ssq = sb("sc_acc", [P, HC, E]), sb("sc_ssq", [P, HT])
        Bt, Ct, CB = sb("sc_B", [P, HC, NS]), sb("sc_C", [P, HT]), sb("sc_CB", [P, HC, P])
        chan, dtab = sb("sc_chan", [P, 2 * GROUPS + 2, TAPS + 1]), sb("sc_dtab", [P, 2 * GROUPS, 2])
        coef, dcoef = sb("sc_coef", [P, GT, TAPS + 1]), sb("sc_dcoef", [P, GT, 2])
        later = sb("sc_later", [P, GH, P], BF16)
        wr, wh, wl = sb("sc_wr", [P, EK, CHUNK]), sb("sc_wh", [P, 4, EK, P], F32R), sb("sc_wl", [P, 4, EK, P], F32R)
        wor = sb("sc_wor", [P, GT, E])
        woh, wol = sb("sc_woh", [P, GT, E], F32R), sb("sc_wol", [P, GT, E], F32R)
        arhs, alhs = sb("sc_arhs", [AK, HC, GH, CL], BF16), sb("sc_alhs", [AK, HT], BF16)
        small = sb("sc_small", [P, KINDS, HC, GH])
        xr = [[sb(f"sc_xr{j}{b}", [P, TAPS - 1 + CHUNK]) for b in range(NBK)] for j in range(GT)]
        ca = sb("sc_ca", [P, GT, CHUNK])
        xT, zT = sb("sc_xT", [P, NBK, GT, CHUNK]), sb("sc_zT", [P, NBK, GT, CHUNK])
        M = [sb(f"sc_M{b}", [P, GH, CL]) for b in range(2)]
        xdt = [sb(f"sc_xdt{b}", [P, GH, HP]) for b in range(2)]
        xdd = [sb(f"sc_xdd{b}", [P, GH, HP]) for b in range(2)]
        ya = [sb(f"sc_y{b}", [P, GC]) for b in range(2)]
        st = [sb(f"sc_s{b}", [P, GC]) for b in range(2)]
        sd = sb("sc_sd", [P, GC])
        gx, sq = sb("sc_gx", [P, GT, 2 * CL]), sb("sc_sq", [P, GT, 2 * CL])
        gh = [sb(f"sc_gh{b}", [P, GT, 2 * CL], F32R) for b in range(2)]
        gl = [sb(f"sc_gl{b}", [P, GT, 2 * CL], F32R) for b in range(2)]
        p_ip = [pb(f"sc_pip{b}", [P, CHUNK]) for b in range(2)]
        p_arg, p_xt, p_y, p_s = pb("sc_parg", [P, GH, CL]), pb("sc_pxt", [P, GC]), pb("sc_py", [P, 2, GC]), pb("sc_ps", [P, GC])
        p_yt, p_op = pb("sc_pyt", [P, GT, 2, CL]), pb("sc_pop", [P, E])

        def wait(e, name, value):
            if not (isinstance(value, int) and value <= 0):
                e.wait_ge(S[name], value)

        q_ip = lambda G, blk, m: G * 8 + hf * 4 + blk * 4 + m
        q_cv = lambda G, blk, j: G * 4 + hf * 2 + blk * 2 + j
        q_st = lambda G, s: G * HC + s - GROUPS if hf else G * (HC - 1) + s - 1
        q_w = lambda G, m: G * 4 + hf * 4 + m

        def bc(kind, c):
            return small[:, kind, c, :].unsqueeze(2).to_broadcast([P, GH, HP])

        heads = lambda a: a.rearrange("p (h d) -> p h d", d=HP)
        n_setup = 4
        with nc.Block() as block:

            @block.sync
            def _(sp):
                sp.dma_start(wr[:, :, :], Wg[0:1, :, :].rearrange("o (k p) n -> p (o k) n", p=P)).then_inc(S["w_raw"], 16)
                for blk in range(NBK):
                    at = slice(blk * CHUNK, (blk + 1) * CHUNK)
                    for src, dst in ((D["xT"][0], xh), (D["xT"][1], xl)):
                        sp.dma_start(dst[:, :, at].bitcast(F32), src[:, :, hf * HT + blk * CHUNK:hf * HT + (blk + 1) * CHUNK]).then_inc(
                            S["x_first" if blk == 0 else "xin"], 16)
                    if blk == 0:
                        sp.dma_start(chan[:, :, :], tables[0]).then_inc(S["x_first"], 16)
                sp.dma_start(Bt[:, :, :], D["B"][:, hf * HC:(hf + 1) * HC, :]).then_inc(S["xin"], 16)
                sp.dma_start(Ct[:, :], D["C"][:, hf * HT:(hf + 1) * HT]).then_inc(S["xin"], 16)
                sp.dma_start(CB[:, :, :], D["CB"][:, hf * HC:(hf + 1) * HC, :]).then_inc(S["xin"], 16)
                sp.dma_start(dtab[:, :, :], tables[1]).then_inc(S["xin"], 16)

                def load_w(grp):
                    sp.dma_start(wr[:, :, :], Wg[ds(grp, 1), :, :].rearrange("o (k p) n -> p (o k) n", p=P)).then_inc(S["w_raw"], 16)

                def load_wo(grp):
                    sp.dma_start(wor[:, :, :], WoT[ds(grp * GC, GC), :].rearrange("(j p) n -> p j n", p=P)).then_inc(S["wo_raw"], 16)

                def load_sums(grp):
                    for n in range(3):
                        src = D["sums"][n, ds(grp * GH, GH), hf * HT:(hf + 1) * HT]
                        sp.dma_start(arhs[n:n + 1, :, :, :], src.rearrange("h (c l) -> c h l", l=CL).unsqueeze(0)).then_inc(S["sums_in"], 16)
                        sp.dma_start(alhs[3 + GH * n:3 + GH * (n + 1), :], src).then_inc(S["sums_in"], 16)

                def load_small(grp):
                    sp.dma_start(small[:, :, :, :].rearrange("p k c h -> p (k c h)"),
                                 D["small"][:, ds((grp * HALVES + hf) * KINDS * HC * GH, KINDS * HC * GH)]).then_inc(S["small_in"], 16)

                def load_state(grp):
                    if hf == 1:
                        sp.dma_start(st[0][:, :], D["state"][ds(grp, 1), :, :].rearrange("o p n -> p (o n)")).then_inc(S["state_in"], 16)

                sp.wait_ge(S["setup"], n_setup * (hf + 1))
                load_wo(0)
                load_sums(0)
                load_small(0)
                load_state(0)

                def after_group(G, grp, last):
                    sp.wait_ge(S["w_low"], q_w(G, 4))
                    load_w(grp if last else grp + 1)
                    sp.wait_ge(S["wo_low"], (G + 1) * GT)
                    if not last:
                        load_wo(grp + 1)
                    sp.wait_ge(S["arg"], G * HC + HC)
                    if not last:
                        load_sums(grp + 1)
                    sp.wait_ge(S["s_next"], G * HC + HC)
                    sp.wait_ge(S["y_sum"], G * HC + HC)
                    sp.wait_ge(S["xdd"], G * HC + HC)
                    if not last:
                        load_small(grp + 1)
                    if hf == 0:
                        sp.dma_start(D["state"][ds(grp, 1), :, :].rearrange("o p n -> p (o n)"), st[0][:, :]).then_inc(S["state_out"], 16)
                    elif not last:
                        load_state(grp + 1)

                with sp.Fori(first, first + GROUPS - 1) as G:
                    after_group(G, G - first, False)
                after_group(first + GROUPS - 1, GROUPS - 1, True)
                if hf == 0:
                    sp.wait_ge(S["state_out"], 16 * GROUPS)
                sp.wait_ge(S["op_added"], (first + GROUPS) * HC)
                sp.dma_start(acc_dram[:, hf * HC:(hf + 1) * HC, :], acc[:, :, :]).then_inc(S["acc_out"], 16)
                sp.wait_ge(S["sq_add"], (first + GROUPS) * 8)
                sp.dma_start(ssq_dram[:, hf * HT:(hf + 1) * HT], ssq[:, :]).then_inc(S["acc_out"], 16)
                sp.wait_ge(S["acc_out"], 32 * (hf + 1))
                sp.wait_ge(S["w_raw"], 16 * (GROUPS + 1) * (hf + 1))

            @block.gpsimd
            def _(pool):
                s0 = n_setup * hf
                pool.wait_ge(S["cleared"], 5 * (hf + 1))
                pool.affine_select(out=later[:, :, :], in_=later[:, :, :], compare_op=ALU.is_ge, fill=NEG, base=0,
                                   pattern=[[0, GH], [1, CL]], channel_multiplier=-1).then_inc(S["setup"], 1)
                for n in range(3):
                    pool.affine_select(out=arhs[:, :, :, :], in_=arhs[:, :, :, :], compare_op=ALU.not_equal, fill=-1.0,
                                       base=-3 - GH * n, pattern=[[0, HC], [-1, GH], [0, CL]],
                                       channel_multiplier=1).then_inc(S["setup"], 1)
                    pool.wait_ge(S["setup"], s0 + 2 + n)

                with pool.Fori(first, first + GROUPS) as G:
                    for s in range(-1, SLOTS):
                        c = s + 1
                        if c < HC:
                            pool.wait_ge(S["xdt"], G * HC + c + 1)
                            pool.wait_ge(S["s_prod"], G * HC + max(c - 1, 0))
                            pool.tensor_tensor(xdd[c % 2][:, :, :], xdt[c % 2][:, :, :], bc(2, c), ALU.mult).then_inc(S["xdd"], 1)
                        if 0 <= s < HC:
                            if s == 0:
                                if hf == 0:
                                    continue
                                pool.wait_ge(S["small_in"], (G + 1) * 16)
                                pool.wait_ge(S["state_in"], (G - first + 1) * 16)
                            pool.wait_ge(S["s_next"], G * HC + s)
                            pool.tensor_tensor(heads(sd[:, :]), heads(st[s % 2][:, :]), bc(3, s), ALU.mult).then_inc(S["s_decayed"], 1)
                        if s in (1, 2):
                            j = s - 1
                            pool.wait_ge(S["wo_high"], G + 1)
                            pool.tensor_tensor(wol[:, j, :], wor[:, j, :], woh[:, j, :].bitcast(F32), ALU.subtract).then_inc(S["wo_low"], 1)
                        if s in (3, 5, 7, 9):
                            p = (s - 3) // 2
                            pool.wait_ge(S["g_sq"], G * 4 + p + 1)
                            for j in range(GT):
                                pool.wait_ge(S["sq_add"], (G * 4 + p) * 2 + j)
                                part = ssq[:, p * 2 * CL:(p + 1) * 2 * CL]
                                pool.tensor_tensor(part, part, sq[:, j, :], ALU.add).then_inc(S["sq_add"], 1)
                        if s in (4, 6, 8, 10):
                            m = s // 2 - 2
                            src = wr[:, :, m * P:(m + 1) * P]
                            pool.wait_ge(S["w_high"], q_w(G, m) + 5)
                            pool.tensor_tensor(wl[:, m, :, :], src, wh[:, m, :, :].bitcast(F32), ALU.subtract).then_inc(S["w_low"], 1)

            @block.tensor
            def _(pe):
                def ip(G, blk, m):
                    wait(pe, "w_low", q_w(G, m) + 1)
                    wait(pe, "ip_read", q_ip(G, blk, m) - 1)
                    for k in range(EK):
                        mm = product3(pe, p_ip[m % 2][:, :], (wh[:, m, k, :], wl[:, m, k, :]),
                                      (xh[:, k, blk * CHUNK:(blk + 1) * CHUNK], xl[:, k, blk * CHUNK:(blk + 1) * CHUNK]),
                                      start=(k == 0), stop=(k == EK - 1))
                    mm.then_inc(S["ip"], 1)

                pe.wait_ge(S["x_first"], 3 * 16 * (hf + 1))
                for m in range(4):
                    ip(first, 0, m)
                pe.wait_ge(S["xin"], 6 * 16 * (hf + 1))
                pe.wait_ge(S["setup"], n_setup * (hf + 1))
                with pe.Fori(first, first + GROUPS) as G:
                    for s in range(-1, SLOTS):
                        if 0 <= s < 4:
                            ip(G, 1, s)
                        c = s + 1
                        if c < HC:
                            if c == 0:
                                pe.wait_ge(S["sums_in"], (G + 1) * 96)
                            pe.wait_ge(S["exped"], G * HC + c)
                            pe.matmul(p_arg[:, :, :], alhs[:, c * CL:(c + 1) * CL], arhs[:, c, :, :], start=True, stop=False)
                            pe.matmul(p_arg[:, :, :], g.identb[:, :], later[:, :, :], start=False, stop=True).then_inc(S["arg"], 1)
                            pe.wait_ge(S["silu"], q_cv(G, c // CB4, 1) + 1)
                            pe.wait_ge(S["xdt"], G * HC + c)
                            for j in range(GT):
                                mm = pe.transpose(p_xt[:, j * P:(j + 1) * P], xT[:, c // CB4, j, (c % CB4) * CL:(c % CB4 + 1) * CL],
                                                  g.ident[:, :])
                            mm.then_inc(S["xt"], 1)
                        if 0 <= s < HC:
                            pe.wait_ge(S["decay"], G * HC + s + 1)
                            pe.wait_ge(S["xdt"], G * HC + s + 1)
                            pe.wait_ge(S["y_sum"], G * HC + s)
                            for h in range(GH):
                                mm = pe.matmul(p_y[:, 0, h * HP:(h + 1) * HP], M[s % 2][:, h, :], xdt[s % 2][:, h, :], start=True, stop=True)
                            if s == 0 and hf == 1:
                                pe.wait_ge(S["state_in"], (G - first + 1) * 16)
                            pe.wait_ge(S["s_next"], G * HC + s)
                            if s or hf:
                                mm = pe.matmul(p_y[:, 1, :], Ct[:, s * CL:(s + 1) * CL], st[s % 2][:, :], start=True, stop=True)
                            mm.then_inc(S["y_prod"], 1)
                            pe.wait_ge(S["xdd"], G * HC + s + 1)
                            pe.matmul(p_s[:, :], Bt[:, s, :], xdd[s % 2][:, :, :], start=True, stop=True).then_inc(S["s_prod"], 1)
                        if 1 <= s <= HC:
                            c = s - 1
                            pe.wait_ge(S["y_sum"], G * HC + c + 1)
                            if c % 2 == 0:
                                pe.wait_ge(S["gate_sum"], (G * 4 + c // 2) * 2)
                            for j in range(GT):
                                mm = pe.transpose(p_yt[:, j, c % 2, :], ya[c % 2][:, j * P:(j + 1) * P], g.ident[:, :])
                            mm.then_inc(S["yt"], 1)
                        if s >= 4:
                            c = s - 4
                            if c == 0:
                                pe.wait_ge(S["wo_low"], (G + 1) * GT)
                            pe.wait_ge(S["g_low"], G * 4 + c // 2 + 1)
                            pe.wait_ge(S["op_added"], G * HC + c)
                            b = (c // 2) % 2
                            for j in range(GT):
                                mm = product3(pe, p_op[:, :], (gh[b][:, j, (c % 2) * CL:(c % 2 + 1) * CL], gl[b][:, j, (c % 2) * CL:(c % 2 + 1) * CL]),
                                              (woh[:, j, :], wol[:, j, :]), start=(j == 0), stop=(j == GT - 1))
                            mm.then_inc(S["op"], 1)
                        if s >= HC:
                            ip(G + 1, 0, s - HC)

            @block.scalar
            def _(act):
                def ip_read(G, blk, m):
                    act.wait_ge(S["ip"], q_ip(G, blk, m) + 1)
                    if m < GT:
                        wait(act, "conv", q_cv(G, blk, m) - 1)
                        act.activation(xr[m][blk][:, TAPS - 1:], p_ip[m % 2][:, :], ACT.Copy).then_inc(S["ip_read"], 1)
                    else:
                        wait(act, "gated", G * 4 + 2 * blk - 2)
                        act.activation(zT[:, blk, m - GT, :], p_ip[m % 2][:, :], ACT.Silu).then_inc(S["ip_read"], 1)

                def silu(G, blk, j):
                    act.wait_ge(S["conv"], q_cv(G, blk, j) + 1)
                    wait(act, "gated", G * 4 + 2 * blk - 2)
                    wait(act, "xt", G * HC + (blk + 1) * CB4 - HC)
                    act.activation(xT[:, blk, j, :], ca[:, j, :], ACT.Silu).then_inc(S["silu"], 1)

                def w_high(m):
                    act.activation(wh[:, m, :, :], wr[:, :, m * P:(m + 1) * P], ACT.Copy).then_inc(S["w_high"], 1)

                act.wait_ge(S["w_raw"], ((GROUPS + 1) * hf + 1) * 16)
                for m in range(4):
                    w_high(m)
                for m in range(4):
                    ip_read(first, 0, m)
                    if m >= 1 and m - 1 < GT:
                        silu(first, 0, m - 1)
                with act.Fori(first, first + GROUPS) as G:
                    for s in range(-1, SLOTS):
                        c = s + 1
                        if s == 3:
                            for j in range(GT):
                                silu(G, 1, j)
                            for m in range(GT, 2 * GT):
                                ip_read(G, 1, m)
                        if c < HC:
                            act.wait_ge(S["arg"], G * HC + c + 1)
                            act.wait_ge(S["y_prod"], G * HC + max(c - 1, 0))
                            act.activation(M[c % 2][:, :, :], p_arg[:, :, :], ACT.Exp).then_inc(S["exped"], 1)
                        if 0 <= s < GT:
                            ip_read(G, 1, s)
                        if s in (3, 5, 7, 9):
                            p = (s - 3) // 2
                            act.wait_ge(S["gated"], G * 4 + p + 1)
                            act.wait_ge(S["op"], G * HC + max(2 * p - 2, 0))
                            act.activation(gh[p % 2][:, :, :], gx[:, :, :], ACT.Copy).then_inc(S["g_high"], 1)
                            act.wait_ge(S["sq_add"], (G * 4 + p) * 2)
                            act.activation(sq[:, :, :], gx[:, :, :], ACT.Square).then_inc(S["g_sq"], 1)
                        if s >= HC + 2:
                            silu(G + 1, 0, s - HC - 2)
                        if s >= HC:
                            ip_read(G + 1, 0, s - HC)
                        if s == 0:
                            act.wait_ge(S["wo_raw"], (G + 1) * 16)
                            act.wait_ge(S["dcoef"], G + 1)
                            act.wait_ge(S["op"], G * HC)
                            for j in range(GT):
                                act.activation(wor[:, j, :], wor[:, j, :], ACT.Copy, scale=dcoef[:, j, 1:2]).then_inc(S["wo_scaled"], 1)
                            act.wait_ge(S["wo_scaled"], (G + 1) * GT)
                            act.activation(woh[:, :, :], wor[:, :, :], ACT.Copy).then_inc(S["wo_high"], 1)
                        if 3 <= s < 7:
                            m = s - 3
                            act.wait_ge(S["w_raw"], (G + hf + 2) * 16)
                            act.wait_ge(S["ip"], q_ip(G, 1, m) + 1)
                            w_high(m)

            @block.vector
            def _(dve):
                def conv(G, blk, j):
                    grp = G - first
                    n = 4 * q_cv(G, blk, j)
                    dve.wait_ge(S["ip_read"], q_ip(G, blk, j) + 1)
                    if blk == 0:
                        before = hist[:, ds(grp * GT + j, 1), :].rearrange("p o k -> p (o k)")
                    else:
                        before = xr[j][0][:, CHUNK:CHUNK + TAPS - 1]
                    dve.tensor_copy(xr[j][blk][:, 0:TAPS - 1], before).then_inc(S["conv_step"], 1)
                    dve.wait_ge(S["conv_step"], n + 1)
                    if blk == NBK - 1:
                        dve.tensor_copy(hist[:, ds(grp * GT + j, 1), :].rearrange("p o k -> p (o k)"),
                                        xr[j][blk][:, CHUNK:CHUNK + TAPS - 1]).then_inc(S["hist"], 1)
                    wait(dve, "silu", q_cv(G, blk, j) - 1)
                    for tap in range(TAPS):
                        src = xr[j][blk][:, tap:tap + CHUNK]
                        w = coef[:, j, tap:tap + 1]
                        if tap == 0:
                            dve.tensor_scalar(ca[:, j, :], src, w, coef[:, j, TAPS:TAPS + 1], ALU.mult,
                                              ALU.add).then_inc(S["conv_step"], 1)
                        else:
                            dve.wait_ge(S["conv_step"], n + 1 + tap)
                            last = tap == TAPS - 1
                            dve.scalar_tensor_tensor(out=ca[:, j, :], in0=src, scalar=w, in1=ca[:, j, :], op0=ALU.mult,
                                                     op1=ALU.add).then_inc(S["conv" if last else "conv_step"], 1)

                def coefficients(G):
                    dve.tensor_copy(coef[:, :, :], chan[:, ds((G - first) * GT, GT), :]).then_inc(S["coef"], 1)
                    dve.wait_ge(S["coef"], G + hf + 1)

                def add_out(G, c):
                    dve.wait_ge(S["op"], G * HC + c + 1)
                    dve.tensor_tensor(acc[:, c, :], acc[:, c, :], p_op[:, :], ALU.add).then_inc(S["op_added"], 1)

                for buf, value in ((arhs[:, :, :, :], 0.0), (alhs[:, :], 1.0), (later[:, :, :], 0.0), (ssq[:, :], 0.0), (acc[:, :, :], 0.0)):
                    dve.memset(buf, value).then_inc(S["cleared"], 1)
                for m in range(4):
                    dve.wait_ge(S["w_high"], q_w(first, m) + 1)
                    dve.tensor_tensor(wl[:, m, :, :], wr[:, :, m * P:(m + 1) * P], wh[:, m, :, :].bitcast(F32), ALU.subtract).then_inc(S["w_low"], 1)
                dve.wait_ge(S["x_first"], 3 * 16 * (hf + 1))
                coefficients(first)
                for j in range(GT):
                    conv(first, 0, j)
                dve.wait_ge(S["xin"], 6 * 16 * (hf + 1))
                with dve.Fori(first, first + GROUPS) as G:
                    for s in range(-1, SLOTS):
                        if 5 <= s <= HC:
                            add_out(G, s - 5)
                        c = s + 1
                        if c < HC:
                            if c == 0:
                                dve.wait_ge(S["small_in"], (G + 1) * 16)
                            dve.wait_ge(S["xt"], G * HC + c + 1)
                            dve.wait_ge(S["y_prod"], G * HC + max(c - 1, 0))
                            dve.wait_ge(S["xdd"], G * HC + max(c - 1, 0))
                            dve.tensor_tensor(xdt[c % 2][:, :, :], heads(p_xt[:, :]), bc(0, c), ALU.mult).then_inc(S["xdt"], 1)
                            dve.wait_ge(S["exped"], G * HC + c + 1)
                            dve.tensor_tensor(M[c % 2][:, :, :], M[c % 2][:, :, :],
                                              CB[:, c, :].unsqueeze(1).to_broadcast([P, GH, CL]), ALU.mult).then_inc(S["decay"], 1)
                        if s == -1:
                            dve.wait_ge(S["wo_scaled"], G * GT)
                            dve.tensor_copy(dcoef[:, :, :], dtab[:, ds((G - first) * GT, GT), :]).then_inc(S["dcoef"], 1)
                            dve.wait_ge(S["dcoef"], G + 1)
                        if 0 <= s < HC:
                            dve.wait_ge(S["y_prod"], G * HC + s + 1)
                            dve.wait_ge(S["yt"], G * HC + max(s - 1, 0))
                            if s == 0 and hf == 0:
                                dve.tensor_copy(ya[0][:, :], p_y[:, 0, :]).then_inc(S["y_sum"], 1)
                                dve.wait_ge(S["s_prod"], G * HC + 1)
                                dve.tensor_copy(st[1][:, :], p_s[:, :]).then_inc(S["s_next"], 1)
                            else:
                                dve.tensor_tensor(heads(ya[s % 2][:, :]), heads(p_y[:, 1, :]), bc(1, s), ALU.mult).then_inc(S["y_scaled"], 1)
                                dve.wait_ge(S["y_scaled"], q_st(G, s) + 1)
                                dve.tensor_tensor(ya[s % 2][:, :], ya[s % 2][:, :], p_y[:, 0, :], ALU.add).then_inc(S["y_sum"], 1)
                                dve.wait_ge(S["s_prod"], G * HC + s + 1)
                                dve.wait_ge(S["s_decayed"], q_st(G, s) + 1)
                                if s == 1 and hf == 0:
                                    dve.wait_ge(S["state_out"], G * 16)
                                dve.tensor_tensor(st[(s + 1) % 2][:, :], sd[:, :], p_s[:, :], ALU.add).then_inc(S["s_next"], 1)
                        if s in (3, 5, 7, 9):
                            p = (s - 3) // 2
                            dve.wait_ge(S["g_high"], G * 4 + p + 1)
                            dve.tensor_tensor(gl[p % 2][:, :, :], gx[:, :, :], gh[p % 2][:, :, :].bitcast(F32), ALU.subtract).then_inc(S["g_low"], 1)
                        if s in (2, 4, 6, 8):
                            p = s // 2 - 1
                            blk, at = p // 2, (p % 2) * 2 * CL
                            dve.wait_ge(S["yt"], G * HC + 2 * p + 2)
                            dve.wait_ge(S["g_sq"], G * 4 + p)
                            dve.wait_ge(S["g_low"], G * 4 + p)
                            for j in range(GT):
                                dve.scalar_tensor_tensor(out=gx[:, j, :], in0=xT[:, blk, j, at:at + 2 * CL], scalar=dcoef[:, j, 0:1],
                                                         in1=p_yt[:, j, :, :].rearrange("p a l -> p (a l)"), op0=ALU.mult,
                                                         op1=ALU.add).then_inc(S["gate_sum"], 1)
                            dve.wait_ge(S["ip_read"], q_ip(G, blk, 3) + 1)
                            dve.wait_ge(S["gate_sum"], (G * 4 + p + 1) * 2)
                            dve.tensor_tensor(gx[:, :, :], gx[:, :, :], zT[:, blk, :, at:at + 2 * CL], ALU.mult).then_inc(S["gated"], 1)
                        if s >= HC:
                            add_out(G, s - 4)
                        if 0 <= s < GT:
                            conv(G, 1, s)
                        if s == HC:
                            coefficients(G + 1)
                        if HC + 1 <= s < HC + 1 + GT:
                            conv(G + 1, 0, s - HC - 1)


def scan_end(nc, g, X, x_dram, acc_dram, ssq_dram, mv):
    with ExitStack() as ctx:
        sb = lambda name, shape, dt=F32: ctx.enter_context(nc.sbuf_tensor(name, shape, dt))
        ssq, ones = sb("se_ssq", [P, T]), sb("se_ones", [P, 1])
        acc = sb("se_acc", [P, 4, E])
        rstd = sb("se_rstd", [P, TT])
        stt = sb("se_stats", [P, 2, 6])
        ps = ctx.enter_context(nc.psum_tensor("se_ps", [P, TT], F32))
        x_in, ss_in, a_in = g.sem("se_x"), g.sem("se_ss"), [g.sem(f"se_a{b}") for b in range(4)]
        made, summed, step, root = g.sem("se_made"), g.sem("se_summed"), g.sem("se_step"), g.sem("se_root")
        added, stats, aggr = g.sem("se_added"), g.sem("se_stats"), g.sem("se_aggr")
        with nc.Block() as block:

            @block.gpsimd
            def _(pool):
                pool.memset(ones[:, :], 1.0).then_inc(made, 1)

            @block.sync
            def _(sp):
                sp.dma_start(ssq[:, :], ssq_dram).then_inc(ss_in, 16)
                sp.dma_start(X[:, :, :], x_dram.rearrange("(i p) n -> p i n", p=P)).then_inc(x_in, 16)
                for i in range(TT):
                    if i >= 4:
                        sp.wait_ge(added, i - 3)
                    sp.dma_start(acc[:, i % 4, :], acc_dram[:, i, :]).then_inc(a_in[i % 4], 16)

            @block.tensor
            def _(pe):
                pe.wait_ge(made, 1)
                pe.wait_ge(ss_in, 16)
                for i in range(TT):
                    mm = pe.matmul(ps[:, i:i + 1], ssq[:, i * P:(i + 1) * P], ones[:, :], start=True, stop=True)
                mm.then_inc(summed, 1)

            @block.scalar
            def _(act):
                act.wait_ge(step, 1)
                act.activation(rstd[:, :], rstd[:, :], ACT.Sqrt).then_inc(root, 1)

            @block.vector
            def _(dve):
                dve.wait_ge(summed, 1)
                dve.tensor_scalar(rstd[:, :], ps[:, :], 1.0 / DI, LN_EPS, ALU.mult, ALU.add).then_inc(step, 1)
                dve.wait_ge(root, 1)
                dve.reciprocal(rstd[:, :], rstd[:, :]).then_inc(step, 1)
                dve.wait_ge(step, 2)
                dve.wait_ge(x_in, 16)
                for i in range(TT):
                    dve.wait_ge(a_in[i % 4], 16 * (i // 4 + 1))
                    dve.scalar_tensor_tensor(out=X[:, i, :], in0=acc[:, i % 4, :], scalar=rstd[:, i:i + 1], in1=X[:, i, :],
                                             op0=ALU.mult, op1=ALU.add).then_inc(added, 1)
                    dve.wait_ge(added, i + 1)
                    dve.bn_stats(stt[:, i % 2, :], X[:, i, :]).then_inc(stats, 1)
                    dve.wait_ge(stats, i + 1)
                    dve.bn_aggr(mv[:, i, :], stt[:, i % 2, :]).then_inc(aggr, 1)


FF = 2048
FT = FF // P


def ffn_weights(nc, g, sources, parts_of):
    (Wgate, Wup, Wdown), (wg, wu, wd) = sources, parts_of
    SLOTS8 = 4
    with ExitStack() as ctx:
        w32 = ctx.enter_context(nc.sbuf_tensor("ff_w8", [P, SLOTS8, FF // 4], mybir.dt.int32))
        w8 = lambda slot: w32[:, slot, :].bitcast(mybir.dt.int8)
        w_in = [g.sem(f"ff_w{b}") for b in range(SLOTS8)]
        made_a, made_d = g.sem("ff_made_a"), g.sem("ff_made_d")
        rows = [(W[k * P:(k + 1) * P, :], w[:, k, :]) for W, w in ((Wgate, wg), (Wup, wu)) for k in range(EK)]
        rows += [(Wdown[4 * k * P:4 * (k + 1) * P, :].rearrange("(k p) n -> p k n", p=P), wd[:, 4 * k:4 * k + 4, :].rearrange("p k n -> p (k n)"))
                 for k in range(FT // 4)]
        with nc.Block() as block:

            @block.sync
            def _(sp):
                for n, (src, dst) in enumerate(rows):
                    if n >= SLOTS8:
                        sp.wait_ge((made_a, made_d)[(n - SLOTS8) % 2], (n - SLOTS8) // 2 + 1)
                    to = w32[:, n % SLOTS8, :]
                    if n >= 2 * EK:
                        to = to.rearrange("p (k n) -> p k n", k=4)
                    sp.dma_start(to, src).then_inc(w_in[n % SLOTS8], 16)

            @block.scalar
            def _(act):
                for n in range(0, len(rows), 2):
                    act.wait_ge(w_in[n % SLOTS8], 16 * (n // SLOTS8 + 1))
                    act.activation(rows[n][1], w8(n % SLOTS8), ACT.Copy).then_inc(made_a, 1)

            @block.vector
            def _(dve):
                for n in range(1, len(rows), 2):
                    dve.wait_ge(w_in[n % SLOTS8], 16 * (n // SLOTS8 + 1))
                    dve.tensor_copy(rows[n][1], w8(n % SLOTS8)).then_inc(made_d, 1)


def ffn(nc, g, X, xT_dram, weights, scales, s_down, st_all):
    with ExitStack() as ctx:
        sb = lambda name, shape, dt=F32: ctx.enter_context(nc.sbuf_tensor(name, shape, dt))
        pb = lambda name: ctx.enter_context(nc.psum_tensor(name, [P, CHUNK], F32))
        wg, wu, wd = weights
        sc, sdn = sb("ff_sc", [P, 2, FT]), sb("ff_sdn", [P, E])
        xb = [[sb(f"ff_x{p}{b}", [P, EK, CHUNK], F32R) for b in range(2)] for p in range(2)]
        sg, fz = sb("ff_sg", [P, 2, CHUNK]), sb("ff_fz", [P, 2, CHUNK])
        fh, fl = sb("ff_fh", [P, 2, CHUNK], F32R), sb("ff_fl", [P, 2, CHUNK], F32R)
        tmp = sb("ff_tmp", [P, E])
        res, stt = sb("ff_res", [P, 2, E]), sb("ff_stats", [P, 2, 6])
        pg, pu = [pb(f"ff_pg{b}") for b in range(2)], [pb(f"ff_pu{b}") for b in range(2)]
        pd = [pb(f"ff_pd{b}") for b in range(4)]
        vec_in = g.sem("ff_vec")
        x_in = [g.sem(f"ff_x{b}") for b in range(2)]
        gate, up, silu, fused, high, low = (g.sem("ff_" + n) for n in ("gate", "up", "silu", "fused", "high", "low"))
        down, scaled, added, stats, kept = (g.sem("ff_" + n) for n in ("down", "scaled", "added", "stats", "kept"))
        ITER, PER = 2, 2 * FT
        with nc.Block() as block:

            @block.sync
            def _(sp):
                for b in range(2):
                    for p in range(2):
                        sp.dma_start(xb[p][b][:, :, :].bitcast(F32), xT_dram[p][:, :, b * CHUNK:(b + 1) * CHUNK]).then_inc(x_in[b], 16)
                    if b == 0:
                        sp.dma_start(sc[:, :, :], scales).then_inc(vec_in, 16)
                        sp.dma_start(sdn[:, :], s_down.partition_broadcast(P)).then_inc(vec_in, 16)
                for b in range(2):
                    sp.wait_ge(up, (b + 1) * FT)
                    for p in range(2):
                        sp.dma_start(xb[p][b][:, :, :].bitcast(F32), xT_dram[p][:, :, (2 + b) * CHUNK:(3 + b) * CHUNK]).then_inc(x_in[b], 16)

            @block.tensor
            def _(pe):
                with pe.Fori(0, ITER) as it:
                    for t in range(PER + 1):
                        if t < PER:
                            b, f = t // FT, t % FT
                            if f == 0:
                                pe.wait_ge(x_in[b], (it + 1) * 32)
                            pe.wait_ge(fused, it * PER + max(t - 1, 0))
                            for w, ps, s in ((wg, pg, gate), (wu, pu, up)):
                                for k in range(EK):
                                    for part in (1, 0):
                                        mm = pe.matmul(ps[t % 2][:, :], w[:, k, f * P:(f + 1) * P], xb[part][b][:, k, :],
                                                       start=(k == 0 and part == 1), stop=(k == EK - 1 and part == 0))
                                mm.then_inc(s, 1)
                        if t >= 1:
                            n = t - 1
                            f = n % FT
                            pe.wait_ge(low, it * PER + n + 1)
                            for i in range(4):
                                if f == 0:
                                    blk = it * 2 + n // FT
                                    if n // FT == 0:
                                        pe.wait_ge(scaled, blk * 4)
                                    else:
                                        pe.wait_ge(scaled, blk * 4 - 3 + i)
                                sl = slice(i * P, (i + 1) * P)
                                pe.matmul(pd[i][:, :], fl[:, n % 2, sl], wd[:, f, :], start=(f == 0), stop=False)
                                mm = pe.matmul(pd[i][:, :], fh[:, n % 2, sl], wd[:, f, :], start=False, stop=(f == FT - 1))
                            mm.then_inc(down, 1)

            @block.scalar
            def _(act):
                act.wait_ge(vec_in, 32)
                with act.Fori(0, ITER) as it:
                    for t in range(PER + 1):
                        f = t % FT
                        if t < PER:
                            act.wait_ge(gate, it * PER + t + 1)
                            act.activation(sg[:, t % 2, :], pg[t % 2][:, :], ACT.Silu, scale=sc[:, 0, f:f + 1]).then_inc(silu, 1)
                            act.wait_ge(fused, it * PER + t + 1)
                            act.wait_ge(down, it * PER + max(t - 1, 0))
                            act.activation(fh[:, t % 2, :], fz[:, t % 2, :], ACT.Copy).then_inc(high, 1)
                        if t >= 1 and f == 0:
                            for i in range(4):
                                n = (it * 2 + t // FT - 1) * 4 + i
                                act.wait_ge(added, n + 1)
                                act.activation(X[:, ds(n, 1), :].rearrange("p o n -> p (o n)"), res[:, i % 2, :], ACT.Copy).then_inc(kept, 1)
                                act.wait_ge(stats, n + 1)
                                act.activation(st_all[:, ds(n, 1), :].rearrange("p o n -> p (o n)"), stt[:, i % 2, :], ACT.Copy).then_inc(kept, 1)

            @block.vector
            def _(dve):
                dve.wait_ge(vec_in, 32)
                with dve.Fori(0, ITER) as it:
                    for t in range(PER + 1):
                        if t < PER:
                            f = t % FT
                            dve.wait_ge(silu, it * PER + t + 1)
                            dve.wait_ge(up, it * PER + t + 1)
                            dve.wait_ge(low, it * PER + max(t - 1, 0))
                            dve.scalar_tensor_tensor(out=fz[:, t % 2, :], in0=pu[t % 2][:, :], scalar=sc[:, 1, f:f + 1],
                                                     in1=sg[:, t % 2, :], op0=ALU.mult, op1=ALU.mult).then_inc(fused, 1)
                            dve.wait_ge(high, it * PER + t + 1)
                            dve.tensor_tensor(fl[:, t % 2, :], fz[:, t % 2, :], fh[:, t % 2, :].bitcast(F32), ALU.subtract).then_inc(low, 1)
                        if t >= 1 and t % FT == 0:
                            b = t // FT - 1
                            dve.wait_ge(down, it * PER + t)
                            for i in range(4):
                                n = (it * 2 + b) * 4 + i
                                dve.wait_ge(added, n)
                                dve.tensor_tensor(tmp[:, :], pd[i][:, :], sdn[:, :], ALU.mult).then_inc(scaled, 1)
                                dve.wait_ge(scaled, n + 1)
                                row = X[:, ds(n, 1), :].rearrange("p o n -> p (o n)")
                                dve.wait_ge(kept, 2 * (it * 8 + max(b * 4 + i - 1, 0)))
                                dve.tensor_tensor(res[:, i % 2, :], row, tmp[:, :], ALU.add).then_inc(added, 1)
                                dve.wait_ge(added, n + 1)
                                dve.bn_stats(stt[:, i % 2, :], res[:, i % 2, :]).then_inc(stats, 1)


def norm_out(nc, g, X, st_all, out):
    with ExitStack() as ctx:
        mv = ctx.enter_context(nc.sbuf_tensor("no_mv", [P, TT, 2], F32))
        rstd = ctx.enter_context(nc.sbuf_tensor("no_rstd", [P, TT], F32))
        eps, root, inv, normed, stored = (g.sem("no_" + n) for n in ("eps", "root", "inv", "normed", "stored"))
        aggr = g.sem("no_aggr")
        with nc.Block() as block:

            @block.scalar
            def _(act):
                act.wait_ge(eps, 1)
                act.activation(rstd[:, :], rstd[:, :], ACT.Sqrt).then_inc(root, 1)

            @block.vector
            def _(dve):
                for i in range(TT):
                    dve.bn_aggr(mv[:, i, :], st_all[:, i, :]).then_inc(aggr, 1)
                dve.wait_ge(aggr, TT)
                dve.tensor_scalar(rstd[:, :], mv[:, :, 1], LN_EPS, None, ALU.add).then_inc(eps, 1)
                dve.wait_ge(root, 1)
                dve.reciprocal(rstd[:, :], rstd[:, :]).then_inc(inv, 1)
                dve.wait_ge(inv, 1)
                for i in range(TT):
                    dve.tensor_scalar(X[:, i, :], X[:, i, :], mv[:, i, 0:1], rstd[:, i:i + 1], ALU.subtract,
                                      ALU.mult).then_inc(normed, 1)

            @block.sync
            def _(sp):
                for i in range(0, TT, 2):
                    sp.wait_ge(normed, i + 2)
                    sp.dma_start(out[i * P:(i + 2) * P, :].rearrange("(i p) n -> p i n", p=P), X[:, i:i + 2, :]).then_inc(stored, 16)
                sp.wait_ge(stored, 16 * TT // 2)


class Shared:

    def __init__(self, nc, ctx):
        self.nc, self.ctx, self.turns, self.sems = nc, ctx, 0, []
        self.ident = self.sbuf("ident", [P, P])
        self.identb = self.sbuf("identb", [P, P], BF16)
        self.causal = self.sbuf("causal", [P, P], BF16)
        self.causalT = self.sbuf("causalT", [P, P], BF16)
        self.neg_lam = self.sbuf("neg_lam", [P, 1])

    def sbuf(self, name, shape, dt=F32):
        return self.ctx.enter_context(self.nc.sbuf_tensor(name, shape, dt))

    def sem(self, name):
        self.sems.append(self.nc.alloc_semaphore(name=name))
        return self.sems[-1]

    def end_stage(self):
        self.nc.clear_and_free_semaphores(self.sems)
        self.nc.all_engine_barrier()
        self.sems = []

    def tag(self):
        self.turns += 1
        return str(self.turns)


def keep(nc, g, name, pairs):
    stored = g.sem("kept_" + name)
    with nc.Block() as block:

        @block.scalar
        def _(act):
            for src, dst in pairs:
                act.dma_start(dst, src).then_inc(stored, 16)
    return stored, 16 * len(pairs)


def await_kept(nc, kept):
    with nc.Block() as block:

        @block.sync
        def _(sp):
            sp.wait_ge(*kept)


def two_layers(nc, x, xT, Wq, Wk, Wv, Wo, lq1, lk1, lq2, lk2, first, gate, up, down, lora_b, scan_first, chan_table,
               dt_bias, A_log, Wg, WoT, norm_table, w_gate, w_up, w_down, scales, s_down, out):
    def dram(name, shape, dt=F32):
        return nc.dram_tensor(name, shape, dt, kind="Internal").ap()

    by_row = lambda a: a.rearrange("(k p) n -> p k n", p=P)
    with ExitStack() as ctx:
        g = Shared(nc, ctx)
        QD, KD = dram("q_parts", [2, E, T]), dram("k_parts", [2, E, T])
        x2 = dram("x2", [T, E])
        D = dict(small=dram("scan_small", [P, GROUPS * HALVES * KINDS * HC * GH]), sums=dram("scan_sums", [3, NH, T], BF16),
                 B=dram("scan_B", [P, TT, NS]), C=dram("scan_C", [P, T]), CB=dram("scan_CB", [P, TT, P]),
                 state=dram("scan_state", [GROUPS, P, GC]), xT=[dram("x2_high", [P, EK, T]), dram("x2_low", [P, EK, T])])
        x3_parts = [dram("x3_high", [P, EK, T]), dram("x3_low", [P, EK, T])]
        acc_dram, ssq_dram = dram("scan_acc", [P, TT, E]), dram("scan_ssq", [P, T])
        mv = g.sbuf("row_stats", [P, TT, 2])
        hist = g.sbuf("conv_history", [P, 2 * GROUPS + 2, TAPS - 1])
        constants(nc, g)

        def split(c, name, src, rows, cols, raw):
            hi, lo = parts(nc, c, name, [P, rows, cols])
            slot = raw[:, 0:rows * cols].rearrange("p (k n) -> p k n", k=rows)
            return (by_row(src), slot, hi[:, :, :], lo[:, :, :]), (hi, lo)

        with nc.sbuf_tensor("V_then_X", [P, TT, E], F32) as X:
            g.V = X
            with nc.sbuf_tensor("xh", [P, EK, T], F32R) as g.xh, nc.sbuf_tensor("xl", [P, EK, T], F32R) as g.xl:
                qkv(nc, g, xT, Wq, Wk, Wv, QD, KD)
            with nc.sbuf_tensor("A", [P, TT, E], F32) as g.A:
                attention(nc, g, QD, KD, (lq1, lk1, lq2, lk2))
                g.end_stage()
                with ExitStack() as c:
                    ah, al = parts(nc, c, "aT", [P, EK, T])
                    raw = c.enter_context(nc.sbuf_tensor("wo_raw", [P, EK * E], F32))
                    item, wo = split(c, "wo", Wo, EK, E, raw)
                    rms_norm(nc, g, g.A)
                    turn(nc, g, g.A, ah, al, weights=Weights(g, "o", [item]))
                    project_out(nc, g, x, X, ah, al, wo[0], wo[1], mv)
            with ExitStack() as c:
                xh, xl = parts(nc, c, "xT", [P, EK, T])
                with ExitStack() as c2:
                    raw = [c2.enter_context(nc.sbuf_tensor(f"moe_raw{b}", [P, EK * E], F32)) for b in range(2)]
                    items, W = [], {}
                    for n, (name, src, rows, cols) in enumerate((("first", first, EK, EX * RANK + EX), ("gate", gate, EK, E), ("up", up, EK, E),
                                                                 ("down", down, FK, E), ("lora_b", lora_b, 1, E))):
                        item, W[name] = split(c2, name, src, rows, cols, raw[n % 2])
                        items.append(item)
                    W["loraB"] = tuple(w[:, 0, :] for w in W["lora_b"])
                    turn(nc, g, X, xh, xl, mv, weights=Weights(g, "moe", items))
                    moe(nc, g, X, xh, xl, W, mv)
                with ExitStack() as c2:
                    raw = c2.enter_context(nc.sbuf_tensor("scan_raw", [P, EK * 2 * NS + EK * NH], F32))
                    item, W = split(c2, "scan_first", scan_first, EK, 2 * NS + NH, raw)
                    chan = c2.enter_context(nc.sbuf_tensor("chan", [P, 2 * GROUPS + 2, TAPS + 1], F32))
                    turn(nc, g, X, xh, xl, mv, weights=Weights(g, "scan", [item]))
                    g.end_stage()
                    chan_in, hist_zero = g.sem("chan_in"), g.sem("hist_zero")
                    with nc.Block() as block:

                        @block.sync
                        def _(sp):
                            sp.dma_start(chan[:, :, :], chan_table).then_inc(chan_in, 16)
                            sp.wait_ge(chan_in, 16)

                        @block.vector
                        def _(dve):
                            dve.memset(hist[:, :, :], 0.0).then_inc(hist_zero, 1)
                    stored = keep(nc, g, "x2", [(X[:, :, :], by_row(x2)), (xh[:, :, :].bitcast(F32), D["xT"][0]), (xl[:, :, :].bitcast(F32), D["xT"][1])])
                    scan_inputs(nc, g, xh, xl, W, chan, dt_bias, A_log, D)
                    await_kept(nc, stored)
        g.end_stage()
        S = scan_semaphores(g)
        for half in range(HALVES):
            scan_half(nc, g, half, S, D, Wg, WoT, (chan_table, norm_table), hist, ssq_dram, acc_dram)
        g.end_stage()
        with nc.sbuf_tensor("X_1", [P, TT, E], F32) as X, ExitStack() as ff:
            scan_end(nc, g, X, x2, acc_dram, ssq_dram, mv)
            w_ff = tuple(ff.enter_context(nc.sbuf_tensor(f"ff_{n}", shape, F32R)) for n, shape in
                         (("gate", [P, EK, FF]), ("up", [P, EK, FF]), ("down", [P, FT, E])))
            with ExitStack() as c:
                xh, xl = parts(nc, c, "x3T", [P, EK, T])
                turn(nc, g, X, xh, xl, mv)
                kept = keep(nc, g, "x3", [(xh[:, :, :].bitcast(F32), x3_parts[0]), (xl[:, :, :].bitcast(F32), x3_parts[1])])
                ffn_weights(nc, g, (w_gate, w_up, w_down), w_ff)
                await_kept(nc, kept)
            with nc.sbuf_tensor("out_stats", [P, TT, 6], F32) as st_all:
                ffn(nc, g, X, x3_parts, w_ff, scales, s_down, st_all)
                norm_out(nc, g, X, st_all, out)


def kernel(**inputs):
    import numpy as np
    import concourse.bacc as bacc
    from concourse.bass_utils import run_bass_kernel_spmd

    c = np.ascontiguousarray
    i = {n: np.asarray(a) for n, a in inputs.items()}
    x = c(i["L0_attn_x"].reshape(T, E))
    wide = lambda w: c(w.reshape(-1, E).T)
    deep = lambda w: c(w.transpose(0, 2, 1).reshape(-1, E))
    w_in = i["L1_attn_W_in"].T
    grouped = lambda w: w.reshape(E, GROUPS, GC)
    by_channel = lambda a: c(a.reshape(-1, P, a.shape[1]).transpose(1, 0, 2))
    words = lambda a: c(a).view(np.int32)
    args = dict(
        x=x, xT=c(x.T), Wq=i["L0_attn_Wq"], Wk=i["L0_attn_Wk"], Wv=i["L0_attn_Wv"], Wo=i["L0_attn_Wo"],
        lq1=i["L0_attn_lq1"], lk1=i["L0_attn_lk1"], lq2=i["L0_attn_lq2"], lk2=i["L0_attn_lk2"],
        first=c(np.concatenate([i["L0_ffn_lora_A"].reshape(-1, E).T, i["L0_ffn_G"]], 1)),
        gate=wide(i["L0_ffn_gate_w"]), up=wide(i["L0_ffn_up_w"]), down=deep(i["L0_ffn_down_w"]), lora_b=deep(i["L0_ffn_lora_B"]),
        scan_first=c(w_in[:, 2 * DI:]),
        chan_table=by_channel(np.concatenate([i["L1_attn_conv_w"][:, 0, :], i["L1_attn_conv_b"][:, None]], 1)),
        dt_bias=i["L1_attn_dt_bias"], A_log=i["L1_attn_A_log"],
        Wg=c(np.concatenate([grouped(w_in[:, DI:2 * DI]), grouped(w_in[:, :DI])], 2).transpose(1, 0, 2)),
        WoT=c(i["L1_attn_W_out"].T),
        norm_table=by_channel(np.stack([np.repeat(i["L1_attn_D_param"], HP), i["L1_attn_norm_w"]], 1)),
        w_gate=words(i["L1_ffn_w_gate"]), w_up=words(i["L1_ffn_w_up"]), w_down=words(i["L1_ffn_w_down"]),
        scales=c(np.stack([i["L1_ffn_s_gate"].reshape(FT, P).T, i["L1_ffn_s_up"].reshape(FT, P).T], 1)),
        s_down=i["L1_ffn_s_down"])
    nc = bacc.Bacc("TRN2", target_bir_lowering=False, num_devices=1)
    arrays, aps = {}, []
    for name, a in args.items():
        arrays[f"in_{name}"] = c(a)
        aps.append(nc.dram_tensor(f"in_{name}", a.shape, mybir.dt.from_np(a.dtype), kind="ExternalInput").ap())
    aps.append(nc.dram_tensor("out", (T, E), F32, kind="ExternalOutput").ap())
    two_layers(nc, *aps)
    r = run_bass_kernel_spmd(nc, [arrays], core_ids=[0])
    return r.results[0]["out"].reshape(1, T, E)
```
